# Optimizing a Trainium2 kernel written in Bass

```python
import numpy as np
import jax
import jax.numpy as jnp

def _softmax(x, axis=-1):
    return jax.nn.softmax(x, axis=axis)

def _gelu(x):
    return jax.nn.gelu(x, approximate=True)

def _silu(x):
    return jax.nn.silu(x)

def _sigmoid(x):
    return jax.nn.sigmoid(x)

def _layernorm(x, axis=-1, eps=1e-05):
    m = jnp.mean(x, axis=axis, keepdims=True)
    v = jnp.var(x, axis=axis, keepdims=True)
    return (x - m) / jnp.sqrt(v + eps)

def _scatter_add(tgt, idx, src, axis=0):
    return tgt.at[idx].add(src)

def _segment_sum(src, seg, n):
    return jax.ops.segment_sum(src, seg, n)
kernel_name = 'mk_adj_ffn_d2_adj_r2_15183e'

def setup_inputs(seed: int=0):
    np.random.seed(seed)
    _w = jnp.asarray

    def _rec_inputs():
        import jax
        import jax.numpy as jnp
        _gk = jax.random.key(seed)
        x = -0.0002928 + 1 * jax.random.normal(jax.random.fold_in(_gk, 1), (16, 512, 128), jnp.float32)
        _a = jax.random.bernoulli(jax.random.fold_in(_gk, 2), 0.00390625, (512, 512))
        _a = jnp.logical_or(_a, jnp.eye(512, dtype=bool))
        _af = _a.astype(jnp.float32)
        _af = _af * jax.random.uniform(jax.random.fold_in(_gk, 3), (512, 512), jnp.float32, 0.05, 1)
        adj = _af
        return (x, adj)
    x, adj = _rec_inputs()

    def _L0_gnn_setup():
        import jax, jax.numpy as jnp
        import numpy as np
        N = 2048
        NFEAT, NHID, NCLASS = (128, 256, 128)
        B = 4

        def _slconv(x, adj, S, W):
            support = jnp.einsum('bnf,fh->bnh', x, W)
            weighting = adj * S
            return jnp.einsum('nm,bmh->bnh', weighting, support)
        key = jax.random.key(seed)
        ks = jax.random.split(key, 6)
        x = jax.random.normal(ks[0], (B, N, NFEAT), dtype=jnp.float32)
        adj = jax.random.uniform(ks[1], (N, N), dtype=jnp.float32)
        S = jnp.ones((N, N), dtype=jnp.float32)
        W1 = jax.random.normal(ks[2], (NFEAT, NHID), dtype=jnp.float32) / np.sqrt(NFEAT)
        W2 = jax.random.normal(ks[3], (NHID, 2 * NHID), dtype=jnp.float32) / np.sqrt(NHID)
        W3 = jax.random.normal(ks[4], (2 * NHID, NCLASS), dtype=jnp.float32) / np.sqrt(2 * NHID)
        return {'x': x, 'adj': adj, 'S': S, 'W1': W1, 'W2': W2, 'W3': W3}
    _L0_gnn_all = _L0_gnn_setup()
    _L0_gnn_in = {k: v for k, v in _L0_gnn_all.items() if k in ('W1', 'W2', 'W3')}
    del _L0_gnn_all

    def _L0_ffn_setup():
        import jax, jax.numpy as jnp
        import numpy as np
        DIM = 128
        HEADS = 8
        NUM_KEYS = 128
        NUM_KV = NUM_KEYS ** 2
        PK_TOPK = 16
        FINAL_TOPK = 16
        DIM_KEY = DIM // 2
        P = 2

        def _pk(x, Wq_pk, pk_keys):
            b, n, _ = x.shape
            q = (x @ Wq_pk).reshape(b, n, P, HEADS, DIM_KEY).transpose(2, 0, 1, 3, 4)
            sim = jnp.einsum('pbnhd,pkhd->pbnhk', q, pk_keys)
            scores, idx = jax.lax.top_k(sim, PK_TOPK)
            idx0 = idx[0]
            idx1 = idx[1] * NUM_KEYS
            index = (idx0[..., :, None] + idx1[..., None, :]).reshape(b, n, HEADS, PK_TOPK * PK_TOPK)
            score = (scores[0][..., :, None] + scores[1][..., None, :]).reshape(b, n, HEADS, PK_TOPK * PK_TOPK)
            final_scores, pk_idx = jax.lax.top_k(score, FINAL_TOPK)
            final_indices = jnp.take_along_axis(index, pk_idx, axis=-1)
            final_scores = jax.nn.softmax(final_scores, axis=-1)
            return (final_scores, final_indices)
        key = jax.random.key(seed)
        ks = jax.random.split(key, 7)
        b, n = (2, 512)
        std = 0.02
        x = jax.random.normal(ks[0], (b, n, DIM), dtype=jnp.float32)
        Wq_pk = jax.random.normal(ks[1], (DIM, P * HEADS * DIM_KEY), dtype=jnp.float32) * std
        pk_keys = jax.random.normal(ks[2], (P, NUM_KEYS, HEADS, DIM_KEY), dtype=jnp.float32) * std
        Wq = jax.random.normal(ks[3], (DIM, HEADS * DIM), dtype=jnp.float32) * std
        keys_table = jax.random.normal(ks[4], (NUM_KV * HEADS, DIM), dtype=jnp.float32) * std
        values_table = jax.random.normal(ks[5], (NUM_KV * HEADS, DIM), dtype=jnp.float32) * std
        Wo = jax.random.normal(ks[6], (DIM * HEADS, DIM), dtype=jnp.float32) * std
        return {'x': x, 'Wq_pk': Wq_pk, 'pk_keys': pk_keys, 'Wq': Wq, 'keys_table': keys_table, 'values_table': values_table, 'Wo': Wo}
    _L0_ffn_all = _L0_ffn_setup()
    _L0_ffn_in = {k: v for k, v in _L0_ffn_all.items() if k in ('Wq_pk', 'pk_keys', 'Wq', 'keys_table', 'values_table', 'Wo')}
    del _L0_ffn_all

    def _L1_gnn_setup():
        import jax, jax.numpy as jnp
        import numpy as np
        B, T, D, H = (64, 1024, 128, 128)
        MAX_SKIP = 4

        def _lstm_last(Wih, Whh, bih, bhh, xs):
            N, _, Hd = xs.shape
            bias = bih + bhh

            def step(carry, x_t):
                h, c = carry
                g = x_t @ Wih.T + h @ Whh.T + bias
                i, f, gg, o = jnp.split(g, 4, axis=-1)
                c = jax.nn.sigmoid(f) * c + jax.nn.sigmoid(i) * jnp.tanh(gg)
                h = jax.nn.sigmoid(o) * jnp.tanh(c)
                return ((h, c), None)
            init = (jnp.zeros((N, Hd), xs.dtype), jnp.zeros((N, Hd), xs.dtype))
            (h_last, _), _ = jax.lax.scan(step, init, jnp.swapaxes(xs, 0, 1))
            return h_last
        key = jax.random.key(seed)
        ks = jax.random.split(key, 8)
        s = 0.05
        x = jax.random.normal(ks[0], (B, T, D), jnp.float32)
        adj = jax.random.uniform(ks[1], (T, T), jnp.float32) / T
        Wg0 = jax.random.normal(ks[2], (D, H), jnp.float32) * s
        bg0 = jnp.zeros((H,), jnp.float32)
        Wg1 = jax.random.normal(ks[3], (H, H), jnp.float32) * s
        bg1 = jnp.zeros((H,), jnp.float32)
        Wih = jax.random.normal(ks[4], (MAX_SKIP, 4 * H, H), jnp.float32) * s
        Whh = jax.random.normal(ks[5], (MAX_SKIP, 4 * H, H), jnp.float32) * s
        bih = jax.random.normal(ks[6], (MAX_SKIP, 4 * H), jnp.float32) * s
        bhh = jax.random.normal(ks[7], (MAX_SKIP, 4 * H), jnp.float32) * s
        return dict(x=x, adj=adj, Wg0=Wg0, bg0=bg0, Wg1=Wg1, bg1=bg1, Wih=Wih, Whh=Whh, bih=bih, bhh=bhh)
    _L1_gnn_all = _L1_gnn_setup()
    _L1_gnn_in = {k: v for k, v in _L1_gnn_all.items() if k in ('Wg0', 'bg0', 'Wg1', 'bg1', 'Wih', 'Whh', 'bih', 'bhh')}
    del _L1_gnn_all

    def _L1_ffn_setup():
        import jax, jax.numpy as jnp
        import numpy as np
        DIM = 128
        H = 8
        D = 64
        G = 64
        INNER = H * D
        SCALE = D ** (-0.5)
        key = jax.random.key(seed)
        ks = jax.random.split(key, 12)
        B, N = (4, 8192)
        x = jax.random.normal(ks[0], (B, N, DIM), dtype=jnp.float32)
        s = lambda fan_in: 1.0 / np.sqrt(fan_in)
        W_fx = jax.random.normal(ks[1], (DIM, INNER), dtype=jnp.float32) * s(DIM)
        b_fx = jnp.zeros((INNER,), dtype=jnp.float32)
        W_x = jax.random.normal(ks[2], (DIM, INNER), dtype=jnp.float32) * s(DIM)
        b_x = jnp.zeros((INNER,), dtype=jnp.float32)
        A = jax.random.normal(ks[3], (G, D), dtype=jnp.float32)
        Q, _ = jnp.linalg.qr(A.T)
        W_slice = Q[:, :G].astype(jnp.float32)
        b_slice = jnp.zeros((G,), dtype=jnp.float32)
        W_q = jax.random.normal(ks[4], (D, D), dtype=jnp.float32) * s(D)
        W_k = jax.random.normal(ks[5], (D, D), dtype=jnp.float32) * s(D)
        W_v = jax.random.normal(ks[6], (D, D), dtype=jnp.float32) * s(D)
        W_out = jax.random.normal(ks[7], (INNER, DIM), dtype=jnp.float32) * s(INNER)
        b_out = jnp.zeros((DIM,), dtype=jnp.float32)
        temperature = jnp.ones((1, H, 1, 1), dtype=jnp.float32) * 0.5
        return {'x': x, 'W_fx': W_fx, 'b_fx': b_fx, 'W_x': W_x, 'b_x': b_x, 'W_slice': W_slice, 'b_slice': b_slice, 'W_q': W_q, 'W_k': W_k, 'W_v': W_v, 'W_out': W_out, 'b_out': b_out, 'temperature': temperature}
    _L1_ffn_all = _L1_ffn_setup()
    _L1_ffn_in = {k: v for k, v in _L1_ffn_all.items() if k in ('W_fx', 'b_fx', 'W_x', 'b_x', 'W_slice', 'b_slice', 'W_q', 'W_k', 'W_v', 'W_out', 'b_out', 'temperature')}
    del _L1_ffn_all
    return {'x': x, 'adj': adj, 'L0_gnn_W1': _L0_gnn_in['W1'], 'L0_gnn_W2': _L0_gnn_in['W2'], 'L0_gnn_W3': _L0_gnn_in['W3'], 'L0_ffn_Wq_pk': _L0_ffn_in['Wq_pk'], 'L0_ffn_pk_keys': _L0_ffn_in['pk_keys'], 'L0_ffn_Wq': _L0_ffn_in['Wq'], 'L0_ffn_keys_table': _L0_ffn_in['keys_table'], 'L0_ffn_values_table': _L0_ffn_in['values_table'], 'L0_ffn_Wo': _L0_ffn_in['Wo'], 'L1_gnn_Wg0': _L1_gnn_in['Wg0'], 'L1_gnn_bg0': _L1_gnn_in['bg0'], 'L1_gnn_Wg1': _L1_gnn_in['Wg1'], 'L1_gnn_bg1': _L1_gnn_in['bg1'], 'L1_gnn_Wih': _L1_gnn_in['Wih'], 'L1_gnn_Whh': _L1_gnn_in['Whh'], 'L1_gnn_bih': _L1_gnn_in['bih'], 'L1_gnn_bhh': _L1_gnn_in['bhh'], 'L1_ffn_W_fx': _L1_ffn_in['W_fx'], 'L1_ffn_b_fx': _L1_ffn_in['b_fx'], 'L1_ffn_W_x': _L1_ffn_in['W_x'], 'L1_ffn_b_x': _L1_ffn_in['b_x'], 'L1_ffn_W_slice': _L1_ffn_in['W_slice'], 'L1_ffn_b_slice': _L1_ffn_in['b_slice'], 'L1_ffn_W_q': _L1_ffn_in['W_q'], 'L1_ffn_W_k': _L1_ffn_in['W_k'], 'L1_ffn_W_v': _L1_ffn_in['W_v'], 'L1_ffn_W_out': _L1_ffn_in['W_out'], 'L1_ffn_b_out': _L1_ffn_in['b_out'], 'L1_ffn_temperature': _L1_ffn_in['temperature']}

def reference(x, adj, L0_gnn_W1, L0_gnn_W2, L0_gnn_W3, L0_ffn_Wq_pk, L0_ffn_pk_keys, L0_ffn_Wq, L0_ffn_keys_table, L0_ffn_values_table, L0_ffn_Wo, L1_gnn_Wg0, L1_gnn_bg0, L1_gnn_Wg1, L1_gnn_bg1, L1_gnn_Wih, L1_gnn_Whh, L1_gnn_bih, L1_gnn_bhh, L1_ffn_W_fx, L1_ffn_b_fx, L1_ffn_W_x, L1_ffn_b_x, L1_ffn_W_slice, L1_ffn_b_slice, L1_ffn_W_q, L1_ffn_W_k, L1_ffn_W_v, L1_ffn_W_out, L1_ffn_b_out, L1_ffn_temperature):
    import jax
    import jax.numpy as jnp

    def _L0_gnn_ref(x, adj, S, W1, W2, W3):
        import jax, jax.numpy as jnp
        import numpy as np
        N = 2048
        NFEAT, NHID, NCLASS = (128, 256, 128)
        B = 4

        def _slconv(x, adj, S, W):
            support = jnp.einsum('bnf,fh->bnh', x, W)
            weighting = adj * S
            return jnp.einsum('nm,bmh->bnh', weighting, support)
        h = jax.nn.relu(_slconv(x, adj, S, W1))
        h = jax.nn.relu(_slconv(h, adj, S, W2))
        return _slconv(h, adj, S, W3)

    def _L0_ffn_ref(x, Wq_pk, pk_keys, Wq, keys_table, values_table, Wo):
        import jax, jax.numpy as jnp
        import numpy as np
        DIM = 128
        HEADS = 8
        NUM_KEYS = 128
        NUM_KV = NUM_KEYS ** 2
        PK_TOPK = 16
        FINAL_TOPK = 16
        DIM_KEY = DIM // 2
        P = 2

        def _pk(x, Wq_pk, pk_keys):
            b, n, _ = x.shape
            q = (x @ Wq_pk).reshape(b, n, P, HEADS, DIM_KEY).transpose(2, 0, 1, 3, 4)
            sim = jnp.einsum('pbnhd,pkhd->pbnhk', q, pk_keys)
            scores, idx = jax.lax.top_k(sim, PK_TOPK)
            idx0 = idx[0]
            idx1 = idx[1] * NUM_KEYS
            index = (idx0[..., :, None] + idx1[..., None, :]).reshape(b, n, HEADS, PK_TOPK * PK_TOPK)
            score = (scores[0][..., :, None] + scores[1][..., None, :]).reshape(b, n, HEADS, PK_TOPK * PK_TOPK)
            final_scores, pk_idx = jax.lax.top_k(score, FINAL_TOPK)
            final_indices = jnp.take_along_axis(index, pk_idx, axis=-1)
            final_scores = jax.nn.softmax(final_scores, axis=-1)
            return (final_scores, final_indices)
        b, n, d = x.shape
        q = (x @ Wq).reshape(b, n, HEADS, DIM) * DIM ** (-0.5)
        kv_scores, indices = _pk(x, Wq_pk, pk_keys)
        offsets = jnp.arange(HEADS, dtype=indices.dtype) * NUM_KV
        ind = indices + offsets[None, None, :, None]
        k = jnp.einsum('bnhk,bnhkd->bnhd', kv_scores, keys_table[ind])
        v = jnp.einsum('bnhk,bnhkd->bnhd', kv_scores, values_table[ind])
        sim = jnp.einsum('bihd,bjhd->bhij', q, k)
        neg = -jnp.finfo(sim.dtype).max
        causal = jnp.tril(jnp.ones((n, n), dtype=bool))
        sim = jnp.where(causal, sim, neg)
        attn = jax.nn.softmax(sim, axis=-1)
        out = jnp.einsum('bhij,bjhd->bhid', attn, v)
        out = out.transpose(0, 2, 1, 3).reshape(b, n, HEADS * DIM)
        return out @ Wo

    def _L1_gnn_ref(x, adj, Wg0, bg0, Wg1, bg1, Wih, Whh, bih, bhh):
        import jax, jax.numpy as jnp
        import numpy as np
        B, T, D, H = (64, 1024, 128, 128)
        MAX_SKIP = 4

        def _lstm_last(Wih, Whh, bih, bhh, xs):
            N, _, Hd = xs.shape
            bias = bih + bhh

            def step(carry, x_t):
                h, c = carry
                g = x_t @ Wih.T + h @ Whh.T + bias
                i, f, gg, o = jnp.split(g, 4, axis=-1)
                c = jax.nn.sigmoid(f) * c + jax.nn.sigmoid(i) * jnp.tanh(gg)
                h = jax.nn.sigmoid(o) * jnp.tanh(c)
                return ((h, c), None)
            init = (jnp.zeros((N, Hd), xs.dtype), jnp.zeros((N, Hd), xs.dtype))
            (h_last, _), _ = jax.lax.scan(step, init, jnp.swapaxes(xs, 0, 1))
            return h_last
        h = jax.nn.relu(jnp.einsum('ts,bsh->bth', adj, x @ Wg0 + bg0))
        h = jax.nn.relu(jnp.einsum('ts,bsh->bth', adj, h @ Wg1 + bg1))
        Bv, Tv, Hd = h.shape
        for p in range(1, MAX_SKIP + 1):
            nw = Tv // p
            wins = h[:, :nw * p, :].reshape(Bv * nw, p, Hd)
            last = _lstm_last(Wih[p - 1], Whh[p - 1], bih[p - 1], bhh[p - 1], wins)
            idx = jnp.arange(nw) * p + (p - 1)
            h = h.at[:, idx, :].set(last.reshape(Bv, nw, Hd))
        return h

    def _L1_ffn_ref(x, W_fx, b_fx, W_x, b_x, W_slice, b_slice, W_q, W_k, W_v, W_out, b_out, temperature):
        import jax, jax.numpy as jnp
        import numpy as np
        DIM = 128
        H = 8
        D = 64
        G = 64
        INNER = H * D
        SCALE = D ** (-0.5)
        B, N, _ = x.shape
        fx_mid = (x @ W_fx + b_fx).reshape(B, N, H, D).transpose(0, 2, 1, 3)
        x_mid = (x @ W_x + b_x).reshape(B, N, H, D).transpose(0, 2, 1, 3)
        temp = jnp.clip(temperature, 0.1, 5.0)
        slice_weights = jax.nn.softmax((x_mid @ W_slice + b_slice) / temp, axis=-1)
        slice_norm = slice_weights.sum(axis=2)
        slice_token = jnp.einsum('bhnc,bhng->bhgc', fx_mid, slice_weights)
        slice_token = slice_token / (slice_norm[..., None] + 1e-05)
        q = slice_token @ W_q
        k = slice_token @ W_k
        v = slice_token @ W_v
        attn = jax.nn.softmax(jnp.einsum('bhgc,bhkc->bhgk', q, k) * SCALE, axis=-1)
        out_slice = jnp.einsum('bhgk,bhkc->bhgc', attn, v)
        out_x = jnp.einsum('bhgc,bhng->bhnc', out_slice, slice_weights)
        out_x = out_x.transpose(0, 2, 1, 3).reshape(B, N, INNER)
        return out_x @ W_out + b_out
    x = x + _L0_gnn_ref(_layernorm(x, axis=-1), adj, adj, L0_gnn_W1, L0_gnn_W2, L0_gnn_W3)
    x = x + _L0_ffn_ref(_layernorm(x, axis=-1), L0_ffn_Wq_pk, L0_ffn_pk_keys, L0_ffn_Wq, L0_ffn_keys_table, L0_ffn_values_table, L0_ffn_Wo)
    x = x + _L1_gnn_ref(_layernorm(x, axis=-1), adj, L1_gnn_Wg0, L1_gnn_bg0, L1_gnn_Wg1, L1_gnn_bg1, L1_gnn_Wih, L1_gnn_Whh, L1_gnn_bih, L1_gnn_bhh)
    x = x + _L1_ffn_ref(_layernorm(x, axis=-1), L1_ffn_W_fx, L1_ffn_b_fx, L1_ffn_W_x, L1_ffn_b_x, L1_ffn_W_slice, L1_ffn_b_slice, L1_ffn_W_q, L1_ffn_W_k, L1_ffn_W_v, L1_ffn_W_out, L1_ffn_b_out, L1_ffn_temperature)
    return x

_drawn_inputs = setup_inputs


def setup_inputs(seed=0):
    import zlib

    import numpy as np

    out = dict(_drawn_inputs(seed))
    spreads = {'L1_gnn_bg0': (0.0, 0.8),
     'L1_gnn_bg1': (0.0, 0.8),
     'L1_ffn_b_fx': (0.0, 0.1),
     'L1_ffn_b_x': (0.0, 0.8),
     'L1_ffn_b_slice': (0.0, 0.8),
     'L1_ffn_b_out': (0.0, 0.1),
     'L1_ffn_temperature': (0.5, 0.6)}
    factors = {'L0_ffn_Wq_pk': 8.0,
     'L0_ffn_pk_keys': 8.0,
     'L0_ffn_Wq': 8.0,
     'L0_ffn_keys_table': 8.0,
     'L0_ffn_values_table': 8.0,
     'L0_ffn_Wo': 8.0,
     'L1_gnn_Wg0': 4.619,
     'L1_gnn_Wg1': 3.134,
     'L1_gnn_Whh': 8.0,
     'L1_gnn_bih': 2.986,
     'L1_gnn_bhh': 3.092,
     'L1_ffn_W_x': 4.58,
     'L1_ffn_W_slice': 5.867,
     'L1_ffn_W_q': 8.0,
     'L1_ffn_W_k': 8.0}
    for name, (base, spread) in spreads.items():
        noise = np.random.default_rng([zlib.crc32(name.encode()), seed]).standard_normal(out[name].shape)
        drawn = base * np.exp(spread * noise) if base else spread * noise
        out[name] = jnp.asarray(drawn.astype(out[name].dtype))
    for name, factor in factors.items():
        out[name] = (out[name] * factor).astype(out[name].dtype)
    return out
```

```python
from contextlib import ExitStack

import concourse.bass as bass
from concourse import mybir

F32 = mybir.dt.float32
U32 = mybir.dt.uint32
ALU = mybir.AluOpType
ACT = mybir.ActivationFunctionType
AX = mybir.AxisListType.X

P = 128
B, N, D = 16, 512, 128
T = N // P
H1, H2 = 256, 512
HEADS, DK, NKEYS, TOPK = 8, 64, 128, 16
NKV = NKEYS * NKEYS
SKIPS = 4
SH, SD, G = 8, 64, 64
POS = T * HEADS
UJ = 4
UNITS = TOPK // UJ
SLOTS = 8
EPS = 1e-5
LSTM_AT = {19: (0, 1), 20: (2, 3), 21: (4, 5), 22: (6, 7), 23: (8, 9), 24: (10,)}
MASKED = -1.0e30
TAKEN = -3.0e38
ATT_SCALE = float(D) ** -0.5
SLICE_SCALE = float(SD) ** -0.5

ROWS = []
_at = 0
for _i, _k, _n in ((0, 1, 16), (1, 1, 8), (2, 1, 5), (3, 1, 4), (4, 1, 3), (5, 3, 2), (8, 8, 1)):
    ROWS.append((_i, _k, _n, _at))
    _at += _k * _n
NC = _at

LSTM = [(1, 0, 0, 256), (1, 0, 256, 256)] + [(p, s, 0, N // p) for p in range(2, SKIPS + 1) for s in range(p)]

LAST_OF = {u[0]: u for u in LSTM}

ATT_AT = [(p // 2, 2 * (p % 2), 2 * (p % 2) + 1) for p in range(2 * HEADS)]


class Signal:

    def __init__(self, sem, steps, start=0):
        self.sem, self.n, self.start = sem, len(steps), start
        self.index = {s: k for k, s in enumerate(steps)}
        assert len(self.index) == self.n

    def at(self, b, step):
        return b * self.n + self.index[step] + 1 + self.start


def wait_apart(engine, sem, value, passed):
    engine.wait_ge(sem, value)
    engine.sem_inc(passed, 1)


FRONT_PE = ["Az", "h1a", "h1b", "Ah0", "Ah1"] + [f"h2{c}" for c in range(4)] + ["P", "y", "zT"]
FRONT_ACT = ["sd", "Az", "h1a", "h1b", "Ah0", "Ah1"] + [f"h2{c}" for c in range(4)] + ["P", "sd1", "zT"]
FRONT_DVE = ["st", "mv", "rs", "z", "x1", "st1", "mv1", "rs1", "z1"]
ATT_PE, ATT_ACT, ATT_DVE = [], [], []
for _h, _a, _b in ATT_AT:
    ATT_PE += [("q", _h)] * (_a == 0) + [(k, _h, i) for k in "sTv" for i in (_a, _b)]
    ATT_ACT += [("q", _h)] * (_a == 0) + [(k, _h, i) for k in "edTo" for i in (_a, _b)]
    ATT_DVE += [(k, _h, i) for i in (_a, _b) for k in "mxn"] + [("r", _h, i) for i in (_a, _b)]
POST_PE = (["wo", "Uz", "g1", "Ug", "g2"] + [("gates", u) for u in LSTM] + ["ht", "zT"]
           + [("lg", t) for t in range(T)] + ["Y", "nr", "st", "q", "k", "v", "sim", "aT", "vw", "G"]
           + [("wT", t) for t in range(T)] + ["o"])
POST_ACT = (["sd", "Uz", "g1", "Ug", "g2"] + [(k, u) for u in LSTM for k in ("gates", "tc")] + ["sd3", "zT"]
            + [("ex", t) for t in range(T)] + ["st", "q", "k", "v", "aex", "aT", "vw0", "vw1", "G"]
            + [("wT", t) for t in range(T)])
POST_DVE = (["x2", "st", "mv", "rs", "z"]
            + [(k, u) for u in LSTM for k in ((("fc",) if u[1] else ()) + ("ig",) + (("c",) if u[1] else ()) + ("h",))]
            + ["x3", "st3", "mv3", "rs3", "z3"] + [(k, t) for t in range(T) for k in ("mx", "sb", "sm", "rc", "sw")]
            + ["n1", "n2", "Yn", "nn", "amx", "asb", "asm", "arc", "at", "o"])
KEYS_DVE = ["max", "idx", "rep", "max2", "idx2", "f", "cand", "cmax", "cpos", "crep", "cmax2", "cpos2", "neg",
            "posf"] + [f"{k}{h}" for h in range(2) for k in ("eq", "sel", "row")]
COPIES = ["KV", "X"]


def build(nc, x, adjT, w1, w2, w3, wqpkT, keysT, wq, table, wo, wg0, wg1, bg0, bg1, wihT, whhT, bih, bhh,
          wfx, bfx, wxT, bx, wsl, bsl, temp, wqs, wks, wvs, wout, bout, c_ident, c_mask, c_iota, c_ones, out):
    with ExitStack() as ctx:
        def sb(name, shape, dt=F32):
            return ctx.enter_context(nc.sbuf_tensor(name, shape, dt))

        def bank(name):
            return ctx.enter_context(nc.psum_tensor(name, [P, 512], F32))

        def sem(name):
            return ctx.enter_context(nc.semaphore(name))

        adj_s = sb("adj_s", [P, T, N])
        adj2_s = sb("adj2_s", [P, T, N])
        w1_s, w2_s, w3_s = sb("w1_s", [P, H1]), sb("w2_s", [P, 2, H2]), sb("w3_s", [P, 4, D])
        keymap = sb("keymap", [P, HEADS, 2, NKEYS])
        wq_s, wo_s = sb("wq_s", [P, HEADS, D]), sb("wo_s", [P, HEADS, D])
        wg0_s, wg1_s = sb("wg0_s", [P, D]), sb("wg1_s", [P, D])
        lw = sb("lw", [P, 2, 2, 4 * D])
        lbias, lbias2 = sb("lbias", [P, SKIPS, 4]), sb("lbias2", [P, SKIPS, 4])
        wfx_s, slmap = sb("wfx_s", [P, SH * SD]), sb("slmap", [P, SH * G])
        wqs_s, wks_s, wvs_s = (sb(n, [SD, SD]) for n in ("wqs_s", "wks_s", "wvs_s"))
        wout_s = sb("wout_s", [SD, SH, D])
        rows = sb("rows", [65, 2 * 512])
        bfx_r, nn_r = rows[0:1, 0:512], rows[0:1, 512:1024]
        slb_r, bout_r = rows[32:33, 0:512], rows[32:33, 512:512 + D]
        ra_r, bg0_r, bg1_r = rows[64:65, 0:512], rows[64:65, 512:512 + D], rows[64:65, 512 + D:512 + 2 * D]
        temp_s, tinv = sb("temp_s", [P, SH]), sb("tinv", [P, SH])
        ident, mask, iota, ones = sb("ident", [P, P]), sb("mask", [P, P]), sb("iota", [P, NC]), sb("ones", [P, P])
        eps = sb("eps", [P, 1])
        ring = sb("ring", [P, SLOTS, UJ, 2 * D])
        diag = sb("diag", [P, 2, UJ, P])
        idx = sb("idx", [P, 2, HEADS, TOPK], U32)
        wts, wsum, winv = sb("wts", [P, 2, HEADS, TOPK]), sb("wsum", [P, 2, HEADS]), sb("winv", [P, 2, HEADS])
        KT, V = sb("KT", [P, HEADS, N]), sb("V", [P, T, HEADS, D])
        tv, ti, tf = sb("tv", [P, 2, 2, TOPK]), sb("ti", [P, 2, 2, TOPK], U32), sb("tf", [P, 2, 2, TOPK])
        work = sb("work", [P, TOPK * NC])
        rep = work[:, 0:4 * NKEYS].rearrange("p (h q k) -> p h q k", h=2, q=2)
        eq = work[:, :].rearrange("p (k c) -> p k c", c=NC)
        cs, ci, crep = sb("cs", [P, 2, NC]), sb("ci", [P, 2, NC]), sb("crep", [P, 2, NC])
        fs, fp, fpf = sb("fs", [P, 2, TOPK]), sb("fp", [P, 2, TOPK], U32), sb("fpf", [P, 2, TOPK])
        neg = sb("neg", [P, 2, 1])
        x_s = sb("x_s", [P, T, D])
        h12, ah = sb("h12", [P, 4, 512]), sb("ah", [P, 2, N])
        up, z = ah[:, 0, :], h12[:, 3, :].rearrange("p (t d) -> p t d", t=T)
        h1_s = h12[:, 0:2, :].rearrange("p a (b c) -> p (a b) c", b=2)
        x1, z1T = sb("x1", [P, T, D]), sb("z1T", [P, N])
        f_st, f_mv, f_sd, f_rs = (sb(n, s) for n, s in
                                  (("f_st", [P, T, 6]), ("f_mv", [P, T, 2]), ("f_sd", [P, T]), ("f_rs", [P, T])))
        KTa, Va = sb("KTa", [P, HEADS, 2 * P]), sb("Va", [P, 2, HEADS, D])
        x1a, z1Ta = sb("x1a", [P, T, D]), sb("z1Ta", [P, N])
        qo = sb("qo", [P, HEADS, N])
        prob, probT = sb("prob", [P, 2, N]), sb("probT", [P, 2, N])
        a_mx, a_sm, a_dg = sb("a_mx", [P, 2, 2]), sb("a_sm", [P, 2, 2]), sb("a_dg", [P, 2, P])
        x2 = sb("x2", [P, T, D])
        p_st, p_mv, p_sd, p_rs = (sb(n, s) for n, s in
                                  (("p_st", [P, T, 6]), ("p_mv", [P, T, 2]), ("p_sd", [P, T]), ("p_rs", [P, T])))
        s_mx, s_sm = sb("s_mx", [P, SH]), sb("s_sm", [P, 2, SH])
        left = qo[:, :, :].rearrange("p h n -> p (h n)")
        z2 = left[:, 0:512].rearrange("p (t d) -> p t d", t=T)
        u2, g1_s, hT = left[:, 512:1024], left[:, 1024:1536].rearrange("p (t d) -> p t d", t=T), left[:, 1536:2048]
        gates = left[:, 2048:3072].rearrange("p (k n) -> p k n", k=4)
        cell, ctan, hid, ig = (left[:, 3072 + 256 * k:3072 + 256 * (k + 1)] for k in range(4))
        z3T, lg, Yn, rn = u2, left[:, 1024:1536], left[:, 2048:2560], left[:, 2560:3072]
        sw = KTa[:, :, :].rearrange("p h n -> p (h n)").rearrange("p (t n) -> p t n", t=T)
        swT = Va[:, :, :, :].rearrange("p a h d -> p (a h d)").rearrange("p (c n) -> p c n", c=T)
        stT, qs, ks, vs = (left[0:SD, 512 * k:512 * (k + 1)] for k in (2, 3, 6, 7))
        sat, satT = prob[0:G, 0, :], prob[0:G, 1, :]
        vw = left[0:G, 2048:3072].rearrange("p (h d) -> p h d", h=SH)
        gout = probT[:, 0, :].rearrange("p (c d) -> p c d", c=4)
        spare = ring[:, :, :, :].rearrange("p a b c -> p (a b c)")
        wqpk_u = spare[0:DK, 0:2048].rearrange("p (a f) -> p a f", a=2 * HEADS)
        keys_u = spare[0:DK, 2048:4096].rearrange("p (a k) -> p a k", a=2 * HEADS)
        wx_u = spare[0:SD, 4096:5120].rearrange("p (h f) -> p h f", h=SH)
        wsl_u, bx_u, bsl_u = spare[0:SD, 5120:5184], spare[0:SD, 5184:5192], spare[32:33, 5248:5760]

        S, KV0, KV1, FA, FB, FC, AA, AB = (bank(f"bank_{n}") for n in "S KV0 KV1 FA FB FC AA AB".split())
        A, KV = (AA, AB), (KV0, KV1)

        consts_in, x_in, stored = sem("consts_in"), sem("x_in"), sem("stored")
        passed_dve, passed_pe, passed_pool = sem("passed_dve"), sem("passed_pe"), sem("passed_pool")
        lw_in = [sem("lw_in0"), sem("lw_in1")]
        merged, merged_copied = sem("merged"), sem("merged_copied")
        setup_dve = sem("setup_dve")
        gathered = [sem(f"gathered{k}") for k in range(SLOTS)]
        slots_free, diags_made, pairs_out = sem("slots_free"), sem("diags_made"), sem("pairs_out")
        sims = sem("sims")
        wexp, winverted, wnorm = sem("wexp"), sem("winverted"), sem("wnorm")
        fpe, fact, fdve = (Signal(sem(n), s) for n, s in
                           (("front_products", FRONT_PE), ("front_copies", FRONT_ACT), ("front_sums", FRONT_DVE)))
        ape, aact, adve = (Signal(sem(n), s) for n, s in
                           (("att_products", ATT_PE), ("att_copies", ATT_ACT), ("att_sums", ATT_DVE)))
        ppe, pact, pdve = (Signal(sem(n), s, start) for n, s, start in
                           (("post_products", POST_PE, len(POST_PE)), ("post_copies", POST_ACT, 0), ("post_sums", POST_DVE, 0)))
        keys = Signal(sem("keys_done"), KEYS_DVE)
        copied = [Signal(sem(f"copied_{n}"), [n]) for n in COPIES]
        kv_copied, x_copied = copied

        block = ctx.enter_context(nc.Block())
        loads = [(adj_s[:, :, :], adjT.rearrange("(t p) n -> p t n", p=P)), (w1_s[:, :], w1),
                 (w2_s[:, :, :], w2.rearrange("(c p) n -> p c n", p=P)),
                 (w3_s[:, :, :], w3.rearrange("(c p) n -> p c n", p=P)),
                 (wqpk_u, wqpkT), (keys_u, keysT), (wq_s[:, :, :], wq.rearrange("p (h d) -> p h d", h=HEADS)),
                 (wo_s[:, :, :], wo.rearrange("(h p) d -> p h d", p=P)), (wg0_s[:, :], wg0), (wg1_s[:, :], wg1),
                 (lbias[:, :, :], bih),
                 (lbias2[:, :, :], bhh), (wfx_s[:, :], wfx), (wx_u, wxT), (wsl_u, wsl), (bx_u, bx), (bsl_u, bsl),
                 (temp_s[:, :], temp), (wqs_s[:, :], wqs), (wks_s[:, :], wks), (wvs_s[:, :], wvs),
                 (wout_s[:, :, :], wout.rearrange("(h p) d -> p h d", p=SD)), (bfx_r, bfx), (bg0_r, bg0),
                 (bg1_r, bg1), (bout_r, bout), (ident[:, :], c_ident), (mask[:, :], c_mask), (iota[:, :], c_iota),
                 (ones[:, :], c_ones)]
        LOADED = 16 * len(loads)
        MERGED, SETUP_DVE = HEADS // 2 + 3, 9

        def cols(t):
            return slice(t * P, (t + 1) * P)

        @block.sync
        def _(sp):
            def load_x(b, first=False):
                if not first:
                    sp.wait_ge(fdve.sem, fdve.at(b - 1, "x1"))
                sp.dma_start(x_s[:, :, :], x[b].rearrange("(t p) d -> p t d", p=P)).then_inc(x_in, 16)

            def store(b):
                sp.wait_ge(pdve.sem, pdve.at(b, "o"))
                sp.dma_start(out[b].rearrange("(t p) d -> p t d", p=P), x2[:, :, :]).then_inc(stored, 16)

            sp.sem_inc(stored, 16)
            def load_lstm(b):
                for p in range(1, SKIPS + 1):
                    if p > 2:
                        sp.wait_ge(ppe.sem, ppe.at(b, ("gates", LAST_OF[p - 2])))
                    else:
                        sp.wait_ge(ppe.sem, ppe.at(b - 1, ("gates", LAST_OF[p + 2])))
                    sp.dma_start(lw[:, p % 2, 0, :], wihT[:, p - 1, :]).then_inc(lw_in[p % 2], 16)
                    sp.dma_start(lw[:, p % 2, 1, :], whhT[:, p - 1, :]).then_inc(lw_in[p % 2], 16)

            load_x(0, True)
            for dst, src in loads:
                sp.dma_start(dst, src).then_inc(consts_in, 16)
            load_x(1)
            with nc.sync.Fori(1, B - 1) as b:
                load_x(b + 1)
                load_lstm(b - 1)
                store(b - 1)
            for b in (B - 2, B - 1):
                load_lstm(b)
                store(b)
            sp.wait_ge(stored, 16 * (B + 1))

        @block.gpsimd
        def _(pool):
            pool.wait_ge(merged, MERGED)
            pool.wait_ge(setup_dve, SETUP_DVE)
            with nc.gpsimd.Fori(0, B * T // 2) as m:
                for r in range(2 * HEADS):
                    wait_apart(pool, keys.sem, keys.at(m * HEADS + r // 2, "row1"), passed_pool)
                    for u in range(UNITS):
                        slot = (UNITS * r + u) % SLOTS
                        wait_apart(pool, slots_free, m * (2 * HEADS * UNITS) + UNITS * r + u + 1, passed_pool)
                        for j in range(UJ):
                            k = u * UJ + j
                            nc.gpsimd.indirect_dma_start(
                                ring[:, slot, j, :], None, table,
                                bass.IndirectOffsetOnAxis(ap=idx[:, r // HEADS, r % HEADS, k:k + 1], axis=0),
                                bounds_check=HEADS * NKV - 1, oob_is_err=False).then_inc(gathered[slot], 16)

        @block.tensor
        def _(pe):
            mm, tr = nc.tensor.matmul, nc.tensor.transpose

            def setup():
                pe.wait_ge(consts_in, LOADED)
                for h in range(HEADS):
                    if h % 2 == 0 and h >= 4:
                        pe.wait_ge(merged_copied, h // 2 - 1)
                    for p in range(2):
                        last = mm(A[h // 2 % 2][:, cols(2 * (h % 2) + p)], wqpk_u[:, p * HEADS + h, :],
                                  keys_u[:, p * HEADS + h, :], start=True, stop=True)
                    if h % 2:
                        last.then_inc(merged, 1)
                for h in range(SH):
                    last = mm(FA[:, h * G:(h + 1) * G], wx_u[:, h, :], wsl_u, start=True, stop=True)
                last.then_inc(merged, 1)
                for h in range(SH):
                    last = mm(FB[32:33, h * G:(h + 1) * G], bx_u[:, h:h + 1], wsl_u, start=True, stop=True)
                last.then_inc(merged, 1)
                for m in range(T):
                    last = mm(FC[64:65, :], ones[:, 0:1], adj_s[:, m, :], start=(m == 0), stop=(m == T - 1))
                last.then_inc(merged, 1)
                pe.sem_inc(slots_free, SLOTS)
                pe.sem_inc(ppe.sem, ppe.n)
                pe.wait_ge(merged_copied, HEADS // 2)
                pe.wait_ge(setup_dve, SETUP_DVE)

            def front(b, p):
                if p == 1:
                    pe.wait_ge(fdve.sem, fdve.at(b, "z"))
                    for m in range(T):
                        last = mm(FA[:, :], z[:, m, :], adj2_s[:, m, :], start=(m == 0), stop=(m == T - 1))
                    last.then_inc(fpe.sem, 1)
                if p == 3:
                    pe.wait_ge(fact.sem, fact.at(b, "Az"))
                    for half, k in ((FB, "h1a"), (FA, "h1b")):
                        for t in range(2):
                            tt = t + 2 * (k == "h1b")
                            last = mm(half[:, t * H1:(t + 1) * H1], up[:, cols(tt)], w1_s[:, :], start=True, stop=True)
                        last.then_inc(fpe.sem, 1)
                if p == 5:
                    pe.wait_ge(fact.sem, fact.at(b, "h1b"))
                    for c, to in enumerate((FB, FA)):
                        for m in range(T):
                            last = mm(to[:, :], h1_s[:, m, cols(c)], adj2_s[:, m, :], start=(m == 0), stop=(m == T - 1))
                        last.then_inc(fpe.sem, 1)
                if p in (7, 9):
                    for c in ((0, 1) if p == 7 else (2, 3)):
                        pe.wait_ge(fact.sem, fact.at(b, "Ah1" if c < 2 else f"h2{c - 2}"))
                        for g in range(2):
                            last = mm((FB, FA)[c % 2][:, :], w2_s[:, g, cols(c)], ah[:, g, :], start=(g == 0), stop=(g == 1))
                        last.then_inc(fpe.sem, 1)
                if p == 11:
                    pe.wait_ge(fact.sem, fact.at(b, "h23"))
                    for t in range(T):
                        for c in range(4):
                            last = mm(FB[:, cols(t)], h12[:, c, cols(t)], w3_s[:, c, :], start=(c == 0), stop=(c == 3))
                    last.then_inc(fpe.sem, 1)
                if p == 19:
                    pe.wait_ge(fact.sem, fact.at(b, "P"))
                    for t in range(T):
                        for m in range(T):
                            last = mm(FA[:, cols(t)], adj2_s[:, m, cols(t)], up[:, cols(m)], start=(m == 0), stop=(m == T - 1))
                    last.then_inc(fpe.sem, 1)
                if p == 23:
                    pe.wait_ge(fdve.sem, fdve.at(b, "z1"))
                    for t in range(T):
                        last = tr(FB[:, cols(t)], z[:, t, :], ident[:, :])
                    last.then_inc(fpe.sem, 1)

            def similarities(b, t, p, first=False):
                pair = b * (POS // 2) + (t * HEADS + p) // 2
                if t == 0 and p == 0:
                    pe.wait_ge(fact.sem, fact.at(b, "zT"))
                if not first:
                    pe.wait_ge(keys.sem, keys.at(pair - 1, "rep"))
                mm(S[:, :], z1T[:, cols(t)], keymap[:, p:p + 2, :, :].rearrange("p a b k -> p (a b k)"),
                   start=True, stop=True).then_inc(sims, 1)

            def weigh(b, p, u, first=False):
                unit = b * (POS * UNITS) + p * UNITS + u
                slot, use = (p * UNITS + u) % SLOTS, b * (POS * UNITS // SLOTS) + (p * UNITS + u) // SLOTS
                if u == 0 and not (first and p < 2):
                    pe.wait_ge(pairs_out, b * POS + p - 1)
                pe.wait_ge(diags_made, unit + 1)
                pe.wait_ge(gathered[slot], (use + 1) * (16 * UJ))
                for j in range(UJ):
                    st, en = (u == 0 and j == 0), (u == UNITS - 1 and j == UJ - 1)
                    mm(KV[p % 2][:, 0:P], ring[:, slot, j, 0:D], diag[:, u % 2, j, :], start=st, stop=en,
                       skip_group_check=True)
                    last = mm(KV[p % 2][:, P:2 * P], diag[:, u % 2, j, :], ring[:, slot, j, D:2 * D], start=False,
                              stop=en, skip_group_check=True)
                last.then_inc(slots_free, 1)

            def attend(b, p, part):
                h, ia, ib = ATT_AT[p]
                for i in (ia, ib):
                    bk, n = A[i % 2], (i + 1) * P
                    if part == 0 and i == ia:
                        if ia == 0:
                            if h == 0:
                                pe.wait_ge(x_copied.sem, x_copied.at(b, "X"))
                                pe.wait_ge(kv_copied.sem, kv_copied.at(b, "KV"))
                            else:
                                pe.wait_ge(aact.sem, aact.at(b, ("o", h - 1, 3)))
                            mm(AA[:, :], wq_s[:, h, :], z1Ta[:, :], start=True, stop=True).then_inc(ape.sem, 1)
                            pe.wait_ge(aact.sem, aact.at(b, ("q", h)))
                        else:
                            pe.wait_ge(aact.sem, aact.at(b, ("o", h, 1)))
                    if part == 0:
                        q = qo[:, h, cols(i)]
                        last = mm(bk[:, 0:min(n, 2 * P)], q, KTa[:, h, 0:min(n, 2 * P)], start=True, stop=True)
                        if n > 2 * P:
                            last = mm(bk[:, 2 * P:n], q, KT[:, h, 2 * P:n], start=True, stop=True)
                        last.then_inc(ape.sem, 1)
                    if part == 1:
                        pe.wait_ge(aact.sem, aact.at(b, ("d", h, i)))
                        for j in range(i + 1):
                            last = mm(bk[:, cols(j)], prob[:, i % 2, cols(j)], a_dg[:, i % 2, :], start=True, stop=True)
                        last.then_inc(ape.sem, 1)
                    if part == 2:
                        pe.wait_ge(aact.sem, aact.at(b, ("T", h, i)))
                        for j in range(i + 1):
                            v = Va[:, j, h, :] if j < 2 else V[:, j, h, :]
                            last = mm(bk[:, 0:P], v, probT[:, i % 2, cols(j)], start=(j == 0), stop=(j == i))
                        last.then_inc(ape.sem, 1)

            def lstm(b, k):
                u = LSTM[k]
                p, s, w0, n = u
                xs = hT[:, 0:(N // p) * p].rearrange("q (w p) -> q p w", p=p)[:, s, w0:w0 + n]
                if k == 0:
                    pe.wait_ge(pact.sem, pact.at(b, "g2"))
                else:
                    pe.wait_ge(pdve.sem, pdve.at(b, ("h", LSTM[k - 1])))
                if s == 0 and w0 == 0:
                    pe.wait_ge(lw_in[p % 2], 64 * b + 32 * ((p - 1) // 2 + 1))
                for gate in range(4):
                    to = A[gate // 2][:, (gate % 2) * 256:(gate % 2) * 256 + n]
                    last = mm(to, lw[:, p % 2, 0, cols(gate)], xs, start=True, stop=(s == 0))
                    if s:
                        last = mm(to, lw[:, p % 2, 1, cols(gate)], hid[:, 0:n], start=False, stop=True)
                last.then_inc(ppe.sem, 1)

            def post(b, p):
                if p == 16:
                    pe.wait_ge(aact.sem, aact.at(b, ("o", HEADS - 1, 3)))
                    for t in range(T):
                        for h in range(HEADS):
                            last = mm(AA[:, cols(t)], qo[:, h, cols(t)], wo_s[:, h, :], start=(h == 0), stop=(h == HEADS - 1))
                    last.then_inc(ppe.sem, 1)
                if p == 17:
                    pe.wait_ge(pdve.sem, pdve.at(b, "z"))
                    for m in range(T):
                        last = mm(AB[:, :], z2[:, m, :], adj_s[:, m, :], start=(m == 0), stop=(m == T - 1))
                    last.then_inc(ppe.sem, 1)
                    pe.wait_ge(pact.sem, pact.at(b, "Uz"))
                    for t in range(T):
                        mm(AA[:, cols(t)], u2[:, cols(t)], wg0_s[:, :], start=True, stop=False)
                        last = mm(AA[:, cols(t)], ra_r[:, cols(t)], bg0_r, start=False, stop=True)
                    last.then_inc(ppe.sem, 1)
                if p == 18:
                    pe.wait_ge(pact.sem, pact.at(b, "g1"))
                    for m in range(T):
                        last = mm(AB[:, :], g1_s[:, m, :], adj_s[:, m, :], start=(m == 0), stop=(m == T - 1))
                    last.then_inc(ppe.sem, 1)
                    pe.wait_ge(pact.sem, pact.at(b, "Ug"))
                    mm(AA[:, :], wg1_s[:, :], u2, start=True, stop=False)
                    mm(AA[:, :], bg1_r, ra_r, start=False, stop=True).then_inc(ppe.sem, 1)
                if p in LSTM_AT:
                    for k in LSTM_AT[p]:
                        lstm(b, k)
                if p == 25:
                    pe.wait_ge(pdve.sem, pdve.at(b, ("h", LSTM[-1])))
                    for t in range(T):
                        last = tr(AA[:, cols(t)], hT[:, cols(t)], ident[:, :])
                    last.then_inc(ppe.sem, 1)
                    pe.wait_ge(pdve.sem, pdve.at(b, "z3"))
                    for t in range(T):
                        last = tr(AB[:, cols(t)], z2[:, t, :], ident[:, :])
                    last.then_inc(ppe.sem, 1)
                if p in (26, 27):
                    for t in ((0, 1) if p == 26 else (2, 3)):
                        if t == 0:
                            pe.wait_ge(pact.sem, pact.at(b, "zT"))
                        if t >= 2:
                            pe.wait_ge(pdve.sem, pdve.at(b, ("sb", t - 2)))
                        mm(A[t % 2][:, :], z3T[:, cols(t)], slmap[:, :], start=True, stop=False)
                        mm(A[t % 2][:, :], ones[32:33, :], slb_r, start=False, stop=True).then_inc(ppe.sem, 1)
                if p == 28:
                    pe.wait_ge(pdve.sem, pdve.at(b, ("sw", T - 1)))
                    for t in range(T):
                        last = mm(AA[:, :], z2[:, t, :], sw[:, t, :], start=(t == 0), stop=(t == T - 1))
                    last.then_inc(ppe.sem, 1)
                    for t in range(T):
                        last = mm(AB[:, :], ones[:, :], sw[:, t, :], start=(t == 0), stop=(t == T - 1))
                    last.then_inc(ppe.sem, 1)
                    pe.wait_ge(pdve.sem, pdve.at(b, "nn"))
                    for h in range(SH):
                        c = slice(h * G, (h + 1) * G)
                        mm(AA[0:SD, c], wfx_s[:, c], Yn[:, c], start=True, stop=False)
                        last = mm(AA[0:SD, c], bfx_r[:, c], nn_r[:, c], start=False, stop=True)
                    last.then_inc(ppe.sem, 1)
                if p == 29:
                    wait_apart(pe, pact.sem, pact.at(b, "st"), passed_pe)
                    mm(AB[0:SD, :], wqs_s[:, :], stT, start=True, stop=True).then_inc(ppe.sem, 1)
                    mm(AA[0:SD, :], wks_s[:, :], stT, start=True, stop=True).then_inc(ppe.sem, 1)
                    wait_apart(pe, pact.sem, pact.at(b, "q"), passed_pe)
                    mm(AB[0:SD, :], wvs_s[:, :], stT, start=True, stop=True).then_inc(ppe.sem, 1)
                    wait_apart(pe, pact.sem, pact.at(b, "k"), passed_pe)
                    for h in range(SH):
                        c = slice(h * G, (h + 1) * G)
                        last = mm(AA[0:G, c], qs[:, c], ks[:, c], start=True, stop=True)
                    last.then_inc(ppe.sem, 1)
                if p == 30:
                    wait_apart(pe, pdve.sem, pdve.at(b, "at"), passed_pe)
                    for h in range(SH):
                        c = slice(h * G, (h + 1) * G)
                        last = tr(AA[0:G, c], sat[:, c], ident[0:G, 0:G])
                    last.then_inc(ppe.sem, 1)
                    wait_apart(pe, pact.sem, pact.at(b, "v"), passed_pe)
                    for h in range(SH):
                        to = (AB, FC)[h // 4][0:G, cols(h % 4)]
                        last = mm(to, vs[:, h * G:(h + 1) * G], wout_s[:, h, :], start=True, stop=True)
                    last.then_inc(ppe.sem, 1)
                    wait_apart(pe, pact.sem, pact.at(b, "vw1"), passed_pe)
                    for h in range(SH):
                        to = AA[(h % 2) * G:(h % 2) * G + G, cols(h // 2)]
                        last = mm(to, satT[:, h * G:(h + 1) * G], vw[:, h, :], start=True, stop=True)
                    last.then_inc(ppe.sem, 1)
                if p == 31:
                    pe.wait_ge(pact.sem, pact.at(b, "G"))
                    for t in range(T):
                        if t >= 2:
                            pe.wait_ge(pact.sem, pact.at(b, ("wT", t - 2)))
                        for c in range(4):
                            last = tr(A[t % 2][:, cols(c)], sw[:, t, cols(c)], ident[:, :])
                        last.then_inc(ppe.sem, 1)
                    pe.wait_ge(pact.sem, pact.at(b, ("wT", T - 1)))
                    for t in range(T):
                        for c in range(4):
                            mm(FC[:, cols(t)], swT[:, c, cols(t)], gout[:, c, :], start=(c == 0), stop=False)
                        last = mm(FC[:, cols(t)], ones[32:33, :], bout_r, start=False, stop=True)
                    last.then_inc(ppe.sem, 1)

            def step(b, has_front=True, has_post=True, first=False):
                for p in range(POS):
                    t, h = (p // HEADS + 1) % T, p % HEADS
                    if p % 2 == 0 and (p < POS - HEADS or has_front):
                        similarities(b + 1 if p >= POS - HEADS else b, t, h)
                    if has_post and p < 2 * HEADS:
                        attend(b - 1, p, 0)
                    for u in range(UNITS // 2):
                        weigh(b, p, u, first)
                    if has_post and p < 2 * HEADS:
                        attend(b - 1, p, 1)
                    for u in range(UNITS // 2, UNITS):
                        weigh(b, p, u, first)
                    if has_post and p < 2 * HEADS:
                        attend(b - 1, p, 2)
                    if has_front:
                        front(b + 1, p)
                    if has_post:
                        post(b - 1, p)

            setup()
            for p in range(POS):
                front(0, p)
            for p in range(0, HEADS, 2):
                similarities(0, 0, p, first=(p == 0))
            step(0, has_post=False, first=True)
            with nc.tensor.Fori(1, B - 1) as b:
                step(b)
            step(B - 1, has_front=False)
            for p in range(POS):
                if p < 2 * HEADS:
                    for part in range(3):
                        attend(B - 1, p, part)
                post(B - 1, p)

        @block.scalar
        def _(act):
            af = nc.scalar.activation

            def setup():
                for k in range(HEADS // 2):
                    act.wait_ge(merged, k + 1)
                    af(keymap[:, 2 * k:2 * k + 2, :, :].rearrange("p a b k -> p (a b k)"), A[k % 2][:, :],
                       ACT.Copy).then_inc(merged_copied, 1)
                act.wait_ge(setup_dve, 1)

            def deviation(mv, sd, wait_on, value, done):
                act.wait_ge(wait_on, value)
                af(sd[:, :], mv[:, :, 1], ACT.Sqrt, bias=eps[:, 0:1]).then_inc(done, 1)

            def evacuate(dst, src, chain, b, step_in, done, func=ACT.Copy):
                act.wait_ge(chain.sem, chain.at(b, step_in))
                af(dst, src, func).then_inc(done.sem, 1)

            def front(b, p, prologue=False):
                if p == 1:
                    deviation(f_mv, f_sd, fdve.sem, fdve.at(b, "mv"), fact.sem)
                    evacuate(up, FA[:, :], fpe, b, "Az", fact)
                if p == 3:
                    evacuate(h1_s[:, 0:2, :].rearrange("p a b -> p (a b)"), FB[:, :], fpe, b, "h1a", fact, ACT.Relu)
                    evacuate(h1_s[:, 2:4, :].rearrange("p a b -> p (a b)"), FA[:, :], fpe, b, "h1b", fact, ACT.Relu)
                if p == 5:
                    evacuate(ah[:, 0, :], FB[:, :], fpe, b, "Ah0", fact)
                    evacuate(ah[:, 1, :], FA[:, :], fpe, b, "Ah1", fact)
                if p in (7, 9):
                    for c in ((0, 1) if p == 7 else (2, 3)):
                        evacuate(h12[:, c, :], (FB, FA)[c % 2][:, :], fpe, b, f"h2{c}", fact, ACT.Relu)
                if p == 11:
                    evacuate(up, FB[:, :], fpe, b, "P", fact)
                if p == 21:
                    deviation(f_mv, f_sd, fdve.sem, fdve.at(b, "mv1"), fact.sem)
                if p == 23:
                    if not prologue:
                        act.wait_ge(sims, b * (POS // 2))
                        act.wait_ge(x_copied.sem, x_copied.at(b - 1, "X"))
                    evacuate(z1T[:, :], FB[:, :], fpe, b, "zT", fact)

            def copy_kv(b):
                act.wait_ge(pairs_out, (b + 1) * POS)
                act.wait_ge(ppe.sem, ppe.at(b - 1, "o"))
                af(KTa[:, :, :], KT[:, :, 0:2 * P], ACT.Copy)
                af(Va[:, :, :, :].rearrange("p a h d -> p (a h d)"),
                   V[:, 0:2, :, :].rearrange("p a h d -> p (a h d)"), ACT.Copy).then_inc(kv_copied.sem, 1)

            def copy_x(b, first=False):
                act.wait_ge(fact.sem, fact.at(b, "zT"))
                act.wait_ge(fdve.sem, fdve.at(b, "x1"))
                if not first:
                    act.wait_ge(pdve.sem, pdve.at(b - 1, "x2"))
                af(x1a[:, :, :], x1[:, :, :], ACT.Copy)
                af(z1Ta[:, :], z1T[:, :], ACT.Copy).then_inc(x_copied.sem, 1)

            def weights(b, t, h):
                pair = b * (POS // 2) + (t * HEADS + h) // 2
                act.wait_ge(keys.sem, keys.at(pair, "neg"))
                for k in range(2):
                    last = af(wts[:, t % 2, h + k, :], fs[:, k, :], ACT.Exp, bias=neg[:, k, :],
                              accum_out=wsum[:, t % 2, h + k:h + k + 1])
                last.then_inc(wexp, 1)

            def diagonals(b, p, u, first=False):
                t, h = p // HEADS, p % HEADS
                if u == 0:
                    act.wait_ge(wnorm, b * (POS // 2) + p // 2 + 1)
                if not (first and p == 0 and u < 2):
                    act.wait_ge(slots_free, b * (POS * UNITS) + p * UNITS + u - 1 + SLOTS)
                for j in range(UJ):
                    k = u * UJ + j
                    last = af(diag[:, u % 2, j, :], ident[:, :], ACT.Copy, scale=wts[:, t % 2, h, k:k + 1])
                last.then_inc(diags_made, 1)

            def attend(b, p, part):
                h, ia, ib = ATT_AT[p]
                if part == 0 and ia == 0:
                    evacuate(qo[:, h, :], AA[:, :], ape, b, ("q", h), aact)
                for i in (ia, ib):
                    k, bk, n = i % 2, A[i % 2], (i + 1) * P
                    if part == 0:
                        act.wait_ge(adve.sem, adve.at(b, ("n", h, i)))
                        af(prob[:, k, 0:n], bk[:, 0:n], ACT.Exp, bias=a_mx[:, k, 1:2], scale=ATT_SCALE,
                           accum_out=a_sm[:, k, 0:1]).then_inc(aact.sem, 1)
                for i in (ia, ib):
                    if part == 1:
                        act.wait_ge(adve.sem, adve.at(b, ("r", h, i)))
                        af(a_dg[:, i % 2, :], ident[:, :], ACT.Copy, scale=a_sm[:, i % 2, 1:2]).then_inc(aact.sem, 1)
                for i in (ia, ib):
                    if part == 1:
                        evacuate(probT[:, i % 2, 0:(i + 1) * P], A[i % 2][:, 0:(i + 1) * P], ape, b, ("T", h, i), aact)
                for i in (ia, ib):
                    if part == 2:
                        evacuate(qo[:, h, cols(i)], A[i % 2][:, 0:P], ape, b, ("v", h, i), aact)

            def lstm(b, k):
                u = LSTM[k]
                p, s, w0, n = u
                act.wait_ge(ppe.sem, ppe.at(b, ("gates", u)))
                for gate in range(4):
                    last = af(gates[:, gate, 0:n], A[gate // 2][:, (gate % 2) * 256:(gate % 2) * 256 + n],
                              ACT.Tanh if gate == 2 else ACT.Sigmoid, bias=lbias[:, p - 1, gate:gate + 1])
                last.then_inc(pact.sem, 1)
                act.wait_ge(pdve.sem, pdve.at(b, ("c" if s else "ig", u)))
                af(ctan[:, 0:n], cell[:, 0:n], ACT.Tanh).then_inc(pact.sem, 1)

            def post(b, p):
                if p == 17:
                    deviation(p_mv, p_sd, pdve.sem, pdve.at(b, "mv"), pact.sem)
                    evacuate(u2, AB[:, :], ppe, b, "Uz", pact)
                    evacuate(g1_s.rearrange("p t d -> p (t d)"), AA[:, :], ppe, b, "g1", pact, ACT.Relu)
                if p == 18:
                    evacuate(u2, AB[:, :], ppe, b, "Ug", pact)
                    evacuate(hT, AA[:, :], ppe, b, "g2", pact, ACT.Relu)
                if p in LSTM_AT:
                    for k in LSTM_AT[p]:
                        lstm(b, k)
                if p == 25:
                    deviation(p_mv, p_sd, pdve.sem, pdve.at(b, "mv3"), pact.sem)
                    evacuate(z3T, AB[:, :], ppe, b, "zT", pact)
                if p in (26, 27):
                    for t in ((0, 1) if p == 26 else (2, 3)):
                        act.wait_ge(pdve.sem, pdve.at(b, ("sb", t)))
                        af(sw[:, t, :], lg, ACT.Exp).then_inc(pact.sem, 1)
                if p == 28:
                    evacuate(stT, AA[0:SD, :], ppe, b, "st", pact)
                if p == 29:
                    evacuate(qs, AB[0:SD, :], ppe, b, "q", pact)
                    evacuate(ks, AA[0:SD, :], ppe, b, "k", pact)
                    evacuate(vs, AB[0:SD, :], ppe, b, "v", pact)
                    act.wait_ge(pdve.sem, pdve.at(b, "asb"))
                    af(sat, sat, ACT.Exp, scale=SLICE_SCALE).then_inc(pact.sem, 1)
                if p == 30:
                    evacuate(satT, AA[0:G, :], ppe, b, "aT", pact)
                    evacuate(vw[:, 0:4, :].rearrange("p h d -> p (h d)"), AB[0:G, :], ppe, b, "vw", pact)
                    evacuate(vw[:, 4:8, :].rearrange("p h d -> p (h d)"), FC[0:G, :], ppe, b, "vw", pact)
                    evacuate(gout.rearrange("p c d -> p (c d)"), AA[:, :], ppe, b, "G", pact)
                if p == 31:
                    for t in range(T):
                        evacuate(swT[:, :, cols(t)], A[t % 2][:, :].rearrange("p (c n) -> p c n", c=4), ppe, b,
                                 ("wT", t), pact)

            def step(b, has_front=True, has_post=True, first=False):
                if has_post:
                    copy_kv(b - 1)
                for p in range(POS):
                    if has_post and p < 2 * HEADS:
                        attend(b - 1, p, 0)
                    for u in range(UNITS // 2):
                        diagonals(b, p, u, first)
                    if has_post and p < 2 * HEADS:
                        attend(b - 1, p, 1)
                    for u in range(UNITS // 2, UNITS):
                        diagonals(b, p, u, first)
                    if p % 2 == 0 and (p < POS - HEADS or has_front):
                        weights(b + 1 if p >= POS - HEADS else b, (p // HEADS + 1) % T, p % HEADS)
                    if has_post and p < 2 * HEADS:
                        attend(b - 1, p, 2)
                    if has_front:
                        front(b + 1, p)
                    if has_post:
                        post(b - 1, p)
                    if p == 17:
                        copy_x(b, first=first)

            setup()
            for p in range(POS):
                front(0, p, prologue=True)
            for p in range(0, HEADS, 2):
                weights(0, 0, p)
            step(0, has_post=False, first=True)
            with nc.scalar.Fori(1, B - 1) as b:
                step(b)
            step(B - 1, has_front=False)
            copy_kv(B - 1)
            for p in range(POS):
                if p < 2 * HEADS:
                    for part in range(3):
                        attend(B - 1, p, part)
                post(B - 1, p)

        @block.vector
        def _(dve):
            tt, ts, tc, red = nc.vector.tensor_tensor, nc.vector.tensor_scalar, nc.vector.tensor_copy, nc.vector.tensor_reduce

            def wide(ap, axis, n):
                ap = ap.unsqueeze(axis)
                shape = list(ap.shape)
                shape[axis] = n
                return ap.to_broadcast(shape)

            def setup():
                nc.vector.memset(eps[:, :], EPS).then_inc(setup_dve, 1)
                dve.wait_ge(consts_in, LOADED)
                tt(adj2_s[:, :, :], adj_s[:, :, :], adj_s[:, :, :], ALU.mult).then_inc(setup_dve, 1)
                ts(tinv[:, :], temp_s[:, :], 0.1, 5.0, ALU.max, ALU.min).then_inc(setup_dve, 1)
                dve.wait_ge(setup_dve, 3)
                nc.vector.reciprocal(tinv[:, :], tinv[:, :]).then_inc(setup_dve, 1)
                dve.wait_ge(setup_dve, 4)
                dve.wait_ge(merged, HEADS // 2 + 1)
                tt(slmap[:, :].rearrange("p (h g) -> p h g", h=SH), FA[:, :].rearrange("p (h g) -> p h g", h=SH),
                   wide(tinv[:, :], 2, G), ALU.mult).then_inc(setup_dve, 1)
                dve.wait_ge(merged, HEADS // 2 + 2)
                tt(slb_r, FB[32:33, :], bsl_u, ALU.add).then_inc(setup_dve, 1)
                dve.wait_ge(setup_dve, 6)
                b3 = slb_r.rearrange("p (h g) -> p h g", h=SH)
                tt(b3, b3, wide(tinv[32:33, :], 2, G), ALU.mult).then_inc(setup_dve, 1)
                dve.wait_ge(merged, MERGED)
                tc(ra_r, FC[64:65, :]).then_inc(setup_dve, 1)
                tt(lbias[:, :, :], lbias[:, :, :], lbias2[:, :, :], ALU.add).then_inc(setup_dve, 1)

            def statistics(src, st, mv, chain, b, names):
                for t in range(T):
                    last = nc.vector.bn_stats(st[:, t, :], src[:, t, :])
                last.then_inc(chain.sem, 1)
                wait_apart(dve, chain.sem, chain.at(b, names[0]), passed_dve)
                for t in range(T):
                    last = nc.vector.bn_aggr(mv[:, t, :], st[:, t, :])
                last.then_inc(chain.sem, 1)

            def normalise(dst, src, mv, sd, rs, chain, b, names):
                nc.vector.reciprocal(rs[:, :], sd[:, :]).then_inc(chain.sem, 1)
                dve.wait_ge(chain.sem, chain.at(b, names[2]))
                for t in range(T):
                    last = ts(dst[:, t, :], src[:, t, :], mv[:, t, 0:1], rs[:, t:t + 1], ALU.subtract, ALU.mult)
                last.then_inc(chain.sem, 1)

            def front(b, p, first=False):
                if p == 0:
                    dve.wait_ge(x_in, 16 * (b + 1))
                    statistics(x_s, f_st, f_mv, fdve, b, ("st", "mv"))
                if p == 1:
                    dve.wait_ge(fact.sem, fact.at(b, "sd"))
                    if not first:
                        dve.wait_ge(fpe.sem, fpe.at(b - 1, "zT"))
                    normalise(z, x_s, f_mv, f_sd, f_rs, fdve, b, ("st", "mv", "rs"))
                if p == 19:
                    dve.wait_ge(fpe.sem, fpe.at(b, "y"))
                    if not first:
                        dve.wait_ge(x_copied.sem, x_copied.at(b - 1, "X"))
                    tt(x1[:, :, :], x_s[:, :, :], FA[:, :].rearrange("p (t d) -> p t d", t=T), ALU.add)\
                        .then_inc(fdve.sem, 1)
                    dve.wait_ge(fdve.sem, fdve.at(b, "x1"))
                    statistics(x1, f_st, f_mv, fdve, b, ("st1", "mv1"))
                if p == 21:
                    dve.wait_ge(fact.sem, fact.at(b, "sd1"))
                    normalise(z, x1, f_mv, f_sd, f_rs, fdve, b, ("st1", "mv1", "rs1"))

            def top_keys(b, t, h, first=False):
                pair = b * (POS // 2) + (t * HEADS + h) // 2
                K = keys

                def after(step):
                    wait_apart(dve, K.sem, K.at(pair, step), passed_dve)

                wait_apart(dve, sims, pair + 1, passed_dve)
                sims_s = S[:, :].rearrange("p (h q k) -> p h q k", h=2, q=2)
                four = [(k, q) for k in range(2) for q in range(2)]
                for k, q in four:
                    last = nc.vector.max(tv[:, k, q, 0:8], sims_s[:, k, q, :])
                last.then_inc(K.sem, 1)
                after("max")
                for k, q in four:
                    last = nc.vector.max_index(ti[:, k, q, 0:8], tv[:, k, q, 0:8], sims_s[:, k, q, :])
                last.then_inc(K.sem, 1)
                for k, q in four:
                    last = nc.vector.match_replace(rep[:, k, q, :], tv[:, k, q, 0:8], sims_s[:, k, q, :], TAKEN)
                last.then_inc(K.sem, 1)
                after("rep")
                for k, q in four:
                    last = nc.vector.max(tv[:, k, q, 8:16], rep[:, k, q, :])
                last.then_inc(K.sem, 1)
                after("max2")
                for k, q in four:
                    last = nc.vector.max_index(ti[:, k, q, 8:16], tv[:, k, q, 8:16], rep[:, k, q, :])
                last.then_inc(K.sem, 1)
                after("idx2")
                for k in range(2):
                    ts(tf[:, k, 0, :], ti[:, k, 0, :], float((h + k) * NKV), None, ALU.add)
                last = ts(tf[:, :, 1, :], ti[:, :, 1, :], float(NKEYS), None, ALU.mult)
                last.then_inc(K.sem, 1)
                after("f")
                for to, of in ((cs, tv), (ci, tf)):
                    for i, ni, nj, at in ROWS:
                        last = tt(to[:, :, at:at + ni * nj].rearrange("p h (i j) -> p h i j", i=ni),
                                  wide(of[:, :, 0, i:i + ni], 3, nj), wide(of[:, :, 1, 0:nj], 2, ni), ALU.add)
                last.then_inc(K.sem, 1)
                after("cand")
                if not first:
                    wait_apart(dve, wexp, pair, passed_dve)
                for k in range(2):
                    last = nc.vector.max(fs[:, k, 0:8], cs[:, k, :])
                last.then_inc(K.sem, 1)
                after("cmax")
                for k in range(2):
                    last = nc.vector.max_index(fp[:, k, 0:8], fs[:, k, 0:8], cs[:, k, :])
                last.then_inc(K.sem, 1)
                for k in range(2):
                    last = nc.vector.match_replace(crep[:, k, :], fs[:, k, 0:8], cs[:, k, :], TAKEN)
                last.then_inc(K.sem, 1)
                after("crep")
                for k in range(2):
                    last = nc.vector.max(fs[:, k, 8:16], crep[:, k, :])
                last.then_inc(K.sem, 1)
                after("cmax2")
                for k in range(2):
                    last = nc.vector.max_index(fp[:, k, 8:16], fs[:, k, 8:16], crep[:, k, :])
                last.then_inc(K.sem, 1)
                ts(neg[:, :, :], fs[:, :, 0:1], -1.0, None, ALU.mult).then_inc(K.sem, 1)
                after("cpos2")
                tc(fpf[:, :, :], fp[:, :, :]).then_inc(K.sem, 1)
                after("posf")
                for k in range(2):
                    if k:
                        after("row0")
                    tt(eq, wide(iota[:, :], 1, TOPK), wide(fpf[:, k, :], 2, NC), ALU.is_equal).then_inc(K.sem, 1)
                    after(f"eq{k}")
                    tt(eq, eq, wide(ci[:, k, :], 1, TOPK), ALU.mult).then_inc(K.sem, 1)
                    after(f"sel{k}")
                    with nc.allow_low_precision("one row number below 2^17 and zeros are summed, exact in float32"):
                        red(idx[:, t % 2, h + k, :], eq, AX, ALU.add).then_inc(K.sem, 1)

            def normalise_weights(b, t, h):
                pair = b * (POS // 2) + (t * HEADS + h) // 2
                dve.wait_ge(wexp, pair + 1)
                nc.vector.reciprocal(winv[:, t % 2, h:h + 2], wsum[:, t % 2, h:h + 2]).then_inc(winverted, 1)
                dve.wait_ge(winverted, pair + 1)
                w = wts[:, t % 2, h:h + 2, :]
                tt(w, w, wide(winv[:, t % 2, h:h + 2], 2, TOPK), ALU.mult).then_inc(wnorm, 1)

            def collect(b, p):
                t, h = p // HEADS, p % HEADS
                dve.wait_ge(slots_free, b * (POS * UNITS) + (p + 1) * UNITS + SLOTS)
                tc(KT[:, h, cols(t)], KV[p % 2][:, 0:P])
                tc(V[:, t, h, :], KV[p % 2][:, P:2 * P]).then_inc(pairs_out, 1)

            def attend(b, p, part):
                h, ia, ib = ATT_AT[p]
                for i in (ia, ib):
                    k, n = i % 2, (i + 1) * P
                    if part == 0:
                        dve.wait_ge(ape.sem, ape.at(b, ("s", h, i)))
                        d = A[k][:, cols(i)]
                        tt(d, d, mask[:, :], ALU.add).then_inc(adve.sem, 1)
                        dve.wait_ge(adve.sem, adve.at(b, ("m", h, i)))
                        nc.vector.reduce_max(a_mx[:, k, 0:1], A[k][:, 0:n], AX).then_inc(adve.sem, 1)
                        dve.wait_ge(adve.sem, adve.at(b, ("x", h, i)))
                        ts(a_mx[:, k, 1:2], a_mx[:, k, 0:1], -ATT_SCALE, None, ALU.mult).then_inc(adve.sem, 1)
                    if part == 1:
                        dve.wait_ge(aact.sem, aact.at(b, ("e", h, i)))
                        nc.vector.reciprocal(a_sm[:, k, 1:2], a_sm[:, k, 0:1]).then_inc(adve.sem, 1)

            def lstm(b, k):
                u = LSTM[k]
                p, s, w0, n = u
                gi, gf, gg, go = (gates[:, k, 0:n] for k in range(4))
                dve.wait_ge(pact.sem, pact.at(b, ("gates", u)))
                c, product = cell[:, 0:n], ig[:, 0:n]
                if s:
                    tt(c, c, gf, ALU.mult).then_inc(pdve.sem, 1)
                    tt(product, gi, gg, ALU.mult).then_inc(pdve.sem, 1)
                    dve.wait_ge(pdve.sem, pdve.at(b, ("ig", u)))
                    tt(c, c, product, ALU.add).then_inc(pdve.sem, 1)
                else:
                    tt(c, gi, gg, ALU.mult).then_inc(pdve.sem, 1)
                dve.wait_ge(pact.sem, pact.at(b, ("tc", u)))
                if s == p - 1:
                    to = hT[:, 0:(N // p) * p].rearrange("q (w p) -> q p w", p=p)[:, s, w0:w0 + n]
                else:
                    to = hid[:, 0:n]
                tt(to, go, ctan[:, 0:n], ALU.mult).then_inc(pdve.sem, 1)

            def post(b, p):
                if p == 16:
                    dve.wait_ge(ppe.sem, ppe.at(b, "wo"))
                    dve.wait_ge(stored, 16 * (b + 1))
                    tt(x2[:, :, :], x1a[:, :, :], AA[:, :].rearrange("p (t d) -> p t d", t=T), ALU.add)\
                        .then_inc(pdve.sem, 1)
                    dve.wait_ge(pdve.sem, pdve.at(b, "x2"))
                    statistics(x2, p_st, p_mv, pdve, b, ("st", "mv"))
                if p == 17:
                    dve.wait_ge(pact.sem, pact.at(b, "sd"))
                    normalise(z2, x2, p_mv, p_sd, p_rs, pdve, b, ("st", "mv", "rs"))
                if p in LSTM_AT:
                    for k in LSTM_AT[p]:
                        lstm(b, k)
                if p == 25:
                    dve.wait_ge(ppe.sem, ppe.at(b, "ht"))
                    tt(x2[:, :, :], x2[:, :, :], AA[:, :].rearrange("p (t d) -> p t d", t=T), ALU.add)\
                        .then_inc(pdve.sem, 1)
                    dve.wait_ge(pdve.sem, pdve.at(b, "x3"))
                    statistics(x2, p_st, p_mv, pdve, b, ("st3", "mv3"))
                    dve.wait_ge(pact.sem, pact.at(b, "sd3"))
                    normalise(z2, x2, p_mv, p_sd, p_rs, pdve, b, ("st3", "mv3", "rs3"))
                if p in (26, 27):
                    for t in ((0, 1) if p == 26 else (2, 3)):
                        logits = A[t % 2][:, :].rearrange("p (h g) -> p h g", h=SH)
                        w = sw[:, t, :].rearrange("p (h g) -> p h g", h=SH)
                        dve.wait_ge(ppe.sem, ppe.at(b, ("lg", t)))
                        nc.vector.reduce_max(s_mx[:, :], logits, AX).then_inc(pdve.sem, 1)
                        dve.wait_ge(pdve.sem, pdve.at(b, ("mx", t)))
                        if t:
                            dve.wait_ge(pact.sem, pact.at(b, ("ex", t - 1)))
                        tt(lg.rearrange("p (h g) -> p h g", h=SH), logits, wide(s_mx[:, :], 2, G), ALU.subtract)\
                            .then_inc(pdve.sem, 1)
                        dve.wait_ge(pact.sem, pact.at(b, ("ex", t)))
                        red(s_sm[:, 0, :], w, AX, ALU.add).then_inc(pdve.sem, 1)
                        dve.wait_ge(pdve.sem, pdve.at(b, ("sm", t)))
                        nc.vector.reciprocal(s_sm[:, 1, :], s_sm[:, 0, :]).then_inc(pdve.sem, 1)
                        dve.wait_ge(pdve.sem, pdve.at(b, ("rc", t)))
                        tt(w, w, wide(s_sm[:, 1, :], 2, G), ALU.mult).then_inc(pdve.sem, 1)
                if p == 28:
                    dve.wait_ge(ppe.sem, ppe.at(b, "nr"))
                    ts(rn, AB[:, :], EPS, None, ALU.add).then_inc(pdve.sem, 1)
                    dve.wait_ge(pdve.sem, pdve.at(b, "n1"))
                    nc.vector.reciprocal(rn, rn).then_inc(pdve.sem, 1)
                    dve.wait_ge(pdve.sem, pdve.at(b, "n2"))
                    tt(Yn, AA[:, :], rn, ALU.mult).then_inc(pdve.sem, 1)
                    tt(nn_r, AB[0:1, :], rn[0:1, :], ALU.mult).then_inc(pdve.sem, 1)
                if p == 29:
                    dve.wait_ge(ppe.sem, ppe.at(b, "sim"))
                    scores = AA[0:G, :].rearrange("p (h g) -> p h g", h=SH)
                    w = sat.rearrange("p (h g) -> p h g", h=SH)
                    nc.vector.reduce_max(s_mx[0:G, :], scores, AX).then_inc(pdve.sem, 1)
                    dve.wait_ge(pdve.sem, pdve.at(b, "amx"))
                    tt(w, scores, wide(s_mx[0:G, :], 2, G), ALU.subtract).then_inc(pdve.sem, 1)
                    dve.wait_ge(pact.sem, pact.at(b, "aex"))
                    red(s_sm[0:G, 0, :], w, AX, ALU.add).then_inc(pdve.sem, 1)
                    dve.wait_ge(pdve.sem, pdve.at(b, "asm"))
                    nc.vector.reciprocal(s_sm[0:G, 1, :], s_sm[0:G, 0, :]).then_inc(pdve.sem, 1)
                    dve.wait_ge(pdve.sem, pdve.at(b, "arc"))
                    tt(w, w, wide(s_sm[0:G, 1, :], 2, G), ALU.mult).then_inc(pdve.sem, 1)
                if p == 31:
                    dve.wait_ge(ppe.sem, ppe.at(b, "o"))
                    tt(x2[:, :, :], x2[:, :, :], FC[:, :].rearrange("p (t d) -> p t d", t=T), ALU.add)\
                        .then_inc(pdve.sem, 1)

            def step(b, has_front=True, has_post=True):
                for p in range(POS):
                    ahead = (b + 1 if p >= POS - HEADS else b, (p // HEADS + 1) % T)
                    if has_post and p < 2 * HEADS:
                        attend(b - 1, p, 0)
                        attend(b - 1, p, 1)
                    if p < POS - HEADS or has_front:
                        if p % 2 == 0:
                            top_keys(*ahead, p % HEADS)
                        else:
                            normalise_weights(*ahead, p % HEADS - 1)
                    collect(b, p)
                    if has_front:
                        front(b + 1, p)
                    if has_post:
                        post(b - 1, p)

            setup()
            for p in range(POS):
                front(0, p, first=True)
            for p in range(0, HEADS, 2):
                top_keys(0, 0, p, first=(p == 0))
                normalise_weights(0, 0, p)
            step(0, has_post=False)
            with nc.vector.Fori(1, B - 1) as b:
                step(b)
            step(B - 1, has_front=False)
            for p in range(POS):
                if p < 2 * HEADS:
                    attend(B - 1, p, 0)
                    attend(B - 1, p, 1)
                post(B - 1, p)


def kernel(**a):
    import numpy as np
    import concourse.bacc as bacc
    from concourse.bass_utils import run_bass_kernel_spmd

    f = np.float32
    a = {k: np.asarray(v) for k, v in a.items()}
    eye = np.eye(P, dtype=f)
    arrays = {
        "x": a["x"], "adjT": a["adj"].T, "w1": a["L0_gnn_W1"], "w2": a["L0_gnn_W2"], "w3": a["L0_gnn_W3"],
        "wqpkT": a["L0_ffn_Wq_pk"].reshape(D, 2 * HEADS, DK).transpose(2, 1, 0),
        "keysT": a["L0_ffn_pk_keys"].transpose(3, 0, 2, 1).reshape(DK, 2 * HEADS, NKEYS),
        "wq": a["L0_ffn_Wq"],
        "table": np.concatenate([a["L0_ffn_keys_table"], a["L0_ffn_values_table"]], axis=1),
        "wo": a["L0_ffn_Wo"], "wg0": a["L1_gnn_Wg0"], "wg1": a["L1_gnn_Wg1"],
        "bg0": a["L1_gnn_bg0"].reshape(1, D), "bg1": a["L1_gnn_bg1"].reshape(1, D),
        "wihT": a["L1_gnn_Wih"].transpose(2, 0, 1), "whhT": a["L1_gnn_Whh"].transpose(2, 0, 1),
        "bih": a["L1_gnn_bih"].reshape(SKIPS, 4, D).transpose(2, 0, 1),
        "bhh": a["L1_gnn_bhh"].reshape(SKIPS, 4, D).transpose(2, 0, 1),
        "wfx": a["L1_ffn_W_fx"], "bfx": a["L1_ffn_b_fx"].reshape(1, SH * SD),
        "wxT": a["L1_ffn_W_x"].reshape(D, SH, SD).transpose(2, 1, 0), "bx": a["L1_ffn_b_x"].reshape(SH, SD).T,
        "wsl": a["L1_ffn_W_slice"], "bsl": np.tile(a["L1_ffn_b_slice"].reshape(1, G), (1, SH)),
        "temp": np.tile(a["L1_ffn_temperature"].reshape(1, SH), (P, 1)),
        "wqs": a["L1_ffn_W_q"], "wks": a["L1_ffn_W_k"], "wvs": a["L1_ffn_W_v"], "wout": a["L1_ffn_W_out"],
        "bout": a["L1_ffn_b_out"].reshape(1, D),
        "c_ident": eye, "c_mask": np.triu(np.full((P, P), MASKED, f), 1),
        "c_iota": np.tile(np.arange(NC, dtype=f), (P, 1)), "c_ones": np.ones((P, P), f),
    }
    order = ["x", "adjT", "w1", "w2", "w3", "wqpkT", "keysT", "wq", "table", "wo", "wg0", "wg1", "bg0", "bg1",
             "wihT", "whhT", "bih", "bhh", "wfx", "bfx", "wxT", "bx", "wsl", "bsl", "temp", "wqs", "wks", "wvs",
             "wout", "bout", "c_ident", "c_mask", "c_iota", "c_ones"]
    nc = bacc.Bacc("TRN2", target_bir_lowering=False, num_devices=1)
    feed, args = {}, []
    for name in order:
        v = np.ascontiguousarray(arrays[name])
        feed[f"in_{name}"] = v
        args.append(nc.dram_tensor(f"in_{name}", v.shape, mybir.dt.from_np(v.dtype), kind="ExternalInput").ap())
    result = nc.dram_tensor("result", (B, N, D), F32, kind="ExternalOutput").ap()
    build(nc, *args, result)
    r = run_bass_kernel_spmd(nc, [feed], core_ids=[0])
    return r.results[0]["result"]
```

```python
from contextlib import ExitStack

import concourse.bass as bass
from concourse import mybir

F32 = mybir.dt.float32
U32 = mybir.dt.uint32
ALU = mybir.AluOpType
ACT = mybir.ActivationFunctionType
AX = mybir.AxisListType.X

P = 128
B, N, D = 16, 512, 128
T = N // P
H1, H2 = 256, 512
HEADS, DK, NKEYS, TOPK = 8, 64, 128, 16
NKV = NKEYS * NKEYS
SKIPS = 4
SH, SD, G = 8, 64, 64
POS = T * HEADS
UJ = 4
UNITS = TOPK // UJ
SLOTS = 8
EPS = 1e-5
MASKED = -1.0e30
TAKEN = -3.0e38
ATT_SCALE = float(D) ** -0.5
SLICE_SCALE = float(SD) ** -0.5

ROWS = []
_at = 0
for _i, _k, _n in ((0, 1, 16), (1, 1, 8), (2, 1, 5), (3, 1, 4), (4, 1, 3), (5, 3, 2), (8, 8, 1)):
    ROWS.append((_i, _k, _n, _at))
    _at += _k * _n
NC = _at

LSTM = [(1, 0, 0, 256), (1, 0, 256, 256)] + [(p, s, 0, N // p) for p in range(2, SKIPS + 1) for s in range(p)]

FRONT_AT = {"stats": 0, "z": 1, "Az": 3, "h1": 5, "Ah0": 8, "Ah1": 10, "h20": 13, "h21": 15, "h22": 17, "h23": 19,
            "P": 22, "y": 75, "z1": 77, "zT": 90}
POST_AT = {"wo": 67, "z": 68, "Uz": 69, "g1": 70, "Ug": 71, "g2": 72, "ht": 96, "z3": 97, "zT": 98, "lg0": 99,
           "lg1": 100, "lg2": 101, "lg3": 102, "Y": 104, "st": 106, "qk": 107, "v": 108, "sim": 109, "aT": 111,
           "vw": 112, "G": 113, "wT0": 114, "wT1": 115, "wT2": 116, "wT3": 117, "o": 119}
LSTM_AT = {74 + 2 * k: k for k in range(len(LSTM))}
TOP_AT = {0: "best 8 keys", 2: "next 8 keys", 4: "pairs", 6: "rows 0", 7: "rows 1"}
COPY_X_AT = 70
LAST_OF = {u[0]: u for u in LSTM}

ATT_AT = [(p // 2, 2 * (p % 2), 2 * (p % 2) + 1) for p in range(2 * HEADS)]


class Signal:

    def __init__(self, sem, steps, start=0):
        self.sem, self.n, self.start = sem, len(steps), start
        self.index = {s: k for k, s in enumerate(steps)}
        assert len(self.index) == self.n

    def at(self, b, step):
        return b * self.n + self.index[step] + 1 + self.start


def wait_apart(engine, sem, value, passed):
    engine.wait_ge(sem, value)
    engine.sem_inc(passed, 1)


FRONT_PE = ["Az", "h1a", "h1b", "Ah0", "Ah1"] + [f"h2{c}" for c in range(4)] + ["P", "y", "zT"]
FRONT_ACT = ["sd", "Az", "h1a", "h1b", "Ah0", "Ah1"] + [f"h2{c}" for c in range(4)] + ["P", "sd1", "zT"]
FRONT_DVE = ["st", "mv", "rs", "z", "x1", "st1", "mv1", "rs1", "z1"]
ATT_PE, ATT_ACT, ATT_DVE = [], [], []
for _h, _a, _b in ATT_AT:
    ATT_PE += [("q", _h)] * (_a == 0) + [(k, _h, i) for k in "sTv" for i in (_a, _b)]
    ATT_ACT += [("q", _h)] * (_a == 0) + [(k, _h, i) for k in "edTo" for i in (_a, _b)]
    ATT_DVE += [(k, _h, i) for i in (_a, _b) for k in "mxn"] + [("r", _h, i) for i in (_a, _b)]
POST_PE = (["wo", "Uz", "g1", "Ug", "g2"] + [("gates", u) for u in LSTM] + ["ht", "zT"]
           + [("lg", t) for t in range(T)] + ["Y", "nr", "st", "q", "k", "v", "sim", "aT", "vw", "G"]
           + [("wT", t) for t in range(T)] + ["o"])
POST_ACT = (["sd", "Uz", "g1", "Ug", "g2"] + [(k, u) for u in LSTM for k in ("gates", "tc")] + ["sd3", "zT"]
            + [("ex", t) for t in range(T)] + ["st", "q", "k", "v", "aex", "aT", "vw0", "vw1", "G"]
            + [("wT", t) for t in range(T)])
POST_DVE = (["x2", "st", "mv", "rs", "z"]
            + [(k, u) for u in LSTM for k in ((("fc",) if u[1] else ()) + ("ig",) + (("c",) if u[1] else ()) + ("h",))]
            + ["x3", "st3", "mv3", "rs3", "z3"] + [(k, t) for t in range(T) for k in ("mx", "sb", "sm", "rc", "sw")]
            + ["n1", "n2", "Yn", "nn", "amx", "asb", "asm", "arc", "at", "o"])
KEYS_DVE = ["max", "idx", "rep", "max2", "idx2", "f", "cand", "cmax", "cpos", "crep", "cmax2", "cpos2", "neg",
            "posf"] + [f"{k}{h}" for h in range(2) for k in ("eq", "sel", "row")]
COPIES = ["KV", "X"]


def build(nc, x, adjT, w1, w2, w3, wqpkT, keysT, wq, table, wo, wg0, wg1, bg0, bg1, wihT, whhT, bih, bhh,
          wfx, bfx, wxT, bx, wsl, bsl, temp, wqs, wks, wvs, wout, bout, c_ident, c_mask, c_iota, c_ones, out):
    with ExitStack() as ctx:
        def sb(name, shape, dt=F32):
            return ctx.enter_context(nc.sbuf_tensor(name, shape, dt))

        def bank(name):
            return ctx.enter_context(nc.psum_tensor(name, [P, 512], F32))

        def sem(name):
            return ctx.enter_context(nc.semaphore(name))

        adj_s = sb("adj_s", [P, T, N])
        adj2_s = sb("adj2_s", [P, T, N])
        w1_s, w2_s, w3_s = sb("w1_s", [P, H1]), sb("w2_s", [P, 2, H2]), sb("w3_s", [P, 4, D])
        keymap = sb("keymap", [P, HEADS, 2, NKEYS])
        wq_s, wo_s = sb("wq_s", [P, HEADS, D]), sb("wo_s", [P, HEADS, D])
        wg0_s, wg1_s = sb("wg0_s", [P, D]), sb("wg1_s", [P, D])
        lw = sb("lw", [P, 2, 2, 4 * D])
        lbias, lbias2 = sb("lbias", [P, SKIPS, 4]), sb("lbias2", [P, SKIPS, 4])
        wfx_s, slmap = sb("wfx_s", [P, SH * SD]), sb("slmap", [P, SH * G])
        wqs_s, wks_s, wvs_s = (sb(n, [SD, SD]) for n in ("wqs_s", "wks_s", "wvs_s"))
        wout_s = sb("wout_s", [SD, SH, D])
        rows = sb("rows", [65, 2 * 512])
        bfx_r, nn_r = rows[0:1, 0:512], rows[0:1, 512:1024]
        slb_r, bout_r = rows[32:33, 0:512], rows[32:33, 512:512 + D]
        ra_r, bg0_r, bg1_r = rows[64:65, 0:512], rows[64:65, 512:512 + D], rows[64:65, 512 + D:512 + 2 * D]
        temp_s, tinv = sb("temp_s", [P, SH]), sb("tinv", [P, SH])
        ident, mask, iota, ones = sb("ident", [P, P]), sb("mask", [P, P]), sb("iota", [P, NC]), sb("ones", [P, P])
        eps = sb("eps", [P, 1])
        ring = sb("ring", [P, SLOTS, UJ, 2 * D])
        diag = sb("diag", [P, 2, UJ, P])
        idx = sb("idx", [P, 2, HEADS, TOPK], U32)
        wts, wsum, winv = sb("wts", [P, 2, HEADS, TOPK]), sb("wsum", [P, 2, HEADS]), sb("winv", [P, 2, HEADS])
        KT, V = sb("KT", [P, HEADS, N]), sb("V", [P, T, HEADS, D])
        tv, ti, tf = sb("tv", [P, 2, 2, TOPK]), sb("ti", [P, 2, 2, TOPK], U32), sb("tf", [P, 2, 2, TOPK])
        work = sb("work", [P, TOPK * NC])
        rep = work[:, 0:4 * NKEYS].rearrange("p (h q k) -> p h q k", h=2, q=2)
        eq = work[:, :].rearrange("p (k c) -> p k c", c=NC)
        cs, ci, crep = sb("cs", [P, 2, NC]), sb("ci", [P, 2, NC]), sb("crep", [P, 2, NC])
        fs, fp, fpf = sb("fs", [P, 2, TOPK]), sb("fp", [P, 2, TOPK], U32), sb("fpf", [P, 2, TOPK])
        neg = sb("neg", [P, 2, 1])
        x_s = sb("x_s", [P, T, D])
        h12, ah = sb("h12", [P, 4, 512]), sb("ah", [P, 2, N])
        up, z = ah[:, 0, :], h12[:, 3, :].rearrange("p (t d) -> p t d", t=T)
        h1_s = h12[:, 0:2, :].rearrange("p a (b c) -> p (a b) c", b=2)
        x1, z1T = sb("x1", [P, T, D]), sb("z1T", [P, N])
        f_st, f_mv, f_sd, f_rs = (sb(n, s) for n, s in
                                  (("f_st", [P, T, 6]), ("f_mv", [P, T, 2]), ("f_sd", [P, T]), ("f_rs", [P, T])))
        KTa, Va = sb("KTa", [P, HEADS, 2 * P]), sb("Va", [P, 2, HEADS, D])
        x1a, z1Ta = sb("x1a", [P, T, D]), sb("z1Ta", [P, N])
        qo = sb("qo", [P, HEADS, N])
        prob, probT = sb("prob", [P, 2, N]), sb("probT", [P, 2, N])
        a_mx, a_sm, a_dg = sb("a_mx", [P, 2, 2]), sb("a_sm", [P, 2, 2]), sb("a_dg", [P, 2, P])
        x2 = sb("x2", [P, T, D])
        p_st, p_mv, p_sd, p_rs = (sb(n, s) for n, s in
                                  (("p_st", [P, T, 6]), ("p_mv", [P, T, 2]), ("p_sd", [P, T]), ("p_rs", [P, T])))
        s_mx, s_sm = sb("s_mx", [P, SH]), sb("s_sm", [P, 2, SH])
        left = qo[:, :, :].rearrange("p h n -> p (h n)")
        z2 = left[:, 0:512].rearrange("p (t d) -> p t d", t=T)
        u2, g1_s, hT = left[:, 512:1024], left[:, 1024:1536].rearrange("p (t d) -> p t d", t=T), left[:, 1536:2048]
        gates = left[:, 2048:3072].rearrange("p (k n) -> p k n", k=4)
        cell, ctan, hid, ig = (left[:, 3072 + 256 * k:3072 + 256 * (k + 1)] for k in range(4))
        z3T, lg, Yn, rn = u2, left[:, 1024:1536], left[:, 2048:2560], left[:, 2560:3072]
        sw = KTa[:, :, :].rearrange("p h n -> p (h n)").rearrange("p (t n) -> p t n", t=T)
        swT = Va[:, :, :, :].rearrange("p a h d -> p (a h d)").rearrange("p (c n) -> p c n", c=T)
        stT, qs, ks, vs = (left[0:SD, 512 * k:512 * (k + 1)] for k in (2, 3, 6, 7))
        sat, satT = prob[0:G, 0, :], prob[0:G, 1, :]
        vw = left[0:G, 2048:3072].rearrange("p (h d) -> p h d", h=SH)
        gout = probT[:, 0, :].rearrange("p (c d) -> p c d", c=4)
        spare = ring[:, :, :, :].rearrange("p a b c -> p (a b c)")
        wqpk_u = spare[0:DK, 0:2048].rearrange("p (a f) -> p a f", a=2 * HEADS)
        keys_u = spare[0:DK, 2048:4096].rearrange("p (a k) -> p a k", a=2 * HEADS)
        wx_u = spare[0:SD, 4096:5120].rearrange("p (h f) -> p h f", h=SH)
        wsl_u, bx_u, bsl_u = spare[0:SD, 5120:5184], spare[0:SD, 5184:5192], spare[32:33, 5248:5760]

        S, KV0, KV1, FA, FB, FC, AA, AB = (bank(f"bank_{n}") for n in "S KV0 KV1 FA FB FC AA AB".split())
        A, KV = (AA, AB), (KV0, KV1)

        consts_in, x_in, stored = sem("consts_in"), sem("x_in"), sem("stored")
        passed_dve, passed_pe, passed_pool = sem("passed_dve"), sem("passed_pe"), sem("passed_pool")
        lw_in = [sem("lw_in0"), sem("lw_in1")]
        merged, merged_copied = sem("merged"), sem("merged_copied")
        setup_dve = sem("setup_dve")
        gathered = [sem(f"gathered{k}") for k in range(SLOTS)]
        slots_free, diags_made, pairs_out = sem("slots_free"), sem("diags_made"), sem("pairs_out")
        sims = sem("sims")
        wexp, winverted, wnorm = sem("wexp"), sem("winverted"), sem("wnorm")
        fpe, fact, fdve = (Signal(sem(n), s) for n, s in
                           (("front_products", FRONT_PE), ("front_copies", FRONT_ACT), ("front_sums", FRONT_DVE)))
        ape, aact, adve = (Signal(sem(n), s) for n, s in
                           (("att_products", ATT_PE), ("att_copies", ATT_ACT), ("att_sums", ATT_DVE)))
        ppe, pact, pdve = (Signal(sem(n), s, start) for n, s, start in
                           (("post_products", POST_PE, len(POST_PE)), ("post_copies", POST_ACT, 0), ("post_sums", POST_DVE, 0)))
        keys = Signal(sem("keys_done"), KEYS_DVE)
        copied = [Signal(sem(f"copied_{n}"), [n]) for n in COPIES]
        kv_copied, x_copied = copied

        block = ctx.enter_context(nc.Block())
        loads = [(adj_s[:, :, :], adjT.rearrange("(t p) n -> p t n", p=P)), (w1_s[:, :], w1),
                 (w2_s[:, :, :], w2.rearrange("(c p) n -> p c n", p=P)),
                 (w3_s[:, :, :], w3.rearrange("(c p) n -> p c n", p=P)),
                 (wqpk_u, wqpkT), (keys_u, keysT), (wq_s[:, :, :], wq.rearrange("p (h d) -> p h d", h=HEADS)),
                 (wo_s[:, :, :], wo.rearrange("(h p) d -> p h d", p=P)), (wg0_s[:, :], wg0), (wg1_s[:, :], wg1),
                 (lbias[:, :, :], bih),
                 (lbias2[:, :, :], bhh), (wfx_s[:, :], wfx), (wx_u, wxT), (wsl_u, wsl), (bx_u, bx), (bsl_u, bsl),
                 (temp_s[:, :], temp), (wqs_s[:, :], wqs), (wks_s[:, :], wks), (wvs_s[:, :], wvs),
                 (wout_s[:, :, :], wout.rearrange("(h p) d -> p h d", p=SD)), (bfx_r, bfx), (bg0_r, bg0),
                 (bg1_r, bg1), (bout_r, bout), (ident[:, :], c_ident), (mask[:, :], c_mask), (iota[:, :], c_iota),
                 (ones[:, :], c_ones)]
        LOADED = 16 * len(loads)
        MERGED, SETUP_DVE = HEADS // 2 + 3, 9

        def cols(t):
            return slice(t * P, (t + 1) * P)

        @block.sync
        def _(sp):
            def load_x(b, first=False):
                if not first:
                    sp.wait_ge(fdve.sem, fdve.at(b - 1, "x1"))
                sp.dma_start(x_s[:, :, :], x[b].rearrange("(t p) d -> p t d", p=P)).then_inc(x_in, 16)

            def store(b):
                sp.wait_ge(pdve.sem, pdve.at(b, "o"))
                sp.dma_start(out[b].rearrange("(t p) d -> p t d", p=P), x2[:, :, :]).then_inc(stored, 16)

            sp.sem_inc(stored, 16)
            def load_lstm(b):
                for p in range(1, SKIPS + 1):
                    if p > 2:
                        sp.wait_ge(ppe.sem, ppe.at(b, ("gates", LAST_OF[p - 2])))
                    else:
                        sp.wait_ge(ppe.sem, ppe.at(b - 1, ("gates", LAST_OF[p + 2])))
                    sp.dma_start(lw[:, p % 2, 0, :], wihT[:, p - 1, :]).then_inc(lw_in[p % 2], 16)
                    sp.dma_start(lw[:, p % 2, 1, :], whhT[:, p - 1, :]).then_inc(lw_in[p % 2], 16)

            load_x(0, True)
            for dst, src in loads:
                sp.dma_start(dst, src).then_inc(consts_in, 16)
            load_x(1)
            with nc.sync.Fori(1, B - 1) as b:
                load_x(b + 1)
                load_lstm(b - 1)
                store(b - 1)
            for b in (B - 2, B - 1):
                load_lstm(b)
                store(b)
            sp.wait_ge(stored, 16 * (B + 1))

        @block.gpsimd
        def _(pool):
            pool.wait_ge(merged, MERGED)
            pool.wait_ge(setup_dve, SETUP_DVE)
            with nc.gpsimd.Fori(0, B * T // 2) as m:
                for r in range(2 * HEADS):
                    wait_apart(pool, keys.sem, keys.at(m * HEADS + r // 2, "row1"), passed_pool)
                    for u in range(UNITS):
                        slot = (UNITS * r + u) % SLOTS
                        wait_apart(pool, slots_free, m * (2 * HEADS * UNITS) + UNITS * r + u + 1, passed_pool)
                        for j in range(UJ):
                            k = u * UJ + j
                            nc.gpsimd.indirect_dma_start(
                                ring[:, slot, j, :], None, table,
                                bass.IndirectOffsetOnAxis(ap=idx[:, r // HEADS, r % HEADS, k:k + 1], axis=0),
                                bounds_check=HEADS * NKV - 1, oob_is_err=False).then_inc(gathered[slot], 16)

        @block.tensor
        def _(pe):
            mm, tr = nc.tensor.matmul, nc.tensor.transpose

            def setup():
                pe.wait_ge(consts_in, LOADED)
                for h in range(HEADS):
                    if h % 2 == 0 and h >= 4:
                        pe.wait_ge(merged_copied, h // 2 - 1)
                    for p in range(2):
                        last = mm(A[h // 2 % 2][:, cols(2 * (h % 2) + p)], wqpk_u[:, p * HEADS + h, :],
                                  keys_u[:, p * HEADS + h, :], start=True, stop=True)
                    if h % 2:
                        last.then_inc(merged, 1)
                for h in range(SH):
                    last = mm(FA[:, h * G:(h + 1) * G], wx_u[:, h, :], wsl_u, start=True, stop=True)
                last.then_inc(merged, 1)
                for h in range(SH):
                    last = mm(FB[32:33, h * G:(h + 1) * G], bx_u[:, h:h + 1], wsl_u, start=True, stop=True)
                last.then_inc(merged, 1)
                for m in range(T):
                    last = mm(FC[64:65, :], ones[:, 0:1], adj_s[:, m, :], start=(m == 0), stop=(m == T - 1))
                last.then_inc(merged, 1)
                pe.sem_inc(slots_free, SLOTS)
                pe.sem_inc(ppe.sem, ppe.n)
                pe.wait_ge(merged_copied, HEADS // 2)
                pe.wait_ge(setup_dve, SETUP_DVE)

            def front(b, at):
                if at == FRONT_AT["Az"]:
                    pe.wait_ge(fdve.sem, fdve.at(b, "z"))
                    for m in range(T):
                        last = mm(FA[:, :], z[:, m, :], adj2_s[:, m, :], start=(m == 0), stop=(m == T - 1))
                    last.then_inc(fpe.sem, 1)
                if at == FRONT_AT["h1"]:
                    pe.wait_ge(fact.sem, fact.at(b, "Az"))
                    for half, k in ((FB, "h1a"), (FA, "h1b")):
                        for t in range(2):
                            tt = t + 2 * (k == "h1b")
                            last = mm(half[:, t * H1:(t + 1) * H1], up[:, cols(tt)], w1_s[:, :], start=True, stop=True)
                        last.then_inc(fpe.sem, 1)
                for c in range(2):
                    if at == FRONT_AT[f"Ah{c}"]:
                        pe.wait_ge(fact.sem, fact.at(b, "h1b"))
                        for m in range(T):
                            last = mm((FB, FA)[c][:, :], h1_s[:, m, cols(c)], adj2_s[:, m, :], start=(m == 0),
                                      stop=(m == T - 1))
                        last.then_inc(fpe.sem, 1)
                for c in range(4):
                    if at == FRONT_AT[f"h2{c}"]:
                        pe.wait_ge(fact.sem, fact.at(b, "Ah1" if c < 2 else f"h2{c - 2}"))
                        for g in range(2):
                            last = mm((FB, FA)[c % 2][:, :], w2_s[:, g, cols(c)], ah[:, g, :], start=(g == 0), stop=(g == 1))
                        last.then_inc(fpe.sem, 1)
                if at == FRONT_AT["P"]:
                    pe.wait_ge(fact.sem, fact.at(b, "h23"))
                    for t in range(T):
                        for c in range(4):
                            last = mm(FB[:, cols(t)], h12[:, c, cols(t)], w3_s[:, c, :], start=(c == 0), stop=(c == 3))
                    last.then_inc(fpe.sem, 1)
                if at == FRONT_AT["y"]:
                    pe.wait_ge(fact.sem, fact.at(b, "P"))
                    for t in range(T):
                        for m in range(T):
                            last = mm(FA[:, cols(t)], adj2_s[:, m, cols(t)], up[:, cols(m)], start=(m == 0), stop=(m == T - 1))
                    last.then_inc(fpe.sem, 1)
                if at == FRONT_AT["zT"]:
                    pe.wait_ge(fdve.sem, fdve.at(b, "z1"))
                    for t in range(T):
                        last = tr(FB[:, cols(t)], z[:, t, :], ident[:, :])
                    last.then_inc(fpe.sem, 1)

            def similarities(b, t, p, first=False):
                if t >= T:
                    b, t = b + 1, t - T
                pair = b * (POS // 2) + (t * HEADS + p) // 2
                if t == 0 and p == 0:
                    pe.wait_ge(fact.sem, fact.at(b, "zT"))
                if not first:
                    pe.wait_ge(keys.sem, keys.at(pair - 1, "rep"))
                mm(S[:, :], z1T[:, cols(t)], keymap[:, p:p + 2, :, :].rearrange("p a b k -> p (a b k)"),
                   start=True, stop=True).then_inc(sims, 1)

            def weigh(b, p, u, first=False):
                unit = b * (POS * UNITS) + p * UNITS + u
                slot, use = (p * UNITS + u) % SLOTS, b * (POS * UNITS // SLOTS) + (p * UNITS + u) // SLOTS
                if u == 0 and not (first and p < 2):
                    pe.wait_ge(pairs_out, b * POS + p - 1)
                pe.wait_ge(diags_made, unit + 1)
                pe.wait_ge(gathered[slot], (use + 1) * (16 * UJ))
                for j in range(UJ):
                    st, en = (u == 0 and j == 0), (u == UNITS - 1 and j == UJ - 1)
                    mm(KV[p % 2][:, 0:P], ring[:, slot, j, 0:D], diag[:, u % 2, j, :], start=st, stop=en,
                       skip_group_check=True)
                    last = mm(KV[p % 2][:, P:2 * P], diag[:, u % 2, j, :], ring[:, slot, j, D:2 * D], start=False,
                              stop=en, skip_group_check=True)
                last.then_inc(slots_free, 1)

            def attend(b, p, part):
                h, ia, ib = ATT_AT[p]
                for i in (ia, ib):
                    bk, n = A[i % 2], (i + 1) * P
                    if part == "q" and i == ia:
                        if ia == 0:
                            if h == 0:
                                pe.wait_ge(x_copied.sem, x_copied.at(b, "X"))
                                pe.wait_ge(kv_copied.sem, kv_copied.at(b, "KV"))
                            else:
                                pe.wait_ge(aact.sem, aact.at(b, ("o", h - 1, 3)))
                            mm(AA[:, :], wq_s[:, h, :], z1Ta[:, :], start=True, stop=True).then_inc(ape.sem, 1)
                        else:
                            pe.wait_ge(aact.sem, aact.at(b, ("o", h, 1)))
                    if part == "s":
                        if i == 0:
                            pe.wait_ge(aact.sem, aact.at(b, ("q", h)))
                        q = qo[:, h, cols(i)]
                        last = mm(bk[:, 0:min(n, 2 * P)], q, KTa[:, h, 0:min(n, 2 * P)], start=True, stop=True)
                        if n > 2 * P:
                            last = mm(bk[:, 2 * P:n], q, KT[:, h, 2 * P:n], start=True, stop=True)
                        last.then_inc(ape.sem, 1)
                    if part == "T":
                        pe.wait_ge(aact.sem, aact.at(b, ("d", h, i)))
                        for j in range(i + 1):
                            last = mm(bk[:, cols(j)], prob[:, i % 2, cols(j)], a_dg[:, i % 2, :], start=True, stop=True)
                        last.then_inc(ape.sem, 1)
                    if part == "v":
                        pe.wait_ge(aact.sem, aact.at(b, ("T", h, i)))
                        for j in range(i + 1):
                            v = Va[:, j, h, :] if j < 2 else V[:, j, h, :]
                            last = mm(bk[:, 0:P], v, probT[:, i % 2, cols(j)], start=(j == 0), stop=(j == i))
                        last.then_inc(ape.sem, 1)

            def lstm(b, k):
                u = LSTM[k]
                p, s, w0, n = u
                xs = hT[:, 0:(N // p) * p].rearrange("q (w p) -> q p w", p=p)[:, s, w0:w0 + n]
                if k == 0:
                    pe.wait_ge(pact.sem, pact.at(b, "g2"))
                else:
                    pe.wait_ge(pdve.sem, pdve.at(b, ("h", LSTM[k - 1])))
                if s == 0 and w0 == 0:
                    pe.wait_ge(lw_in[p % 2], 64 * b + 32 * ((p - 1) // 2 + 1))
                for gate in range(4):
                    to = A[gate // 2][:, (gate % 2) * 256:(gate % 2) * 256 + n]
                    last = mm(to, lw[:, p % 2, 0, cols(gate)], xs, start=True, stop=(s == 0))
                    if s:
                        last = mm(to, lw[:, p % 2, 1, cols(gate)], hid[:, 0:n], start=False, stop=True)
                last.then_inc(ppe.sem, 1)

            def post(b, at):
                if at == POST_AT["wo"]:
                    pe.wait_ge(aact.sem, aact.at(b, ("o", HEADS - 1, 3)))
                    for t in range(T):
                        for h in range(HEADS):
                            last = mm(AA[:, cols(t)], qo[:, h, cols(t)], wo_s[:, h, :], start=(h == 0), stop=(h == HEADS - 1))
                    last.then_inc(ppe.sem, 1)
                if at == POST_AT["Uz"]:
                    pe.wait_ge(pdve.sem, pdve.at(b, "z"))
                    for m in range(T):
                        last = mm(AB[:, :], z2[:, m, :], adj_s[:, m, :], start=(m == 0), stop=(m == T - 1))
                    last.then_inc(ppe.sem, 1)
                if at == POST_AT["g1"]:
                    pe.wait_ge(pact.sem, pact.at(b, "Uz"))
                    for t in range(T):
                        mm(AA[:, cols(t)], u2[:, cols(t)], wg0_s[:, :], start=True, stop=False)
                        last = mm(AA[:, cols(t)], ra_r[:, cols(t)], bg0_r, start=False, stop=True)
                    last.then_inc(ppe.sem, 1)
                if at == POST_AT["Ug"]:
                    pe.wait_ge(pact.sem, pact.at(b, "g1"))
                    for m in range(T):
                        last = mm(AB[:, :], g1_s[:, m, :], adj_s[:, m, :], start=(m == 0), stop=(m == T - 1))
                    last.then_inc(ppe.sem, 1)
                if at == POST_AT["g2"]:
                    pe.wait_ge(pact.sem, pact.at(b, "Ug"))
                    mm(AA[:, :], wg1_s[:, :], u2, start=True, stop=False)
                    mm(AA[:, :], bg1_r, ra_r, start=False, stop=True).then_inc(ppe.sem, 1)
                if at in LSTM_AT:
                    lstm(b, LSTM_AT[at])
                if at == POST_AT["ht"]:
                    pe.wait_ge(pdve.sem, pdve.at(b, ("h", LSTM[-1])))
                    for t in range(T):
                        last = tr(AA[:, cols(t)], hT[:, cols(t)], ident[:, :])
                    last.then_inc(ppe.sem, 1)
                if at == POST_AT["zT"]:
                    pe.wait_ge(pdve.sem, pdve.at(b, "z3"))
                    for t in range(T):
                        last = tr(AB[:, cols(t)], z2[:, t, :], ident[:, :])
                    last.then_inc(ppe.sem, 1)
                for t in range(T):
                    if at == POST_AT[f"lg{t}"]:
                        if t == 0:
                            pe.wait_ge(pact.sem, pact.at(b, "zT"))
                        if t >= 2:
                            pe.wait_ge(pdve.sem, pdve.at(b, ("sb", t - 2)))
                        mm(A[t % 2][:, :], z3T[:, cols(t)], slmap[:, :], start=True, stop=False)
                        mm(A[t % 2][:, :], ones[32:33, :], slb_r, start=False, stop=True).then_inc(ppe.sem, 1)
                if at == POST_AT["Y"]:
                    pe.wait_ge(pdve.sem, pdve.at(b, ("sw", T - 1)))
                    for t in range(T):
                        last = mm(AA[:, :], z2[:, t, :], sw[:, t, :], start=(t == 0), stop=(t == T - 1))
                    last.then_inc(ppe.sem, 1)
                    for t in range(T):
                        last = mm(AB[:, :], ones[:, :], sw[:, t, :], start=(t == 0), stop=(t == T - 1))
                    last.then_inc(ppe.sem, 1)
                if at == POST_AT["st"]:
                    pe.wait_ge(pdve.sem, pdve.at(b, "nn"))
                    for h in range(SH):
                        c = slice(h * G, (h + 1) * G)
                        mm(AA[0:SD, c], wfx_s[:, c], Yn[:, c], start=True, stop=False)
                        last = mm(AA[0:SD, c], bfx_r[:, c], nn_r[:, c], start=False, stop=True)
                    last.then_inc(ppe.sem, 1)
                if at == POST_AT["qk"]:
                    wait_apart(pe, pact.sem, pact.at(b, "st"), passed_pe)
                    mm(AB[0:SD, :], wqs_s[:, :], stT, start=True, stop=True).then_inc(ppe.sem, 1)
                    mm(AA[0:SD, :], wks_s[:, :], stT, start=True, stop=True).then_inc(ppe.sem, 1)
                if at == POST_AT["v"]:
                    wait_apart(pe, pact.sem, pact.at(b, "q"), passed_pe)
                    mm(AB[0:SD, :], wvs_s[:, :], stT, start=True, stop=True).then_inc(ppe.sem, 1)
                if at == POST_AT["sim"]:
                    wait_apart(pe, pact.sem, pact.at(b, "k"), passed_pe)
                    for h in range(SH):
                        c = slice(h * G, (h + 1) * G)
                        last = mm(AA[0:G, c], qs[:, c], ks[:, c], start=True, stop=True)
                    last.then_inc(ppe.sem, 1)
                if at == POST_AT["aT"]:
                    wait_apart(pe, pdve.sem, pdve.at(b, "at"), passed_pe)
                    for h in range(SH):
                        c = slice(h * G, (h + 1) * G)
                        last = tr(AA[0:G, c], sat[:, c], ident[0:G, 0:G])
                    last.then_inc(ppe.sem, 1)
                if at == POST_AT["vw"]:
                    wait_apart(pe, pact.sem, pact.at(b, "v"), passed_pe)
                    for h in range(SH):
                        to = (AB, FC)[h // 4][0:G, cols(h % 4)]
                        last = mm(to, vs[:, h * G:(h + 1) * G], wout_s[:, h, :], start=True, stop=True)
                    last.then_inc(ppe.sem, 1)
                if at == POST_AT["G"]:
                    wait_apart(pe, pact.sem, pact.at(b, "vw1"), passed_pe)
                    for h in range(SH):
                        to = AA[(h % 2) * G:(h % 2) * G + G, cols(h // 2)]
                        last = mm(to, satT[:, h * G:(h + 1) * G], vw[:, h, :], start=True, stop=True)
                    last.then_inc(ppe.sem, 1)
                for t in range(T):
                    if at == POST_AT[f"wT{t}"]:
                        pe.wait_ge(pact.sem, pact.at(b, ("wT", t - 2) if t >= 2 else "G"))
                        for c in range(4):
                            last = tr(A[t % 2][:, cols(c)], sw[:, t, cols(c)], ident[:, :])
                        last.then_inc(ppe.sem, 1)
                if at == POST_AT["o"]:
                    pe.wait_ge(pact.sem, pact.at(b, ("wT", T - 1)))
                    for t in range(T):
                        for c in range(4):
                            mm(FC[:, cols(t)], swT[:, c, cols(t)], gout[:, c, :], start=(c == 0), stop=False)
                        last = mm(FC[:, cols(t)], ones[32:33, :], bout_r, start=False, stop=True)
                    last.then_inc(ppe.sem, 1)

            def step(b, has_front=True, has_post=True, first=False):
                for p in range(POS):
                    for u in range(UNITS):
                        at = p * UNITS + u
                        weigh(b, p, u, first)
                        if has_post and u == 0 and 1 <= p <= 2 * HEADS:
                            attend(b - 1, p - 1, "T")
                        if has_post and u == 1 and 1 <= p <= 2 * HEADS:
                            attend(b - 1, p - 1, "v")
                        if u == 2 and p % 2 and (p + 1 < POS - HEADS or has_front):
                            similarities(b, (p + 1) // HEADS + 1, (p + 1) % HEADS)
                        if has_post and u == 2 and p < 2 * HEADS:
                            attend(b - 1, p, "q")
                        if has_post and u == 3 and p < 2 * HEADS:
                            attend(b - 1, p, "s")
                        if has_front:
                            front(b + 1, at)
                        if has_post:
                            post(b - 1, at)

            setup()
            for at in range(POS * UNITS):
                front(0, at)
            for p in range(0, HEADS, 2):
                similarities(0, 0, p, first=(p == 0))
            similarities(0, 1, 0)
            step(0, has_post=False, first=True)
            with nc.tensor.Fori(1, B - 1) as b:
                step(b)
            step(B - 1, has_front=False)
            for p in range(2 * HEADS):
                for part in "qsTv":
                    attend(B - 1, p, part)
            for at in range(POS * UNITS):
                post(B - 1, at)

        @block.scalar
        def _(act):
            af = nc.scalar.activation

            def setup():
                for k in range(HEADS // 2):
                    act.wait_ge(merged, k + 1)
                    af(keymap[:, 2 * k:2 * k + 2, :, :].rearrange("p a b k -> p (a b k)"), A[k % 2][:, :],
                       ACT.Copy).then_inc(merged_copied, 1)
                act.wait_ge(setup_dve, 1)

            def deviation(mv, sd, wait_on, value, done):
                act.wait_ge(wait_on, value)
                af(sd[:, :], mv[:, :, 1], ACT.Sqrt, bias=eps[:, 0:1]).then_inc(done, 1)

            def evacuate(dst, src, chain, b, step_in, done, func=ACT.Copy):
                act.wait_ge(chain.sem, chain.at(b, step_in))
                af(dst, src, func).then_inc(done.sem, 1)

            def front(b, at, prologue=False):
                if at == FRONT_AT["z"]:
                    deviation(f_mv, f_sd, fdve.sem, fdve.at(b, "mv"), fact.sem)
                if at == FRONT_AT["Az"]:
                    evacuate(up, FA[:, :], fpe, b, "Az", fact)
                if at == FRONT_AT["h1"]:
                    evacuate(h1_s[:, 0:2, :].rearrange("p a b -> p (a b)"), FB[:, :], fpe, b, "h1a", fact, ACT.Relu)
                    evacuate(h1_s[:, 2:4, :].rearrange("p a b -> p (a b)"), FA[:, :], fpe, b, "h1b", fact, ACT.Relu)
                if at == FRONT_AT["Ah0"]:
                    evacuate(ah[:, 0, :], FB[:, :], fpe, b, "Ah0", fact)
                if at == FRONT_AT["Ah1"]:
                    evacuate(ah[:, 1, :], FA[:, :], fpe, b, "Ah1", fact)
                for c in range(4):
                    if at == FRONT_AT[f"h2{c}"]:
                        evacuate(h12[:, c, :], (FB, FA)[c % 2][:, :], fpe, b, f"h2{c}", fact, ACT.Relu)
                if at == FRONT_AT["P"]:
                    evacuate(up, FB[:, :], fpe, b, "P", fact)
                if at == FRONT_AT["z1"]:
                    deviation(f_mv, f_sd, fdve.sem, fdve.at(b, "mv1"), fact.sem)
                if at == FRONT_AT["zT"]:
                    if not prologue:
                        act.wait_ge(sims, b * (POS // 2))
                        act.wait_ge(x_copied.sem, x_copied.at(b - 1, "X"))
                    evacuate(z1T[:, :], FB[:, :], fpe, b, "zT", fact)

            def copy_kv(b):
                act.wait_ge(pairs_out, (b + 1) * POS)
                act.wait_ge(ppe.sem, ppe.at(b - 1, "o"))
                af(KTa[:, :, :], KT[:, :, 0:2 * P], ACT.Copy)
                af(Va[:, :, :, :].rearrange("p a h d -> p (a h d)"),
                   V[:, 0:2, :, :].rearrange("p a h d -> p (a h d)"), ACT.Copy).then_inc(kv_copied.sem, 1)

            def copy_x(b, first=False):
                act.wait_ge(fact.sem, fact.at(b, "zT"))
                act.wait_ge(fdve.sem, fdve.at(b, "x1"))
                if not first:
                    act.wait_ge(pdve.sem, pdve.at(b - 1, "x2"))
                af(x1a[:, :, :], x1[:, :, :], ACT.Copy)
                af(z1Ta[:, :], z1T[:, :], ACT.Copy).then_inc(x_copied.sem, 1)

            def weights(b, t, h):
                pair = b * (POS // 2) + (t * HEADS + h) // 2
                act.wait_ge(keys.sem, keys.at(pair, "neg"))
                for k in range(2):
                    last = af(wts[:, t % 2, h + k, :], fs[:, k, :], ACT.Exp, bias=neg[:, k, :],
                              accum_out=wsum[:, t % 2, h + k:h + k + 1])
                last.then_inc(wexp, 1)

            def diagonals(b, p, u, first=False):
                t, h = p // HEADS, p % HEADS
                if u == 0:
                    act.wait_ge(wnorm, b * (POS // 2) + p // 2 + 1)
                if not (first and p == 0 and u < 2):
                    act.wait_ge(slots_free, b * (POS * UNITS) + p * UNITS + u - 1 + SLOTS)
                for j in range(UJ):
                    k = u * UJ + j
                    last = af(diag[:, u % 2, j, :], ident[:, :], ACT.Copy, scale=wts[:, t % 2, h, k:k + 1])
                last.then_inc(diags_made, 1)

            def attend(b, p, part):
                h, ia, ib = ATT_AT[p]
                if part == "q" and ia == 0:
                    evacuate(qo[:, h, :], AA[:, :], ape, b, ("q", h), aact)
                for i in (ia, ib):
                    k, bk, n = i % 2, A[i % 2], (i + 1) * P
                    if part == "e":
                        act.wait_ge(adve.sem, adve.at(b, ("n", h, i)))
                        af(prob[:, k, 0:n], bk[:, 0:n], ACT.Exp, bias=a_mx[:, k, 1:2], scale=ATT_SCALE,
                           accum_out=a_sm[:, k, 0:1]).then_inc(aact.sem, 1)
                    if part == "d":
                        act.wait_ge(adve.sem, adve.at(b, ("r", h, i)))
                        af(a_dg[:, k, :], ident[:, :], ACT.Copy, scale=a_sm[:, k, 1:2]).then_inc(aact.sem, 1)
                    if part == "T":
                        evacuate(probT[:, k, 0:n], bk[:, 0:n], ape, b, ("T", h, i), aact)
                    if part == "o":
                        evacuate(qo[:, h, cols(i)], bk[:, 0:P], ape, b, ("v", h, i), aact)

            def lstm(b, k):
                u = LSTM[k]
                p, s, w0, n = u
                act.wait_ge(ppe.sem, ppe.at(b, ("gates", u)))
                for gate in range(4):
                    last = af(gates[:, gate, 0:n], A[gate // 2][:, (gate % 2) * 256:(gate % 2) * 256 + n],
                              ACT.Tanh if gate == 2 else ACT.Sigmoid, bias=lbias[:, p - 1, gate:gate + 1])
                last.then_inc(pact.sem, 1)
                act.wait_ge(pdve.sem, pdve.at(b, ("c" if s else "ig", u)))
                af(ctan[:, 0:n], cell[:, 0:n], ACT.Tanh).then_inc(pact.sem, 1)

            def post(b, at):
                if at == POST_AT["z"]:
                    deviation(p_mv, p_sd, pdve.sem, pdve.at(b, "mv"), pact.sem)
                if at == POST_AT["Uz"]:
                    evacuate(u2, AB[:, :], ppe, b, "Uz", pact)
                if at == POST_AT["g1"]:
                    evacuate(g1_s.rearrange("p t d -> p (t d)"), AA[:, :], ppe, b, "g1", pact, ACT.Relu)
                if at == POST_AT["Ug"]:
                    evacuate(u2, AB[:, :], ppe, b, "Ug", pact)
                if at == POST_AT["g2"]:
                    evacuate(hT, AA[:, :], ppe, b, "g2", pact, ACT.Relu)
                if at in LSTM_AT:
                    lstm(b, LSTM_AT[at])
                if at == POST_AT["z3"]:
                    deviation(p_mv, p_sd, pdve.sem, pdve.at(b, "mv3"), pact.sem)
                if at == POST_AT["zT"]:
                    evacuate(z3T, AB[:, :], ppe, b, "zT", pact)
                for t in range(T):
                    if at == POST_AT[f"lg{t}"]:
                        act.wait_ge(pdve.sem, pdve.at(b, ("sb", t)))
                        af(sw[:, t, :], lg, ACT.Exp).then_inc(pact.sem, 1)
                if at == POST_AT["st"]:
                    evacuate(stT, AA[0:SD, :], ppe, b, "st", pact)
                if at == POST_AT["qk"]:
                    evacuate(qs, AB[0:SD, :], ppe, b, "q", pact)
                    evacuate(ks, AA[0:SD, :], ppe, b, "k", pact)
                if at == POST_AT["v"]:
                    evacuate(vs, AB[0:SD, :], ppe, b, "v", pact)
                if at == POST_AT["sim"]:
                    act.wait_ge(pdve.sem, pdve.at(b, "asb"))
                    af(sat, sat, ACT.Exp, scale=SLICE_SCALE).then_inc(pact.sem, 1)
                if at == POST_AT["aT"]:
                    evacuate(satT, AA[0:G, :], ppe, b, "aT", pact)
                if at == POST_AT["vw"]:
                    evacuate(vw[:, 0:4, :].rearrange("p h d -> p (h d)"), AB[0:G, :], ppe, b, "vw", pact)
                    evacuate(vw[:, 4:8, :].rearrange("p h d -> p (h d)"), FC[0:G, :], ppe, b, "vw", pact)
                if at == POST_AT["G"]:
                    evacuate(gout.rearrange("p c d -> p (c d)"), AA[:, :], ppe, b, "G", pact)
                for t in range(T):
                    if at == POST_AT[f"wT{t}"]:
                        evacuate(swT[:, :, cols(t)], A[t % 2][:, :].rearrange("p (c n) -> p c n", c=4), ppe, b,
                                 ("wT", t), pact)

            def step(b, has_front=True, has_post=True, first=False, last=False):
                for p in range(POS):
                    if has_post and 1 <= p <= 2 * HEADS:
                        attend(b - 1, p - 1, "d")
                    for u in range(UNITS):
                        at = p * UNITS + u
                        if at + 1 < POS * UNITS:
                            diagonals(b, (at + 1) // UNITS, (at + 1) % UNITS, first)
                        elif not last:
                            diagonals(b + 1, 0, 0)
                        if has_post and at == 0:
                            copy_kv(b - 1)
                        if has_post and u == 0 and 1 <= p <= 2 * HEADS:
                            attend(b - 1, p - 1, "T")
                        if has_post and u == 1 and 1 <= p <= 2 * HEADS:
                            attend(b - 1, p - 1, "o")
                        if u == 1 and p % 2 and (p < POS - HEADS or has_front):
                            weights(b + 1 if p >= POS - HEADS else b, (p // HEADS + 1) % T, p % HEADS - 1)
                        if has_post and u == 2 and p < 2 * HEADS:
                            attend(b - 1, p, "q")
                        if has_post and u == 3 and p < 2 * HEADS:
                            attend(b - 1, p, "e")
                        if has_front:
                            front(b + 1, at)
                        if has_post:
                            post(b - 1, at)
                        if at == COPY_X_AT:
                            copy_x(b, first=first)

            setup()
            for at in range(POS * UNITS):
                front(0, at, prologue=True)
            for p in range(0, HEADS, 2):
                weights(0, 0, p)
            diagonals(0, 0, 0, first=True)
            step(0, has_post=False, first=True)
            with nc.scalar.Fori(1, B - 1) as b:
                step(b)
            step(B - 1, has_front=False, last=True)
            copy_kv(B - 1)
            for p in range(2 * HEADS):
                for part in "qedTo":
                    attend(B - 1, p, part)
            for at in range(POS * UNITS):
                post(B - 1, at)

        @block.vector
        def _(dve):
            tt, ts, tc, red = nc.vector.tensor_tensor, nc.vector.tensor_scalar, nc.vector.tensor_copy, nc.vector.tensor_reduce

            def wide(ap, axis, n):
                ap = ap.unsqueeze(axis)
                shape = list(ap.shape)
                shape[axis] = n
                return ap.to_broadcast(shape)

            def setup():
                nc.vector.memset(eps[:, :], EPS).then_inc(setup_dve, 1)
                dve.wait_ge(consts_in, LOADED)
                tt(adj2_s[:, :, :], adj_s[:, :, :], adj_s[:, :, :], ALU.mult).then_inc(setup_dve, 1)
                ts(tinv[:, :], temp_s[:, :], 0.1, 5.0, ALU.max, ALU.min).then_inc(setup_dve, 1)
                dve.wait_ge(setup_dve, 3)
                nc.vector.reciprocal(tinv[:, :], tinv[:, :]).then_inc(setup_dve, 1)
                dve.wait_ge(setup_dve, 4)
                dve.wait_ge(merged, HEADS // 2 + 1)
                tt(slmap[:, :].rearrange("p (h g) -> p h g", h=SH), FA[:, :].rearrange("p (h g) -> p h g", h=SH),
                   wide(tinv[:, :], 2, G), ALU.mult).then_inc(setup_dve, 1)
                dve.wait_ge(merged, HEADS // 2 + 2)
                tt(slb_r, FB[32:33, :], bsl_u, ALU.add).then_inc(setup_dve, 1)
                dve.wait_ge(setup_dve, 6)
                b3 = slb_r.rearrange("p (h g) -> p h g", h=SH)
                tt(b3, b3, wide(tinv[32:33, :], 2, G), ALU.mult).then_inc(setup_dve, 1)
                dve.wait_ge(merged, MERGED)
                tc(ra_r, FC[64:65, :]).then_inc(setup_dve, 1)
                tt(lbias[:, :, :], lbias[:, :, :], lbias2[:, :, :], ALU.add).then_inc(setup_dve, 1)

            def statistics(src, st, mv, chain, b, names):
                for t in range(T):
                    last = nc.vector.bn_stats(st[:, t, :], src[:, t, :])
                last.then_inc(chain.sem, 1)
                wait_apart(dve, chain.sem, chain.at(b, names[0]), passed_dve)
                for t in range(T):
                    last = nc.vector.bn_aggr(mv[:, t, :], st[:, t, :])
                last.then_inc(chain.sem, 1)

            def normalise(dst, src, mv, sd, rs, chain, b, names):
                nc.vector.reciprocal(rs[:, :], sd[:, :]).then_inc(chain.sem, 1)
                dve.wait_ge(chain.sem, chain.at(b, names[2]))
                for t in range(T):
                    last = ts(dst[:, t, :], src[:, t, :], mv[:, t, 0:1], rs[:, t:t + 1], ALU.subtract, ALU.mult)
                last.then_inc(chain.sem, 1)

            def front(b, at, first=False):
                if at == FRONT_AT["stats"]:
                    dve.wait_ge(x_in, 16 * (b + 1))
                    statistics(x_s, f_st, f_mv, fdve, b, ("st", "mv"))
                if at == FRONT_AT["z"]:
                    dve.wait_ge(fact.sem, fact.at(b, "sd"))
                    if not first:
                        dve.wait_ge(fpe.sem, fpe.at(b - 1, "zT"))
                    normalise(z, x_s, f_mv, f_sd, f_rs, fdve, b, ("st", "mv", "rs"))
                if at == FRONT_AT["y"]:
                    dve.wait_ge(fpe.sem, fpe.at(b, "y"))
                    if not first:
                        dve.wait_ge(x_copied.sem, x_copied.at(b - 1, "X"))
                    tt(x1[:, :, :], x_s[:, :, :], FA[:, :].rearrange("p (t d) -> p t d", t=T), ALU.add)\
                        .then_inc(fdve.sem, 1)
                    dve.wait_ge(fdve.sem, fdve.at(b, "x1"))
                    statistics(x1, f_st, f_mv, fdve, b, ("st1", "mv1"))
                if at == FRONT_AT["z1"]:
                    dve.wait_ge(fact.sem, fact.at(b, "sd1"))
                    normalise(z, x1, f_mv, f_sd, f_rs, fdve, b, ("st1", "mv1", "rs1"))

            def top_keys(b, t, h, first=False):
                for stage in TOP_AT.values():
                    top_stage(stage, b, t, h, first)

            def top_stage(stage, b, t, h, first=False):
                if stage == "best 8 keys":
                    best_8_keys(b, t, h)
                elif stage == "next 8 keys":
                    next_8_keys(b, t, h)
                elif stage == "pairs":
                    pairs(b, t, h, first)
                else:
                    rows_of(b, t, h, int(stage == "rows 1"))

            def best_8_keys(b, t, h):
                pair = b * (POS // 2) + (t * HEADS + h) // 2
                K = keys

                def after(step):
                    wait_apart(dve, K.sem, K.at(pair, step), passed_dve)

                wait_apart(dve, sims, pair + 1, passed_dve)
                sims_s = S[:, :].rearrange("p (h q k) -> p h q k", h=2, q=2)
                four = [(k, q) for k in range(2) for q in range(2)]
                for k, q in four:
                    last = nc.vector.max(tv[:, k, q, 0:8], sims_s[:, k, q, :])
                last.then_inc(K.sem, 1)
                after("max")
                for k, q in four:
                    last = nc.vector.max_index(ti[:, k, q, 0:8], tv[:, k, q, 0:8], sims_s[:, k, q, :])
                last.then_inc(K.sem, 1)
                for k, q in four:
                    last = nc.vector.match_replace(rep[:, k, q, :], tv[:, k, q, 0:8], sims_s[:, k, q, :], TAKEN)
                last.then_inc(K.sem, 1)

            def next_8_keys(b, t, h):
                pair = b * (POS // 2) + (t * HEADS + h) // 2
                K = keys
                four = [(k, q) for k in range(2) for q in range(2)]

                def after(step):
                    wait_apart(dve, K.sem, K.at(pair, step), passed_dve)

                after("rep")
                for k, q in four:
                    last = nc.vector.max(tv[:, k, q, 8:16], rep[:, k, q, :])
                last.then_inc(K.sem, 1)
                after("max2")
                for k, q in four:
                    last = nc.vector.max_index(ti[:, k, q, 8:16], tv[:, k, q, 8:16], rep[:, k, q, :])
                last.then_inc(K.sem, 1)
                after("idx2")
                for k in range(2):
                    ts(tf[:, k, 0, :], ti[:, k, 0, :], float((h + k) * NKV), None, ALU.add)
                last = ts(tf[:, :, 1, :], ti[:, :, 1, :], float(NKEYS), None, ALU.mult)
                last.then_inc(K.sem, 1)

            def pairs(b, t, h, first=False):
                pair = b * (POS // 2) + (t * HEADS + h) // 2
                K = keys

                def after(step):
                    wait_apart(dve, K.sem, K.at(pair, step), passed_dve)

                after("f")
                for to, of in ((cs, tv), (ci, tf)):
                    for i, ni, nj, at in ROWS:
                        last = tt(to[:, :, at:at + ni * nj].rearrange("p h (i j) -> p h i j", i=ni),
                                  wide(of[:, :, 0, i:i + ni], 3, nj), wide(of[:, :, 1, 0:nj], 2, ni), ALU.add)
                last.then_inc(K.sem, 1)
                after("cand")
                if not first:
                    wait_apart(dve, wexp, pair, passed_dve)
                for k in range(2):
                    last = nc.vector.max(fs[:, k, 0:8], cs[:, k, :])
                last.then_inc(K.sem, 1)
                after("cmax")
                for k in range(2):
                    last = nc.vector.max_index(fp[:, k, 0:8], fs[:, k, 0:8], cs[:, k, :])
                last.then_inc(K.sem, 1)
                for k in range(2):
                    last = nc.vector.match_replace(crep[:, k, :], fs[:, k, 0:8], cs[:, k, :], TAKEN)
                last.then_inc(K.sem, 1)
                after("crep")
                for k in range(2):
                    last = nc.vector.max(fs[:, k, 8:16], crep[:, k, :])
                last.then_inc(K.sem, 1)
                after("cmax2")
                for k in range(2):
                    last = nc.vector.max_index(fp[:, k, 8:16], fs[:, k, 8:16], crep[:, k, :])
                last.then_inc(K.sem, 1)
                ts(neg[:, :, :], fs[:, :, 0:1], -1.0, None, ALU.mult).then_inc(K.sem, 1)
                after("cpos2")
                tc(fpf[:, :, :], fp[:, :, :]).then_inc(K.sem, 1)

            def rows_of(b, t, h, k):
                pair = b * (POS // 2) + (t * HEADS + h) // 2
                K = keys

                def after(step):
                    wait_apart(dve, K.sem, K.at(pair, step), passed_dve)

                after("row0" if k else "posf")
                tt(eq, wide(iota[:, :], 1, TOPK), wide(fpf[:, k, :], 2, NC), ALU.is_equal).then_inc(K.sem, 1)
                after(f"eq{k}")
                tt(eq, eq, wide(ci[:, k, :], 1, TOPK), ALU.mult).then_inc(K.sem, 1)
                after(f"sel{k}")
                with nc.allow_low_precision("one row number below 2^17 and zeros are summed, exact in float32"):
                    red(idx[:, t % 2, h + k, :], eq, AX, ALU.add).then_inc(K.sem, 1)

            def normalise_weights(b, t, h):
                pair = b * (POS // 2) + (t * HEADS + h) // 2
                dve.wait_ge(wexp, pair + 1)
                nc.vector.reciprocal(winv[:, t % 2, h:h + 2], wsum[:, t % 2, h:h + 2]).then_inc(winverted, 1)
                dve.wait_ge(winverted, pair + 1)
                w = wts[:, t % 2, h:h + 2, :]
                tt(w, w, wide(winv[:, t % 2, h:h + 2], 2, TOPK), ALU.mult).then_inc(wnorm, 1)

            def collect(b, p):
                t, h = p // HEADS, p % HEADS
                dve.wait_ge(slots_free, b * (POS * UNITS) + (p + 1) * UNITS + SLOTS)
                tc(KT[:, h, cols(t)], KV[p % 2][:, 0:P])
                tc(V[:, t, h, :], KV[p % 2][:, P:2 * P]).then_inc(pairs_out, 1)

            def attend(b, p, part):
                h, ia, ib = ATT_AT[p]
                for i in (ia, ib):
                    k, n = i % 2, (i + 1) * P
                    if part == "m":
                        dve.wait_ge(ape.sem, ape.at(b, ("s", h, i)))
                        d = A[k][:, cols(i)]
                        tt(d, d, mask[:, :], ALU.add).then_inc(adve.sem, 1)
                        dve.wait_ge(adve.sem, adve.at(b, ("m", h, i)))
                        nc.vector.reduce_max(a_mx[:, k, 0:1], A[k][:, 0:n], AX).then_inc(adve.sem, 1)
                        dve.wait_ge(adve.sem, adve.at(b, ("x", h, i)))
                        ts(a_mx[:, k, 1:2], a_mx[:, k, 0:1], -ATT_SCALE, None, ALU.mult).then_inc(adve.sem, 1)
                    if part == "r":
                        dve.wait_ge(aact.sem, aact.at(b, ("e", h, i)))
                        nc.vector.reciprocal(a_sm[:, k, 1:2], a_sm[:, k, 0:1]).then_inc(adve.sem, 1)

            def lstm(b, k):
                u = LSTM[k]
                p, s, w0, n = u
                gi, gf, gg, go = (gates[:, k, 0:n] for k in range(4))
                dve.wait_ge(pact.sem, pact.at(b, ("gates", u)))
                c, product = cell[:, 0:n], ig[:, 0:n]
                if s:
                    tt(c, c, gf, ALU.mult).then_inc(pdve.sem, 1)
                    tt(product, gi, gg, ALU.mult).then_inc(pdve.sem, 1)
                    dve.wait_ge(pdve.sem, pdve.at(b, ("ig", u)))
                    tt(c, c, product, ALU.add).then_inc(pdve.sem, 1)
                else:
                    tt(c, gi, gg, ALU.mult).then_inc(pdve.sem, 1)
                dve.wait_ge(pact.sem, pact.at(b, ("tc", u)))
                if s == p - 1:
                    to = hT[:, 0:(N // p) * p].rearrange("q (w p) -> q p w", p=p)[:, s, w0:w0 + n]
                else:
                    to = hid[:, 0:n]
                tt(to, go, ctan[:, 0:n], ALU.mult).then_inc(pdve.sem, 1)

            def post(b, at):
                if at == POST_AT["wo"]:
                    dve.wait_ge(ppe.sem, ppe.at(b, "wo"))
                    dve.wait_ge(stored, 16 * (b + 1))
                    tt(x2[:, :, :], x1a[:, :, :], AA[:, :].rearrange("p (t d) -> p t d", t=T), ALU.add)\
                        .then_inc(pdve.sem, 1)
                    dve.wait_ge(pdve.sem, pdve.at(b, "x2"))
                    statistics(x2, p_st, p_mv, pdve, b, ("st", "mv"))
                if at == POST_AT["z"]:
                    dve.wait_ge(pact.sem, pact.at(b, "sd"))
                    normalise(z2, x2, p_mv, p_sd, p_rs, pdve, b, ("st", "mv", "rs"))
                if at in LSTM_AT:
                    lstm(b, LSTM_AT[at])
                if at == POST_AT["ht"]:
                    dve.wait_ge(ppe.sem, ppe.at(b, "ht"))
                    tt(x2[:, :, :], x2[:, :, :], AA[:, :].rearrange("p (t d) -> p t d", t=T), ALU.add)\
                        .then_inc(pdve.sem, 1)
                    dve.wait_ge(pdve.sem, pdve.at(b, "x3"))
                    statistics(x2, p_st, p_mv, pdve, b, ("st3", "mv3"))
                if at == POST_AT["z3"]:
                    dve.wait_ge(pact.sem, pact.at(b, "sd3"))
                    normalise(z2, x2, p_mv, p_sd, p_rs, pdve, b, ("st3", "mv3", "rs3"))
                for t in range(T):
                    if at == POST_AT[f"lg{t}"]:
                        logits = A[t % 2][:, :].rearrange("p (h g) -> p h g", h=SH)
                        w = sw[:, t, :].rearrange("p (h g) -> p h g", h=SH)
                        dve.wait_ge(ppe.sem, ppe.at(b, ("lg", t)))
                        nc.vector.reduce_max(s_mx[:, :], logits, AX).then_inc(pdve.sem, 1)
                        dve.wait_ge(pdve.sem, pdve.at(b, ("mx", t)))
                        if t:
                            dve.wait_ge(pact.sem, pact.at(b, ("ex", t - 1)))
                        tt(lg.rearrange("p (h g) -> p h g", h=SH), logits, wide(s_mx[:, :], 2, G), ALU.subtract)\
                            .then_inc(pdve.sem, 1)
                        dve.wait_ge(pact.sem, pact.at(b, ("ex", t)))
                        red(s_sm[:, 0, :], w, AX, ALU.add).then_inc(pdve.sem, 1)
                        dve.wait_ge(pdve.sem, pdve.at(b, ("sm", t)))
                        nc.vector.reciprocal(s_sm[:, 1, :], s_sm[:, 0, :]).then_inc(pdve.sem, 1)
                        dve.wait_ge(pdve.sem, pdve.at(b, ("rc", t)))
                        tt(w, w, wide(s_sm[:, 1, :], 2, G), ALU.mult).then_inc(pdve.sem, 1)
                if at == POST_AT["Y"]:
                    dve.wait_ge(ppe.sem, ppe.at(b, "nr"))
                    ts(rn, AB[:, :], EPS, None, ALU.add).then_inc(pdve.sem, 1)
                    dve.wait_ge(pdve.sem, pdve.at(b, "n1"))
                    nc.vector.reciprocal(rn, rn).then_inc(pdve.sem, 1)
                    dve.wait_ge(pdve.sem, pdve.at(b, "n2"))
                    tt(Yn, AA[:, :], rn, ALU.mult).then_inc(pdve.sem, 1)
                    tt(nn_r, AB[0:1, :], rn[0:1, :], ALU.mult).then_inc(pdve.sem, 1)
                if at == POST_AT["sim"]:
                    dve.wait_ge(ppe.sem, ppe.at(b, "sim"))
                    scores = AA[0:G, :].rearrange("p (h g) -> p h g", h=SH)
                    w = sat.rearrange("p (h g) -> p h g", h=SH)
                    nc.vector.reduce_max(s_mx[0:G, :], scores, AX).then_inc(pdve.sem, 1)
                    dve.wait_ge(pdve.sem, pdve.at(b, "amx"))
                    tt(w, scores, wide(s_mx[0:G, :], 2, G), ALU.subtract).then_inc(pdve.sem, 1)
                    dve.wait_ge(pact.sem, pact.at(b, "aex"))
                    red(s_sm[0:G, 0, :], w, AX, ALU.add).then_inc(pdve.sem, 1)
                    dve.wait_ge(pdve.sem, pdve.at(b, "asm"))
                    nc.vector.reciprocal(s_sm[0:G, 1, :], s_sm[0:G, 0, :]).then_inc(pdve.sem, 1)
                    dve.wait_ge(pdve.sem, pdve.at(b, "arc"))
                    tt(w, w, wide(s_sm[0:G, 1, :], 2, G), ALU.mult).then_inc(pdve.sem, 1)
                if at == POST_AT["o"]:
                    dve.wait_ge(ppe.sem, ppe.at(b, "o"))
                    tt(x2[:, :, :], x2[:, :, :], FC[:, :].rearrange("p (t d) -> p t d", t=T), ALU.add)\
                        .then_inc(pdve.sem, 1)

            def step(b, has_front=True, has_post=True, first=False):
                for p in range(POS):
                    for u in range(UNITS):
                        at = p * UNITS + u
                        if has_post and u == 0 and 1 <= p <= 2 * HEADS:
                            attend(b - 1, p - 1, "r")
                        if at % (2 * UNITS) in TOP_AT and (p < POS - HEADS or has_front):
                            top_stage(TOP_AT[at % (2 * UNITS)], b + 1 if p >= POS - HEADS else b,
                                      (p // HEADS + 1) % T, p % HEADS // 2 * 2)
                        if u == 1 and p % 2 == 0 and (p <= POS - HEADS or has_front) and not (first and p == 0):
                            before = p + HEADS - 2
                            normalise_weights(b + before // POS, before % POS // HEADS, before % HEADS)
                        if u == UNITS - 1:
                            collect(b, p)
                            if has_post and p < 2 * HEADS:
                                attend(b - 1, p, "m")
                        if has_front:
                            front(b + 1, at)
                        if has_post:
                            post(b - 1, at)

            setup()
            for at in range(POS * UNITS):
                front(0, at, first=True)
            for p in range(0, HEADS, 2):
                top_keys(0, 0, p, first=(p == 0))
                normalise_weights(0, 0, p)
            step(0, has_post=False, first=True)
            with nc.vector.Fori(1, B - 1) as b:
                step(b)
            step(B - 1, has_front=False)
            for p in range(2 * HEADS):
                attend(B - 1, p, "m")
                attend(B - 1, p, "r")
            for at in range(POS * UNITS):
                post(B - 1, at)


def kernel(**a):
    import numpy as np
    import concourse.bacc as bacc
    from concourse.bass_utils import run_bass_kernel_spmd

    f = np.float32
    a = {k: np.asarray(v) for k, v in a.items()}
    eye = np.eye(P, dtype=f)
    arrays = {
        "x": a["x"], "adjT": a["adj"].T, "w1": a["L0_gnn_W1"], "w2": a["L0_gnn_W2"], "w3": a["L0_gnn_W3"],
        "wqpkT": a["L0_ffn_Wq_pk"].reshape(D, 2 * HEADS, DK).transpose(2, 1, 0),
        "keysT": a["L0_ffn_pk_keys"].transpose(3, 0, 2, 1).reshape(DK, 2 * HEADS, NKEYS),
        "wq": a["L0_ffn_Wq"],
        "table": np.concatenate([a["L0_ffn_keys_table"], a["L0_ffn_values_table"]], axis=1),
        "wo": a["L0_ffn_Wo"], "wg0": a["L1_gnn_Wg0"], "wg1": a["L1_gnn_Wg1"],
        "bg0": a["L1_gnn_bg0"].reshape(1, D), "bg1": a["L1_gnn_bg1"].reshape(1, D),
        "wihT": a["L1_gnn_Wih"].transpose(2, 0, 1), "whhT": a["L1_gnn_Whh"].transpose(2, 0, 1),
        "bih": a["L1_gnn_bih"].reshape(SKIPS, 4, D).transpose(2, 0, 1),
        "bhh": a["L1_gnn_bhh"].reshape(SKIPS, 4, D).transpose(2, 0, 1),
        "wfx": a["L1_ffn_W_fx"], "bfx": a["L1_ffn_b_fx"].reshape(1, SH * SD),
        "wxT": a["L1_ffn_W_x"].reshape(D, SH, SD).transpose(2, 1, 0), "bx": a["L1_ffn_b_x"].reshape(SH, SD).T,
        "wsl": a["L1_ffn_W_slice"], "bsl": np.tile(a["L1_ffn_b_slice"].reshape(1, G), (1, SH)),
        "temp": np.tile(a["L1_ffn_temperature"].reshape(1, SH), (P, 1)),
        "wqs": a["L1_ffn_W_q"], "wks": a["L1_ffn_W_k"], "wvs": a["L1_ffn_W_v"], "wout": a["L1_ffn_W_out"],
        "bout": a["L1_ffn_b_out"].reshape(1, D),
        "c_ident": eye, "c_mask": np.triu(np.full((P, P), MASKED, f), 1),
        "c_iota": np.tile(np.arange(NC, dtype=f), (P, 1)), "c_ones": np.ones((P, P), f),
    }
    order = ["x", "adjT", "w1", "w2", "w3", "wqpkT", "keysT", "wq", "table", "wo", "wg0", "wg1", "bg0", "bg1",
             "wihT", "whhT", "bih", "bhh", "wfx", "bfx", "wxT", "bx", "wsl", "bsl", "temp", "wqs", "wks", "wvs",
             "wout", "bout", "c_ident", "c_mask", "c_iota", "c_ones"]
    nc = bacc.Bacc("TRN2", target_bir_lowering=False, num_devices=1)
    feed, args = {}, []
    for name in order:
        v = np.ascontiguousarray(arrays[name])
        feed[f"in_{name}"] = v
        args.append(nc.dram_tensor(f"in_{name}", v.shape, mybir.dt.from_np(v.dtype), kind="ExternalInput").ap())
    result = nc.dram_tensor("result", (B, N, D), F32, kind="ExternalOutput").ap()
    build(nc, *args, result)
    r = run_bass_kernel_spmd(nc, [feed], core_ids=[0])
    return r.results[0]["result"]
```

```python
from contextlib import ExitStack

import concourse.bass as bass
from concourse import mybir

F32 = mybir.dt.float32
U32 = mybir.dt.uint32
ALU = mybir.AluOpType
ACT = mybir.ActivationFunctionType
AX = mybir.AxisListType.X

P = 128
B, N, D = 16, 512, 128
T = N // P
H1, H2 = 256, 512
HEADS, DK, NKEYS, TOPK = 8, 64, 128, 16
NKV = NKEYS * NKEYS
SKIPS = 4
SH, SD, G = 8, 64, 64
POS = T * HEADS
UJ = 4
UNITS = TOPK // UJ
SLOTS = 8
EPS = 1e-5
MASKED = -1.0e30
TAKEN = -3.0e38
ATT_SCALE = float(D) ** -0.5
SLICE_SCALE = float(SD) ** -0.5

ROWS = []
_at = 0
for _i, _k, _n in ((0, 1, 16), (1, 1, 8), (2, 1, 5), (3, 1, 4), (4, 1, 3), (5, 3, 2), (8, 8, 1)):
    ROWS.append((_i, _k, _n, _at))
    _at += _k * _n
NC = _at

LSTM = [(1, 0, 0, 256), (1, 0, 256, 256)] + [(p, s, 0, N // p) for p in range(2, SKIPS + 1) for s in range(p)]

FRONT_AT = {"stats": 0, "z": 1, "Az": 3, "h1": 5, "Ah0": 8, "Ah1": 10, "h20": 13, "h21": 15, "h22": 17, "h23": 19,
            "P": 22, "y": 75, "z1": 77, "zT": 90}
POST_AT = {"wo": 67, "z": 68, "Uz": 69, "g1": 70, "Ug": 71, "g2": 72, "ht": 96, "z3": 97, "zT": 98, "lg0": 99,
           "lg1": 100, "lg2": 101, "lg3": 102, "Y": 104, "st": 106, "qk": 107, "v": 108, "sim": 109, "aT": 111,
           "vw": 112, "G": 113, "wT0": 114, "wT1": 115, "wT2": 116, "wT3": 117, "o": 119}
LSTM_AT = {74 + 2 * k: k for k in range(len(LSTM))}
TOP_AT = {0: "best 8 keys", 2: "next 8 keys", 4: "pairs", 6: "rows 0", 7: "rows 1"}
COPY_X_AT = 70
FIRST_WEIGHTS = {1: 2, 3: 4, 4: 6}


def front_unit(at, first):
    return at - 2 * UNITS if first and at < POS * UNITS // 2 else at


LAST_OF = {u[0]: u for u in LSTM}

JOBS = 2 * HEADS
ATT_AT = [(n % HEADS, 2 * (n // HEADS), 2 * (n // HEADS) + 1) for n in range(JOBS)]
OWN_STEP = {2 * HEADS + 1 + 2 * n: n for n in range(HEADS)}
LAST_IN_STEP = [(n, stage) for n in range(HEADS - 1) for stage in range(3)] + [(HEADS - 1, 0)]
LAST_AFTER = [(n - stage, stage) for n in range(HEADS, JOBS + 2) for stage in (2, 1, 0)
              if HEADS - 1 <= n - stage < JOBS and (n - stage, stage) != (HEADS - 1, 0)]


class Signal:

    def __init__(self, sem, steps, start=0):
        self.sem, self.n, self.start = sem, len(steps), start
        self.index = {s: k for k, s in enumerate(steps)}
        assert len(self.index) == self.n

    def at(self, b, step):
        return b * self.n + self.index[step] + 1 + self.start


def wait_apart(engine, sem, value, passed):
    engine.wait_ge(sem, value)
    engine.sem_inc(passed, 1)


FRONT_PE = ["Az", "h1a", "h1b", "Ah0", "Ah1"] + [f"h2{c}" for c in range(4)] + ["P", "y", "zT"]
FRONT_ACT = ["sd", "Az", "h1a", "h1b", "Ah0", "Ah1"] + [f"h2{c}" for c in range(4)] + ["P", "sd1", "zT"]
FRONT_DVE = ["st", "mv", "rs", "z", "x1", "st1", "mv1", "rs1", "z1"]


def att_steps(stages):
    pe, act, dve = [], [], []
    for n, stage in stages:
        h, a, b = ATT_AT[n]
        two = (a, b)
        if stage == 0:
            pe += [("q", h)] * (a == 0) + [("s", h, i) for i in two]
            act += [("q", h)] * (a == 0) + [("e", h, i) for i in two]
            dve += [(k, h, i) for i in two for k in "mxn"]
        if stage == 1:
            pe += [("T", h, i) for i in two]
            act += [(k, h, i) for k in "dT" for i in two]
            dve += [("r", h, i) for i in two]
        if stage == 2:
            pe += [("v", h, i) for i in two]
            act += [("o", h, i) for i in two]
    return pe, act, dve


ATT_PE, ATT_ACT, ATT_DVE = att_steps([(n, stage) for n in range(JOBS) for stage in range(3)])
LAST_PE, LAST_ACT, LAST_DVE = att_steps(LAST_IN_STEP + LAST_AFTER)
POST_PE = (["wo", "Uz", "g1", "Ug", "g2"] + [("gates", u) for u in LSTM] + ["ht", "zT"]
           + [("lg", t) for t in range(T)] + ["Y", "nr", "st", "q", "k", "v", "sim", "aT", "vw", "G"]
           + [("wT", t) for t in range(T)] + ["o"])
POST_ACT = (["sd", "Uz", "g1", "Ug", "g2"] + [(k, u) for u in LSTM for k in ("gates", "tc")] + ["sd3", "zT"]
            + [("ex", t) for t in range(T)] + ["st", "q", "k", "v", "aex", "aT", "vw0", "vw1", "G"]
            + [("wT", t) for t in range(T)])
POST_DVE = (["x2", "st", "mv", "rs", "z"]
            + [(k, u) for u in LSTM for k in ((("fc",) if u[1] else ()) + ("ig",) + (("c",) if u[1] else ()) + ("h",))]
            + ["x3", "st3", "mv3", "rs3", "z3"] + [(k, t) for t in range(T) for k in ("mx", "sb", "sm", "rc", "sw")]
            + ["n1", "n2", "Yn", "nn", "amx", "asb", "asm", "arc", "at", "o"])
KEYS_DVE = ["max", "idx", "rep", "max2", "idx2", "f", "cand", "cmax", "cpos", "crep", "cmax2", "cpos2", "neg",
            "posf"] + [f"{k}{h}" for h in range(2) for k in ("eq", "sel", "row")]
COPIES = ["KV", "X"]


def build(nc, x, adjT, w1, w2, w3, wqpkT, keysT, wq, table, wo, wg0, wg1, bg0, bg1, wihT, whhT, bih, bhh,
          wfx, bfx, wxT, bx, wsl, bsl, temp, wqs, wks, wvs, wout, bout, c_ident, c_mask, c_iota, c_ones, out):
    with ExitStack() as ctx:
        def sb(name, shape, dt=F32):
            return ctx.enter_context(nc.sbuf_tensor(name, shape, dt))

        def bank(name):
            return ctx.enter_context(nc.psum_tensor(name, [P, 512], F32))

        def sem(name):
            return ctx.enter_context(nc.semaphore(name))

        adj_s = sb("adj_s", [P, T, N])
        adj2_s = sb("adj2_s", [P, T, N])
        w1_s, w2_s, w3_s = sb("w1_s", [P, H1]), sb("w2_s", [P, 2, H2]), sb("w3_s", [P, 4, D])
        keymap = sb("keymap", [P, HEADS, 2, NKEYS])
        wq_s, wo_s = sb("wq_s", [P, HEADS, D]), sb("wo_s", [P, HEADS, D])
        wg0_s, wg1_s = sb("wg0_s", [P, D]), sb("wg1_s", [P, D])
        lw = sb("lw", [P, 2, 2, 4 * D])
        lbias, lbias2 = sb("lbias", [P, SKIPS, 4]), sb("lbias2", [P, SKIPS, 4])
        wfx_s, slmap = sb("wfx_s", [P, SH * SD]), sb("slmap", [P, SH * G])
        wqs_s, wks_s, wvs_s = (sb(n, [SD, SD]) for n in ("wqs_s", "wks_s", "wvs_s"))
        wout_s = sb("wout_s", [SD, SH, D])
        rows = sb("rows", [65, 2 * 512])
        bfx_r, nn_r = rows[0:1, 0:512], rows[0:1, 512:1024]
        slb_r, bout_r = rows[32:33, 0:512], rows[32:33, 512:512 + D]
        ra_r, bg0_r, bg1_r = rows[64:65, 0:512], rows[64:65, 512:512 + D], rows[64:65, 512 + D:512 + 2 * D]
        temp_s, tinv = sb("temp_s", [P, SH]), sb("tinv", [P, SH])
        ident, mask, iota, ones = sb("ident", [P, P]), sb("mask", [P, P]), sb("iota", [P, NC]), sb("ones", [P, P])
        eps = sb("eps", [P, 1])
        ring = sb("ring", [P, SLOTS, UJ, 2 * D])
        diag = sb("diag", [P, 2, UJ, P])
        idx = sb("idx", [P, 2, HEADS, TOPK], U32)
        wts, wsum, winv = sb("wts", [P, 2, HEADS, TOPK]), sb("wsum", [P, 2, HEADS]), sb("winv", [P, 2, HEADS])
        KT, V = sb("KT", [P, HEADS, N]), sb("V", [P, T, HEADS, D])
        tv, ti, tf = sb("tv", [P, 2, 2, TOPK]), sb("ti", [P, 2, 2, TOPK], U32), sb("tf", [P, 2, 2, TOPK])
        work = sb("work", [P, TOPK * NC])
        rep = work[:, 0:4 * NKEYS].rearrange("p (h q k) -> p h q k", h=2, q=2)
        eq = work[:, :].rearrange("p (k c) -> p k c", c=NC)
        cs, ci, crep = sb("cs", [P, 2, NC]), sb("ci", [P, 2, NC]), sb("crep", [P, 2, NC])
        fs, fp, fpf = sb("fs", [P, 2, TOPK]), sb("fp", [P, 2, TOPK], U32), sb("fpf", [P, 2, TOPK])
        neg = sb("neg", [P, 2, 1])
        x_s = sb("x_s", [P, T, D])
        h12, ah = sb("h12", [P, 4, 512]), sb("ah", [P, 2, N])
        up, z = ah[:, 0, :], h12[:, 3, :].rearrange("p (t d) -> p t d", t=T)
        h1_s = h12[:, 0:2, :].rearrange("p a (b c) -> p (a b) c", b=2)
        x1, z1T = sb("x1", [P, T, D]), sb("z1T", [P, N])
        f_st, f_mv, f_sd, f_rs = (sb(n, s) for n, s in
                                  (("f_st", [P, T, 6]), ("f_mv", [P, T, 2]), ("f_sd", [P, T]), ("f_rs", [P, T])))
        KTa, Va = sb("KTa", [P, HEADS, 2 * P]), sb("Va", [P, 2, HEADS, D])
        x1a, z1Ta = sb("x1a", [P, T, D]), sb("z1Ta", [P, N])
        qo = sb("qo", [P, HEADS, N])
        prob, probT = sb("prob", [P, 2, N]), sb("probT", [P, 2, N])
        a_mx, a_sm, a_dg = sb("a_mx", [P, 2, 2]), sb("a_sm", [P, 2, 2]), sb("a_dg", [P, 2, P])
        l_mx, l_sm = sb("l_mx", [P, 2, 2]), sb("l_sm", [P, 2, 2])
        x2 = sb("x2", [P, T, D])
        p_st, p_mv, p_sd, p_rs = (sb(n, s) for n, s in
                                  (("p_st", [P, T, 6]), ("p_mv", [P, T, 2]), ("p_sd", [P, T]), ("p_rs", [P, T])))
        s_mx, s_sm = sb("s_mx", [P, SH]), sb("s_sm", [P, 2, SH])
        left = qo[:, :, :].rearrange("p h n -> p (h n)")
        z2 = left[:, 0:512].rearrange("p (t d) -> p t d", t=T)
        u2, g1_s, hT = left[:, 512:1024], left[:, 1024:1536].rearrange("p (t d) -> p t d", t=T), left[:, 1536:2048]
        gates = left[:, 2048:3072].rearrange("p (k n) -> p k n", k=4)
        cell, ctan, hid, ig = (left[:, 3072 + 256 * k:3072 + 256 * (k + 1)] for k in range(4))
        z3T, lg, Yn, rn = u2, left[:, 1024:1536], left[:, 2048:2560], left[:, 2560:3072]
        sw = KTa[:, :, :].rearrange("p h n -> p (h n)").rearrange("p (t n) -> p t n", t=T)
        swT = Va[:, :, :, :].rearrange("p a h d -> p (a h d)").rearrange("p (c n) -> p c n", c=T)
        stT, qs, ks, vs = (left[0:SD, 512 * k:512 * (k + 1)] for k in (2, 3, 6, 7))
        sat, satT = prob[0:G, 0, :], prob[0:G, 1, :]
        vw = left[0:G, 2048:3072].rearrange("p (h d) -> p h d", h=SH)
        gout = probT[:, 0, :].rearrange("p (c d) -> p c d", c=4)
        spare = ring[:, :, :, :].rearrange("p a b c -> p (a b c)")
        wqpk_u = spare[0:DK, 0:2048].rearrange("p (a f) -> p a f", a=2 * HEADS)
        keys_u = spare[0:DK, 2048:4096].rearrange("p (a k) -> p a k", a=2 * HEADS)
        wx_u = spare[0:SD, 4096:5120].rearrange("p (h f) -> p h f", h=SH)
        wsl_u, bx_u, bsl_u = spare[0:SD, 5120:5184], spare[0:SD, 5184:5192], spare[32:33, 5248:5760]

        S, KV0, KV1, FA, FB, FC, AA, AB = (bank(f"bank_{n}") for n in "S KV0 KV1 FA FB FC AA AB".split())
        A, KV = (AA, AB), (KV0, KV1)
        REGULAR = (A, prob, probT, a_mx, a_sm, a_dg)
        SPARE = ((FA, FB), ah, w2_s, l_mx, l_sm, w1_s[:, :].rearrange("p (k n) -> p k n", k=2))
        RING = (KV, *(ring[:, k, :, :].rearrange("p j (a n) -> p (j a n)", a=2).rearrange("p (k n) -> p k n", k=2)
                      for k in (0, 1)), *(ring[:, 2, k, 0:4].rearrange("p (k c) -> p k c", k=2) for k in (0, 1)),
                ring[:, 3, 0, :].rearrange("p (k n) -> p k n", k=2))

        def att_work(n, last):
            if not last:
                return REGULAR
            return SPARE if n < HEADS else (RING, SPARE, REGULAR)[n % 3]

        def q_of(h, last):
            if not last:
                return qo[:, h, :]
            return adj2_s[:, h, :] if h < T else h12[:, h - T, :]


        merge_in, front_in, consts_in, x_in = sem("merge_in"), sem("front_in"), sem("consts_in"), sem("x_in")
        stored = sem("stored")
        passed_dve, passed_pe, passed_pool = sem("passed_dve"), sem("passed_pe"), sem("passed_pool")
        lw_in = [sem("lw_in0"), sem("lw_in1")]
        merged, merged_copied = sem("merged"), sem("merged_copied")
        setup_dve = sem("setup_dve")
        gathered = [sem(f"gathered{k}") for k in range(SLOTS)]
        slots_free, diags_made, pairs_out = sem("slots_free"), sem("diags_made"), sem("pairs_out")
        sims = sem("sims")
        wexp, winverted, wnorm = sem("wexp"), sem("winverted"), sem("wnorm")
        fpe, fact, fdve = (Signal(sem(n), s) for n, s in
                           (("front_products", FRONT_PE), ("front_copies", FRONT_ACT), ("front_sums", FRONT_DVE)))
        ape, aact, adve = (Signal(sem(n), s) for n, s in
                           (("att_products", ATT_PE), ("att_copies", ATT_ACT), ("att_sums", ATT_DVE)))
        ape_l, aact_l, adve_l = Signal(ape.sem, LAST_PE), Signal(aact.sem, LAST_ACT), Signal(adve.sem, LAST_DVE)
        ppe, pact, pdve = (Signal(sem(n), s, start) for n, s, start in
                           (("post_products", POST_PE, len(POST_PE)), ("post_copies", POST_ACT, 0), ("post_sums", POST_DVE, 0)))
        keys = Signal(sem("keys_done"), KEYS_DVE)
        copied = [Signal(sem(f"copied_{n}"), [n]) for n in COPIES]
        kv_copied, x_copied = copied

        block = ctx.enter_context(nc.Block())
        merge_loads = [(wqpk_u, wqpkT), (keys_u, keysT), (wx_u, wxT), (wsl_u, wsl), (bx_u, bx)]
        front_loads = [(adj_s[:, :, :], adjT.rearrange("(t p) n -> p t n", p=P)), (w1_s[:, :], w1),
                       (w2_s[:, :, :], w2.rearrange("(c p) n -> p c n", p=P)),
                       (w3_s[:, :, :], w3.rearrange("(c p) n -> p c n", p=P)), (ident[:, :], c_ident)]
        loads = [(temp_s[:, :], temp), (bsl_u, bsl), (iota[:, :], c_iota), (ones[:, :], c_ones),
                 (lbias[:, :, :], bih), (lbias2[:, :, :], bhh),
                 (wq_s[:, :, :], wq.rearrange("p (h d) -> p h d", h=HEADS)),
                 (wo_s[:, :, :], wo.rearrange("(h p) d -> p h d", p=P)), (wg0_s[:, :], wg0), (wg1_s[:, :], wg1),
                 (wfx_s[:, :], wfx), (wqs_s[:, :], wqs), (wks_s[:, :], wks), (wvs_s[:, :], wvs),
                 (wout_s[:, :, :], wout.rearrange("(h p) d -> p h d", p=SD)), (bfx_r, bfx), (bg0_r, bg0),
                 (bg1_r, bg1), (bout_r, bout), (mask[:, :], c_mask)]
        MERGED = HEADS // 2 + 3
        ADJ2, SLICE_MAP, SETUP_DVE = 2, 7, 9

        def cols(t):
            return slice(t * P, (t + 1) * P)

        @block.sync
        def _(sp):
            def load_x(b, first=False):
                if not first:
                    sp.wait_ge(fdve.sem, fdve.at(b - 1, "x1"))
                sp.dma_start(x_s[:, :, :], x[b].rearrange("(t p) d -> p t d", p=P)).then_inc(x_in, 16)

            def store(b):
                sp.wait_ge(pdve.sem, pdve.at(b, "o"))
                sp.dma_start(out[b].rearrange("(t p) d -> p t d", p=P), x2[:, :, :]).then_inc(stored, 16)

            sp.sem_inc(stored, 16)
            def load_lstm(b):
                for p in range(1, SKIPS + 1):
                    if p > 2:
                        sp.wait_ge(ppe.sem, ppe.at(b, ("gates", LAST_OF[p - 2])))
                    else:
                        sp.wait_ge(ppe.sem, ppe.at(b - 1, ("gates", LAST_OF[p + 2])))
                    sp.dma_start(lw[:, p % 2, 0, :], wihT[:, p - 1, :]).then_inc(lw_in[p % 2], 16)
                    sp.dma_start(lw[:, p % 2, 1, :], whhT[:, p - 1, :]).then_inc(lw_in[p % 2], 16)

            load_x(0, True)
            for group, arrived in ((merge_loads, merge_in), (front_loads, front_in), (loads, consts_in)):
                for dst, src in group:
                    sp.dma_start(dst, src).then_inc(arrived, 16)
            load_x(1)
            with nc.sync.Fori(1, B - 1) as b:
                load_x(b + 1)
                load_lstm(b - 1)
                store(b - 1)
            for b in (B - 2, B - 1):
                load_lstm(b)
                store(b)
            sp.wait_ge(stored, 16 * (B + 1))

        @block.gpsimd
        def _(pool):
            pool.wait_ge(merged, MERGED - 1)
            pool.wait_ge(setup_dve, SLICE_MAP)
            with nc.gpsimd.Fori(0, B * T // 2) as m:
                for r in range(2 * HEADS):
                    wait_apart(pool, keys.sem, keys.at(m * HEADS + r // 2, "row1"), passed_pool)
                    for u in range(UNITS):
                        slot = (UNITS * r + u) % SLOTS
                        wait_apart(pool, slots_free, m * (2 * HEADS * UNITS) + UNITS * r + u + 1, passed_pool)
                        for j in range(UJ):
                            k = u * UJ + j
                            nc.gpsimd.indirect_dma_start(
                                ring[:, slot, j, :], None, table,
                                bass.IndirectOffsetOnAxis(ap=idx[:, r // HEADS, r % HEADS, k:k + 1], axis=0),
                                bounds_check=HEADS * NKV - 1, oob_is_err=False).then_inc(gathered[slot], 16)

        @block.tensor
        def _(pe):
            mm, tr = nc.tensor.matmul, nc.tensor.transpose

            def setup():
                pe.wait_ge(merge_in, 16 * len(merge_loads))
                for h in range(HEADS):
                    if h % 2 == 0 and h >= 4:
                        pe.wait_ge(merged_copied, h // 2 - 1)
                    for p in range(2):
                        last = mm(A[h // 2 % 2][:, cols(2 * (h % 2) + p)], wqpk_u[:, p * HEADS + h, :],
                                  keys_u[:, p * HEADS + h, :], start=True, stop=True)
                    if h % 2:
                        last.then_inc(merged, 1)
                for h in range(SH):
                    last = mm(KV0[:, h * G:(h + 1) * G], wx_u[:, h, :], wsl_u, start=True, stop=True)
                last.then_inc(merged, 1)
                for h in range(SH):
                    last = mm(KV1[32:33, h * G:(h + 1) * G], bx_u[:, h:h + 1], wsl_u, start=True, stop=True)
                last.then_inc(merged, 1)
                pe.sem_inc(slots_free, SLOTS)
                pe.sem_inc(ppe.sem, ppe.n)
                pe.wait_ge(front_in, 16 * len(front_loads))
                pe.wait_ge(setup_dve, ADJ2)

            def row_sums():
                pe.wait_ge(consts_in, 16 * len(loads))
                for m in range(T):
                    last = mm(FC[64:65, :], ones[:, 0:1], adj_s[:, m, :], start=(m == 0), stop=(m == T - 1))
                last.then_inc(merged, 1)

            def front(b, at):
                if at == FRONT_AT["Az"]:
                    pe.wait_ge(fdve.sem, fdve.at(b, "z"))
                    for m in range(T):
                        last = mm(FA[:, :], z[:, m, :], adj2_s[:, m, :], start=(m == 0), stop=(m == T - 1))
                    last.then_inc(fpe.sem, 1)
                if at == FRONT_AT["h1"]:
                    pe.wait_ge(fact.sem, fact.at(b, "Az"))
                    for half, k in ((FB, "h1a"), (FA, "h1b")):
                        for t in range(2):
                            tt = t + 2 * (k == "h1b")
                            last = mm(half[:, t * H1:(t + 1) * H1], up[:, cols(tt)], w1_s[:, :], start=True, stop=True)
                        last.then_inc(fpe.sem, 1)
                for c in range(2):
                    if at == FRONT_AT[f"Ah{c}"]:
                        pe.wait_ge(fact.sem, fact.at(b, "h1b"))
                        for m in range(T):
                            last = mm((FB, FA)[c][:, :], h1_s[:, m, cols(c)], adj2_s[:, m, :], start=(m == 0),
                                      stop=(m == T - 1))
                        last.then_inc(fpe.sem, 1)
                for c in range(4):
                    if at == FRONT_AT[f"h2{c}"]:
                        pe.wait_ge(fact.sem, fact.at(b, "Ah1" if c < 2 else f"h2{c - 2}"))
                        for g in range(2):
                            last = mm((FB, FA)[c % 2][:, :], w2_s[:, g, cols(c)], ah[:, g, :], start=(g == 0), stop=(g == 1))
                        last.then_inc(fpe.sem, 1)
                if at == FRONT_AT["P"]:
                    pe.wait_ge(fact.sem, fact.at(b, "h23"))
                    for t in range(T):
                        for c in range(4):
                            last = mm(FB[:, cols(t)], h12[:, c, cols(t)], w3_s[:, c, :], start=(c == 0), stop=(c == 3))
                    last.then_inc(fpe.sem, 1)
                if at == FRONT_AT["y"]:
                    pe.wait_ge(fact.sem, fact.at(b, "P"))
                    for t in range(T):
                        for m in range(T):
                            last = mm(FA[:, cols(t)], adj2_s[:, m, cols(t)], up[:, cols(m)], start=(m == 0), stop=(m == T - 1))
                    last.then_inc(fpe.sem, 1)
                if at == FRONT_AT["zT"]:
                    pe.wait_ge(fdve.sem, fdve.at(b, "z1"))
                    for t in range(T):
                        last = tr(FB[:, cols(t)], z[:, t, :], ident[:, :])
                    last.then_inc(fpe.sem, 1)

            def similarities(b, t, p, first=False):
                if t >= T:
                    b, t = b + 1, t - T
                pair = b * (POS // 2) + (t * HEADS + p) // 2
                if t == 0 and p == 0:
                    pe.wait_ge(fact.sem, fact.at(b, "zT"))
                if not first:
                    pe.wait_ge(keys.sem, keys.at(pair - 1, "rep"))
                mm(S[:, :], z1T[:, cols(t)], keymap[:, p:p + 2, :, :].rearrange("p a b k -> p (a b k)"),
                   start=True, stop=True).then_inc(sims, 1)

            def weigh(b, p, u, first=False):
                unit = b * (POS * UNITS) + p * UNITS + u
                slot, use = (p * UNITS + u) % SLOTS, b * (POS * UNITS // SLOTS) + (p * UNITS + u) // SLOTS
                if u == 0 and not (first and p < 2):
                    pe.wait_ge(pairs_out, b * POS + p - 1)
                pe.wait_ge(diags_made, unit + 1)
                pe.wait_ge(gathered[slot], (use + 1) * (16 * UJ))
                for j in range(UJ):
                    st, en = (u == 0 and j == 0), (u == UNITS - 1 and j == UJ - 1)
                    mm(KV[p % 2][:, 0:P], ring[:, slot, j, 0:D], diag[:, u % 2, j, :], start=st, stop=en,
                       skip_group_check=True)
                    last = mm(KV[p % 2][:, P:2 * P], diag[:, u % 2, j, :], ring[:, slot, j, D:2 * D], start=False,
                              stop=en, skip_group_check=True)
                last.then_inc(slots_free, 1)

            def attend(b, job, part, last_batch=False):
                h, ia, ib = ATT_AT[job]
                banks, probs, probsT, _, _, dg = att_work(job, last_batch)
                products, copies = (ape_l, aact_l) if last_batch else (ape, aact)
                qh = q_of(h, last_batch)
                if part == "q":
                    before = job - 3 if last_batch and job >= HEADS else job - 1
                    if before >= 0 and not (last_batch and job in (HEADS, HEADS + 1)):
                        pe.wait_ge(copies.sem, copies.at(b, ("o", ATT_AT[before][0], ATT_AT[before][2])))
                    if last_batch:
                        pe.wait_ge(pairs_out, (b + 1) * POS if ia else b * POS + ib * HEADS + h + 1)
                    elif job == 0:
                        pe.wait_ge(x_copied.sem, x_copied.at(b, "X"))
                        pe.wait_ge(kv_copied.sem, kv_copied.at(b, "KV"))
                    if ia == 0:
                        mm(banks[0][:, :], wq_s[:, h, :], z1T[:, :] if last_batch else z1Ta[:, :], start=True,
                           stop=True).then_inc(products.sem, 1)
                for i in (ia, ib):
                    bk, n = banks[i % 2], (i + 1) * P
                    if part == "s":
                        if i == 0:
                            pe.wait_ge(copies.sem, copies.at(b, ("q", h)))
                        q, kept = qh[:, cols(i)], min(n, 2 * P)
                        if last_batch:
                            last = mm(bk[:, 0:n], q, KT[:, h, 0:n], start=True, stop=True)
                        else:
                            last = mm(bk[:, 0:kept], q, KTa[:, h, 0:kept], start=True, stop=True)
                            if n > kept:
                                last = mm(bk[:, kept:n], q, KT[:, h, kept:n], start=True, stop=True)
                        last.then_inc(products.sem, 1)
                    if part == "T":
                        pe.wait_ge(copies.sem, copies.at(b, ("d", h, i)))
                        for j in range(i + 1):
                            last = mm(bk[:, cols(j)], probs[:, i % 2, cols(j)], dg[:, i % 2, :], start=True, stop=True)
                        last.then_inc(products.sem, 1)
                    if part == "v":
                        pe.wait_ge(copies.sem, copies.at(b, ("T", h, i)))
                        for j in range(i + 1):
                            v = V[:, j, h, :] if last_batch or j >= 2 else Va[:, j, h, :]
                            last = mm(bk[:, 0:P], v, probsT[:, i % 2, cols(j)], start=(j == 0), stop=(j == i))
                        last.then_inc(products.sem, 1)

            def lstm(b, k):
                u = LSTM[k]
                p, s, w0, n = u
                xs = hT[:, 0:(N // p) * p].rearrange("q (w p) -> q p w", p=p)[:, s, w0:w0 + n]
                if k == 0:
                    pe.wait_ge(pact.sem, pact.at(b, "g2"))
                else:
                    pe.wait_ge(pdve.sem, pdve.at(b, ("h", LSTM[k - 1])))
                if s == 0 and w0 == 0:
                    pe.wait_ge(lw_in[p % 2], 64 * b + 32 * ((p - 1) // 2 + 1))
                for gate in range(4):
                    to = A[gate // 2][:, (gate % 2) * 256:(gate % 2) * 256 + n]
                    last = mm(to, lw[:, p % 2, 0, cols(gate)], xs, start=True, stop=(s == 0))
                    if s:
                        last = mm(to, lw[:, p % 2, 1, cols(gate)], hid[:, 0:n], start=False, stop=True)
                last.then_inc(ppe.sem, 1)

            def post(b, at, last_batch=False):
                if at == POST_AT["wo"]:
                    copies = aact_l if last_batch else aact
                    pe.wait_ge(copies.sem, copies.at(b, ("o", HEADS - 1, T - 1)))
                    for t in range(T):
                        for h in range(HEADS):
                            last = mm(AA[:, cols(t)], q_of(h, last_batch)[:, cols(t)], wo_s[:, h, :], start=(h == 0), stop=(h == HEADS - 1))
                    last.then_inc(ppe.sem, 1)
                if at == POST_AT["Uz"]:
                    pe.wait_ge(pdve.sem, pdve.at(b, "z"))
                    for m in range(T):
                        last = mm(AB[:, :], z2[:, m, :], adj_s[:, m, :], start=(m == 0), stop=(m == T - 1))
                    last.then_inc(ppe.sem, 1)
                if at == POST_AT["g1"]:
                    pe.wait_ge(pact.sem, pact.at(b, "Uz"))
                    for t in range(T):
                        mm(AA[:, cols(t)], u2[:, cols(t)], wg0_s[:, :], start=True, stop=False)
                        last = mm(AA[:, cols(t)], ra_r[:, cols(t)], bg0_r, start=False, stop=True)
                    last.then_inc(ppe.sem, 1)
                if at == POST_AT["Ug"]:
                    pe.wait_ge(pact.sem, pact.at(b, "g1"))
                    for m in range(T):
                        last = mm(AB[:, :], g1_s[:, m, :], adj_s[:, m, :], start=(m == 0), stop=(m == T - 1))
                    last.then_inc(ppe.sem, 1)
                if at == POST_AT["g2"]:
                    pe.wait_ge(pact.sem, pact.at(b, "Ug"))
                    mm(AA[:, :], wg1_s[:, :], u2, start=True, stop=False)
                    mm(AA[:, :], bg1_r, ra_r, start=False, stop=True).then_inc(ppe.sem, 1)
                if at in LSTM_AT:
                    lstm(b, LSTM_AT[at])
                if at == POST_AT["ht"]:
                    pe.wait_ge(pdve.sem, pdve.at(b, ("h", LSTM[-1])))
                    for t in range(T):
                        last = tr(AA[:, cols(t)], hT[:, cols(t)], ident[:, :])
                    last.then_inc(ppe.sem, 1)
                if at == POST_AT["zT"]:
                    pe.wait_ge(pdve.sem, pdve.at(b, "z3"))
                    for t in range(T):
                        last = tr(AB[:, cols(t)], z2[:, t, :], ident[:, :])
                    last.then_inc(ppe.sem, 1)
                for t in range(T):
                    if at == POST_AT[f"lg{t}"]:
                        if t == 0:
                            pe.wait_ge(pact.sem, pact.at(b, "zT"))
                        if t >= 2:
                            pe.wait_ge(pdve.sem, pdve.at(b, ("sb", t - 2)))
                        mm(A[t % 2][:, :], z3T[:, cols(t)], slmap[:, :], start=True, stop=False)
                        mm(A[t % 2][:, :], ones[32:33, :], slb_r, start=False, stop=True).then_inc(ppe.sem, 1)
                if at == POST_AT["Y"]:
                    pe.wait_ge(pdve.sem, pdve.at(b, ("sw", T - 1)))
                    for t in range(T):
                        last = mm(AA[:, :], z2[:, t, :], sw[:, t, :], start=(t == 0), stop=(t == T - 1))
                    last.then_inc(ppe.sem, 1)
                    for t in range(T):
                        last = mm(AB[:, :], ones[:, :], sw[:, t, :], start=(t == 0), stop=(t == T - 1))
                    last.then_inc(ppe.sem, 1)
                if at == POST_AT["st"]:
                    pe.wait_ge(pdve.sem, pdve.at(b, "nn"))
                    for h in range(SH):
                        c = slice(h * G, (h + 1) * G)
                        mm(AA[0:SD, c], wfx_s[:, c], Yn[:, c], start=True, stop=False)
                        last = mm(AA[0:SD, c], bfx_r[:, c], nn_r[:, c], start=False, stop=True)
                    last.then_inc(ppe.sem, 1)
                if at == POST_AT["qk"]:
                    wait_apart(pe, pact.sem, pact.at(b, "st"), passed_pe)
                    mm(AB[0:SD, :], wqs_s[:, :], stT, start=True, stop=True).then_inc(ppe.sem, 1)
                    mm(AA[0:SD, :], wks_s[:, :], stT, start=True, stop=True).then_inc(ppe.sem, 1)
                if at == POST_AT["v"]:
                    wait_apart(pe, pact.sem, pact.at(b, "q"), passed_pe)
                    mm(AB[0:SD, :], wvs_s[:, :], stT, start=True, stop=True).then_inc(ppe.sem, 1)
                if at == POST_AT["sim"]:
                    wait_apart(pe, pact.sem, pact.at(b, "k"), passed_pe)
                    for h in range(SH):
                        c = slice(h * G, (h + 1) * G)
                        last = mm(AA[0:G, c], qs[:, c], ks[:, c], start=True, stop=True)
                    last.then_inc(ppe.sem, 1)
                if at == POST_AT["aT"]:
                    wait_apart(pe, pdve.sem, pdve.at(b, "at"), passed_pe)
                    for h in range(SH):
                        c = slice(h * G, (h + 1) * G)
                        last = tr(AA[0:G, c], sat[:, c], ident[0:G, 0:G])
                    last.then_inc(ppe.sem, 1)
                if at == POST_AT["vw"]:
                    wait_apart(pe, pact.sem, pact.at(b, "v"), passed_pe)
                    for h in range(SH):
                        to = (AB, FC)[h // 4][0:G, cols(h % 4)]
                        last = mm(to, vs[:, h * G:(h + 1) * G], wout_s[:, h, :], start=True, stop=True)
                    last.then_inc(ppe.sem, 1)
                if at == POST_AT["G"]:
                    wait_apart(pe, pact.sem, pact.at(b, "vw1"), passed_pe)
                    for h in range(SH):
                        to = AA[(h % 2) * G:(h % 2) * G + G, cols(h // 2)]
                        last = mm(to, satT[:, h * G:(h + 1) * G], vw[:, h, :], start=True, stop=True)
                    last.then_inc(ppe.sem, 1)
                for t in range(T):
                    if at == POST_AT[f"wT{t}"]:
                        pe.wait_ge(pact.sem, pact.at(b, ("wT", t - 2) if t >= 2 else "G"))
                        for c in range(4):
                            last = tr(A[t % 2][:, cols(c)], sw[:, t, cols(c)], ident[:, :])
                        last.then_inc(ppe.sem, 1)
                if at == POST_AT["o"]:
                    pe.wait_ge(pact.sem, pact.at(b, ("wT", T - 1)))
                    for t in range(T):
                        for c in range(4):
                            mm(FC[:, cols(t)], swT[:, c, cols(t)], gout[:, c, :], start=(c == 0), stop=False)
                        last = mm(FC[:, cols(t)], ones[32:33, :], bout_r, start=False, stop=True)
                    last.then_inc(ppe.sem, 1)

            def step(b, has_front=True, has_post=True, first=False):
                for p in range(POS):
                    for u in range(UNITS):
                        at = p * UNITS + u
                        weigh(b, p, u, first)
                        if first and at == 2:
                            similarities(0, 0, 6)
                        if first and at == 4:
                            similarities(0, 1, 0)
                        if has_post and u == 0 and 1 <= p <= 2 * HEADS:
                            attend(b - 1, p - 1, "T")
                        if has_post and u == 1 and 1 <= p <= 2 * HEADS:
                            attend(b - 1, p - 1, "v")
                        if u == 2 and p % 2 and (p + 1 < POS - HEADS or has_front):
                            similarities(b, (p + 1) // HEADS + 1, (p + 1) % HEADS)
                        if has_post and u == 2 and p < 2 * HEADS:
                            attend(b - 1, p, "q")
                        if has_post and u == 3 and p < 2 * HEADS:
                            attend(b - 1, p, "s")
                        if not has_front:
                            if u < 2 and p - 1 in OWN_STEP:
                                attend(b, OWN_STEP[p - 1], "Tv"[u], True)
                            if u >= 2 and p in OWN_STEP:
                                attend(b, OWN_STEP[p], "qs"[u - 2], True)
                        if has_front:
                            front(b + 1, front_unit(at, first))
                        if has_post:
                            post(b - 1, at)

            setup()
            for at in range(POS * UNITS):
                front(0, at)
            pe.wait_ge(merged_copied, HEADS // 2)
            similarities(0, 0, 0, first=True)
            row_sums()
            similarities(0, 0, 2)
            similarities(0, 0, 4)
            pe.wait_ge(setup_dve, SLICE_MAP)
            step(0, has_post=False, first=True)
            pe.wait_ge(setup_dve, SETUP_DVE)
            with nc.tensor.Fori(1, B - 1) as b:
                step(b)
            step(B - 1, has_front=False)
            for n, stage in LAST_AFTER:
                for part in ("qs", "T", "v")[stage]:
                    attend(B - 1, n, part, True)
            for at in range(POS * UNITS):
                post(B - 1, at, True)

        @block.scalar
        def _(act):
            af = nc.scalar.activation

            def setup():
                act.wait_ge(setup_dve, 1)
                front(0, FRONT_AT["z"], prologue=True)
                for k in range(HEADS // 2):
                    act.wait_ge(merged, k + 1)
                    af(keymap[:, 2 * k:2 * k + 2, :, :].rearrange("p a b k -> p (a b k)"), A[k % 2][:, :],
                       ACT.Copy).then_inc(merged_copied, 1)

            def deviation(mv, sd, wait_on, value, done):
                act.wait_ge(wait_on, value)
                af(sd[:, :], mv[:, :, 1], ACT.Sqrt, bias=eps[:, 0:1]).then_inc(done, 1)

            def evacuate(dst, src, chain, b, step_in, done, func=ACT.Copy):
                act.wait_ge(chain.sem, chain.at(b, step_in))
                af(dst, src, func).then_inc(done.sem, 1)

            def front(b, at, prologue=False):
                if at == FRONT_AT["z"]:
                    deviation(f_mv, f_sd, fdve.sem, fdve.at(b, "mv"), fact.sem)
                if at == FRONT_AT["Az"]:
                    evacuate(up, FA[:, :], fpe, b, "Az", fact)
                if at == FRONT_AT["h1"]:
                    evacuate(h1_s[:, 0:2, :].rearrange("p a b -> p (a b)"), FB[:, :], fpe, b, "h1a", fact, ACT.Relu)
                    evacuate(h1_s[:, 2:4, :].rearrange("p a b -> p (a b)"), FA[:, :], fpe, b, "h1b", fact, ACT.Relu)
                if at == FRONT_AT["Ah0"]:
                    evacuate(ah[:, 0, :], FB[:, :], fpe, b, "Ah0", fact)
                if at == FRONT_AT["Ah1"]:
                    evacuate(ah[:, 1, :], FA[:, :], fpe, b, "Ah1", fact)
                for c in range(4):
                    if at == FRONT_AT[f"h2{c}"]:
                        evacuate(h12[:, c, :], (FB, FA)[c % 2][:, :], fpe, b, f"h2{c}", fact, ACT.Relu)
                if at == FRONT_AT["P"]:
                    evacuate(up, FB[:, :], fpe, b, "P", fact)
                if at == FRONT_AT["z1"]:
                    deviation(f_mv, f_sd, fdve.sem, fdve.at(b, "mv1"), fact.sem)
                if at == FRONT_AT["zT"]:
                    if not prologue:
                        act.wait_ge(sims, b * (POS // 2))
                        act.wait_ge(x_copied.sem, x_copied.at(b - 1, "X"))
                    evacuate(z1T[:, :], FB[:, :], fpe, b, "zT", fact)

            def copy_kv(b):
                act.wait_ge(pairs_out, (b + 1) * POS)
                act.wait_ge(ppe.sem, ppe.at(b - 1, "o"))
                af(KTa[:, :, :], KT[:, :, 0:2 * P], ACT.Copy)
                af(Va[:, :, :, :].rearrange("p a h d -> p (a h d)"),
                   V[:, 0:2, :, :].rearrange("p a h d -> p (a h d)"), ACT.Copy).then_inc(kv_copied.sem, 1)

            def copy_x(b, first=False):
                act.wait_ge(fact.sem, fact.at(b, "zT"))
                act.wait_ge(fdve.sem, fdve.at(b, "x1"))
                if not first:
                    act.wait_ge(pdve.sem, pdve.at(b - 1, "x2"))
                af(x1a[:, :, :], x1[:, :, :], ACT.Copy)
                af(z1Ta[:, :], z1T[:, :], ACT.Copy).then_inc(x_copied.sem, 1)

            def weights(b, t, h):
                pair = b * (POS // 2) + (t * HEADS + h) // 2
                act.wait_ge(keys.sem, keys.at(pair, "neg"))
                for k in range(2):
                    last = af(wts[:, t % 2, h + k, :], fs[:, k, :], ACT.Exp, bias=neg[:, k, :],
                              accum_out=wsum[:, t % 2, h + k:h + k + 1])
                last.then_inc(wexp, 1)

            def diagonals(b, p, u, first=False):
                t, h = p // HEADS, p % HEADS
                if u == 0:
                    act.wait_ge(wnorm, b * (POS // 2) + p // 2 + 1)
                if not (first and p == 0 and u < 2):
                    act.wait_ge(slots_free, b * (POS * UNITS) + p * UNITS + u - 1 + SLOTS)
                for j in range(UJ):
                    k = u * UJ + j
                    last = af(diag[:, u % 2, j, :], ident[:, :], ACT.Copy, scale=wts[:, t % 2, h, k:k + 1])
                last.then_inc(diags_made, 1)

            def attend(b, job, part, last_batch=False):
                h, ia, ib = ATT_AT[job]
                banks, probs, probsT, mx, sm, dg = att_work(job, last_batch)
                products, copies, sums = (ape_l, aact_l, adve_l) if last_batch else (ape, aact, adve)
                qh = q_of(h, last_batch)
                if part == "q" and ia == 0:
                    evacuate(qh, banks[0][:, :], products, b, ("q", h), copies)
                for i in (ia, ib):
                    k, bk, n = i % 2, banks[i % 2], (i + 1) * P
                    if part == "e":
                        act.wait_ge(sums.sem, sums.at(b, ("n", h, i)))
                        af(probs[:, k, 0:n], bk[:, 0:n], ACT.Exp, bias=mx[:, k, 1:2], scale=ATT_SCALE,
                           accum_out=sm[:, k, 0:1]).then_inc(copies.sem, 1)
                    if part == "d":
                        act.wait_ge(sums.sem, sums.at(b, ("r", h, i)))
                        af(dg[:, k, :], ident[:, :], ACT.Copy, scale=sm[:, k, 1:2]).then_inc(copies.sem, 1)
                    if part == "T":
                        evacuate(probsT[:, k, 0:n], bk[:, 0:n], products, b, ("T", h, i), copies)
                    if part == "o":
                        evacuate(qh[:, cols(i)], bk[:, 0:P], products, b, ("v", h, i), copies)

            def lstm(b, k):
                u = LSTM[k]
                p, s, w0, n = u
                act.wait_ge(ppe.sem, ppe.at(b, ("gates", u)))
                for gate in range(4):
                    last = af(gates[:, gate, 0:n], A[gate // 2][:, (gate % 2) * 256:(gate % 2) * 256 + n],
                              ACT.Tanh if gate == 2 else ACT.Sigmoid, bias=lbias[:, p - 1, gate:gate + 1])
                last.then_inc(pact.sem, 1)
                act.wait_ge(pdve.sem, pdve.at(b, ("c" if s else "ig", u)))
                af(ctan[:, 0:n], cell[:, 0:n], ACT.Tanh).then_inc(pact.sem, 1)

            def post(b, at):
                if at == POST_AT["z"]:
                    deviation(p_mv, p_sd, pdve.sem, pdve.at(b, "mv"), pact.sem)
                if at == POST_AT["Uz"]:
                    evacuate(u2, AB[:, :], ppe, b, "Uz", pact)
                if at == POST_AT["g1"]:
                    evacuate(g1_s.rearrange("p t d -> p (t d)"), AA[:, :], ppe, b, "g1", pact, ACT.Relu)
                if at == POST_AT["Ug"]:
                    evacuate(u2, AB[:, :], ppe, b, "Ug", pact)
                if at == POST_AT["g2"]:
                    evacuate(hT, AA[:, :], ppe, b, "g2", pact, ACT.Relu)
                if at in LSTM_AT:
                    lstm(b, LSTM_AT[at])
                if at == POST_AT["z3"]:
                    deviation(p_mv, p_sd, pdve.sem, pdve.at(b, "mv3"), pact.sem)
                if at == POST_AT["zT"]:
                    evacuate(z3T, AB[:, :], ppe, b, "zT", pact)
                for t in range(T):
                    if at == POST_AT[f"lg{t}"]:
                        act.wait_ge(pdve.sem, pdve.at(b, ("sb", t)))
                        af(sw[:, t, :], lg, ACT.Exp).then_inc(pact.sem, 1)
                if at == POST_AT["st"]:
                    evacuate(stT, AA[0:SD, :], ppe, b, "st", pact)
                if at == POST_AT["qk"]:
                    evacuate(qs, AB[0:SD, :], ppe, b, "q", pact)
                    evacuate(ks, AA[0:SD, :], ppe, b, "k", pact)
                if at == POST_AT["v"]:
                    evacuate(vs, AB[0:SD, :], ppe, b, "v", pact)
                if at == POST_AT["sim"]:
                    act.wait_ge(pdve.sem, pdve.at(b, "asb"))
                    af(sat, sat, ACT.Exp, scale=SLICE_SCALE).then_inc(pact.sem, 1)
                if at == POST_AT["aT"]:
                    evacuate(satT, AA[0:G, :], ppe, b, "aT", pact)
                if at == POST_AT["vw"]:
                    evacuate(vw[:, 0:4, :].rearrange("p h d -> p (h d)"), AB[0:G, :], ppe, b, "vw", pact)
                    evacuate(vw[:, 4:8, :].rearrange("p h d -> p (h d)"), FC[0:G, :], ppe, b, "vw", pact)
                if at == POST_AT["G"]:
                    evacuate(gout.rearrange("p c d -> p (c d)"), AA[:, :], ppe, b, "G", pact)
                for t in range(T):
                    if at == POST_AT[f"wT{t}"]:
                        evacuate(swT[:, :, cols(t)], A[t % 2][:, :].rearrange("p (c n) -> p c n", c=4), ppe, b,
                                 ("wT", t), pact)

            def step(b, has_front=True, has_post=True, first=False, last=False):
                for p in range(POS):
                    if has_post and 1 <= p <= 2 * HEADS:
                        attend(b - 1, p - 1, "d")
                    for u in range(UNITS):
                        at = p * UNITS + u
                        if at + 1 < POS * UNITS:
                            diagonals(b, (at + 1) // UNITS, (at + 1) % UNITS, first)
                        elif not last:
                            diagonals(b + 1, 0, 0)
                        if first and at in FIRST_WEIGHTS:
                            weights(0, 0, FIRST_WEIGHTS[at])
                        if has_post and at == 0:
                            copy_kv(b - 1)
                        if has_post and u == 0 and 1 <= p <= 2 * HEADS:
                            attend(b - 1, p - 1, "T")
                        if has_post and u == 1 and 1 <= p <= 2 * HEADS:
                            attend(b - 1, p - 1, "o")
                        if u == 1 and p % 2 and (p < POS - HEADS or has_front):
                            weights(b + 1 if p >= POS - HEADS else b, (p // HEADS + 1) % T, p % HEADS - 1)
                        if has_post and u == 2 and p < 2 * HEADS:
                            attend(b - 1, p, "q")
                        if has_post and u == 3 and p < 2 * HEADS:
                            attend(b - 1, p, "e")
                        if not has_front:
                            if u < 2 and p - 1 in OWN_STEP:
                                for part in ("dT", "o")[u]:
                                    attend(b, OWN_STEP[p - 1], part, True)
                            if u >= 2 and p in OWN_STEP:
                                attend(b, OWN_STEP[p], "qe"[u - 2], True)
                        if has_front:
                            front(b + 1, front_unit(at, first))
                        if has_post:
                            post(b - 1, at)
                        if at == COPY_X_AT:
                            copy_x(b, first=first)

            setup()
            for at in range(FRONT_AT["z"] + 1, POS * UNITS):
                front(0, at, prologue=True)
            weights(0, 0, 0)
            diagonals(0, 0, 0, first=True)
            step(0, has_post=False, first=True)
            with nc.scalar.Fori(1, B - 1) as b:
                step(b)
            step(B - 1, has_front=False, last=True)
            for n, stage in LAST_AFTER:
                for part in ("qe", "dT", "o")[stage]:
                    attend(B - 1, n, part, True)
            for at in range(POS * UNITS):
                post(B - 1, at)

        @block.vector
        def _(dve):
            tt, ts, tc, red = nc.vector.tensor_tensor, nc.vector.tensor_scalar, nc.vector.tensor_copy, nc.vector.tensor_reduce

            def wide(ap, axis, n):
                ap = ap.unsqueeze(axis)
                shape = list(ap.shape)
                shape[axis] = n
                return ap.to_broadcast(shape)

            def setup():
                nc.vector.memset(eps[:, :], EPS).then_inc(setup_dve, 1)
                for at in (FRONT_AT["stats"], FRONT_AT["z"]):
                    front(0, at, first=True)
                dve.wait_ge(front_in, 16 * len(front_loads))
                tt(adj2_s[:, :, :], adj_s[:, :, :], adj_s[:, :, :], ALU.mult).then_inc(setup_dve, 1)
                dve.wait_ge(consts_in, 16 * len(loads))
                ts(tinv[:, :], temp_s[:, :], 0.1, 5.0, ALU.max, ALU.min).then_inc(setup_dve, 1)
                dve.wait_ge(setup_dve, 3)
                nc.vector.reciprocal(tinv[:, :], tinv[:, :]).then_inc(setup_dve, 1)
                dve.wait_ge(setup_dve, 4)
                dve.wait_ge(merged, MERGED - 2)
                tt(slmap[:, :].rearrange("p (h g) -> p h g", h=SH), KV0[:, :].rearrange("p (h g) -> p h g", h=SH),
                   wide(tinv[:, :], 2, G), ALU.mult).then_inc(setup_dve, 1)
                dve.wait_ge(merged, MERGED - 1)
                tt(slb_r, KV1[32:33, :], bsl_u, ALU.add).then_inc(setup_dve, 1)
                dve.wait_ge(setup_dve, 6)
                b3 = slb_r.rearrange("p (h g) -> p h g", h=SH)
                tt(b3, b3, wide(tinv[32:33, :], 2, G), ALU.mult).then_inc(setup_dve, 1)
                tt(lbias[:, :, :], lbias[:, :, :], lbias2[:, :, :], ALU.add).then_inc(setup_dve, 1)

            def statistics(src, st, mv, chain, b, names):
                for t in range(T):
                    last = nc.vector.bn_stats(st[:, t, :], src[:, t, :])
                last.then_inc(chain.sem, 1)
                wait_apart(dve, chain.sem, chain.at(b, names[0]), passed_dve)
                for t in range(T):
                    last = nc.vector.bn_aggr(mv[:, t, :], st[:, t, :])
                last.then_inc(chain.sem, 1)

            def normalise(dst, src, mv, sd, rs, chain, b, names):
                nc.vector.reciprocal(rs[:, :], sd[:, :]).then_inc(chain.sem, 1)
                dve.wait_ge(chain.sem, chain.at(b, names[2]))
                for t in range(T):
                    last = ts(dst[:, t, :], src[:, t, :], mv[:, t, 0:1], rs[:, t:t + 1], ALU.subtract, ALU.mult)
                last.then_inc(chain.sem, 1)

            def front(b, at, first=False):
                if at == FRONT_AT["stats"]:
                    dve.wait_ge(x_in, 16 * (b + 1))
                    statistics(x_s, f_st, f_mv, fdve, b, ("st", "mv"))
                if at == FRONT_AT["z"]:
                    dve.wait_ge(fact.sem, fact.at(b, "sd"))
                    if not first:
                        dve.wait_ge(fpe.sem, fpe.at(b - 1, "zT"))
                    normalise(z, x_s, f_mv, f_sd, f_rs, fdve, b, ("st", "mv", "rs"))
                if at == FRONT_AT["y"]:
                    dve.wait_ge(fpe.sem, fpe.at(b, "y"))
                    if not first:
                        dve.wait_ge(x_copied.sem, x_copied.at(b - 1, "X"))
                    tt(x1[:, :, :], x_s[:, :, :], FA[:, :].rearrange("p (t d) -> p t d", t=T), ALU.add)\
                        .then_inc(fdve.sem, 1)
                    dve.wait_ge(fdve.sem, fdve.at(b, "x1"))
                    statistics(x1, f_st, f_mv, fdve, b, ("st1", "mv1"))
                if at == FRONT_AT["z1"]:
                    dve.wait_ge(fact.sem, fact.at(b, "sd1"))
                    normalise(z, x1, f_mv, f_sd, f_rs, fdve, b, ("st1", "mv1", "rs1"))

            def top_keys(b, t, h, first=False):
                for stage in TOP_AT.values():
                    top_stage(stage, b, t, h, first)

            def top_stage(stage, b, t, h, first=False):
                if stage == "best 8 keys":
                    best_8_keys(b, t, h)
                elif stage == "next 8 keys":
                    next_8_keys(b, t, h)
                elif stage == "pairs":
                    pairs(b, t, h, first)
                else:
                    rows_of(b, t, h, int(stage == "rows 1"))

            def best_8_keys(b, t, h):
                pair = b * (POS // 2) + (t * HEADS + h) // 2
                K = keys

                def after(step):
                    wait_apart(dve, K.sem, K.at(pair, step), passed_dve)

                wait_apart(dve, sims, pair + 1, passed_dve)
                sims_s = S[:, :].rearrange("p (h q k) -> p h q k", h=2, q=2)
                four = [(k, q) for k in range(2) for q in range(2)]
                for k, q in four:
                    last = nc.vector.max(tv[:, k, q, 0:8], sims_s[:, k, q, :])
                last.then_inc(K.sem, 1)
                after("max")
                for k, q in four:
                    last = nc.vector.max_index(ti[:, k, q, 0:8], tv[:, k, q, 0:8], sims_s[:, k, q, :])
                last.then_inc(K.sem, 1)
                for k, q in four:
                    last = nc.vector.match_replace(rep[:, k, q, :], tv[:, k, q, 0:8], sims_s[:, k, q, :], TAKEN)
                last.then_inc(K.sem, 1)

            def next_8_keys(b, t, h):
                pair = b * (POS // 2) + (t * HEADS + h) // 2
                K = keys
                four = [(k, q) for k in range(2) for q in range(2)]

                def after(step):
                    wait_apart(dve, K.sem, K.at(pair, step), passed_dve)

                after("rep")
                for k, q in four:
                    last = nc.vector.max(tv[:, k, q, 8:16], rep[:, k, q, :])
                last.then_inc(K.sem, 1)
                after("max2")
                for k, q in four:
                    last = nc.vector.max_index(ti[:, k, q, 8:16], tv[:, k, q, 8:16], rep[:, k, q, :])
                last.then_inc(K.sem, 1)
                after("idx2")
                for k in range(2):
                    ts(tf[:, k, 0, :], ti[:, k, 0, :], float((h + k) * NKV), None, ALU.add)
                last = ts(tf[:, :, 1, :], ti[:, :, 1, :], float(NKEYS), None, ALU.mult)
                last.then_inc(K.sem, 1)

            def pairs(b, t, h, first=False):
                pair = b * (POS // 2) + (t * HEADS + h) // 2
                K = keys

                def after(step):
                    wait_apart(dve, K.sem, K.at(pair, step), passed_dve)

                after("f")
                for to, of in ((cs, tv), (ci, tf)):
                    for i, ni, nj, at in ROWS:
                        last = tt(to[:, :, at:at + ni * nj].rearrange("p h (i j) -> p h i j", i=ni),
                                  wide(of[:, :, 0, i:i + ni], 3, nj), wide(of[:, :, 1, 0:nj], 2, ni), ALU.add)
                last.then_inc(K.sem, 1)
                after("cand")
                if not first:
                    wait_apart(dve, wexp, pair, passed_dve)
                for k in range(2):
                    last = nc.vector.max(fs[:, k, 0:8], cs[:, k, :])
                last.then_inc(K.sem, 1)
                after("cmax")
                for k in range(2):
                    last = nc.vector.max_index(fp[:, k, 0:8], fs[:, k, 0:8], cs[:, k, :])
                last.then_inc(K.sem, 1)
                for k in range(2):
                    last = nc.vector.match_replace(crep[:, k, :], fs[:, k, 0:8], cs[:, k, :], TAKEN)
                last.then_inc(K.sem, 1)
                after("crep")
                for k in range(2):
                    last = nc.vector.max(fs[:, k, 8:16], crep[:, k, :])
                last.then_inc(K.sem, 1)
                after("cmax2")
                for k in range(2):
                    last = nc.vector.max_index(fp[:, k, 8:16], fs[:, k, 8:16], crep[:, k, :])
                last.then_inc(K.sem, 1)
                ts(neg[:, :, :], fs[:, :, 0:1], -1.0, None, ALU.mult).then_inc(K.sem, 1)
                after("cpos2")
                tc(fpf[:, :, :], fp[:, :, :]).then_inc(K.sem, 1)

            def rows_of(b, t, h, k):
                pair = b * (POS // 2) + (t * HEADS + h) // 2
                K = keys

                def after(step):
                    wait_apart(dve, K.sem, K.at(pair, step), passed_dve)

                after("row0" if k else "posf")
                tt(eq, wide(iota[:, :], 1, TOPK), wide(fpf[:, k, :], 2, NC), ALU.is_equal).then_inc(K.sem, 1)
                after(f"eq{k}")
                tt(eq, eq, wide(ci[:, k, :], 1, TOPK), ALU.mult).then_inc(K.sem, 1)
                after(f"sel{k}")
                with nc.allow_low_precision("one row number below 2^17 and zeros are summed, exact in float32"):
                    red(idx[:, t % 2, h + k, :], eq, AX, ALU.add).then_inc(K.sem, 1)

            def normalise_weights(b, t, h):
                pair = b * (POS // 2) + (t * HEADS + h) // 2
                dve.wait_ge(wexp, pair + 1)
                nc.vector.reciprocal(winv[:, t % 2, h:h + 2], wsum[:, t % 2, h:h + 2]).then_inc(winverted, 1)
                dve.wait_ge(winverted, pair + 1)
                w = wts[:, t % 2, h:h + 2, :]
                tt(w, w, wide(winv[:, t % 2, h:h + 2], 2, TOPK), ALU.mult).then_inc(wnorm, 1)

            def collect(b, p):
                t, h = p // HEADS, p % HEADS
                dve.wait_ge(slots_free, b * (POS * UNITS) + (p + 1) * UNITS + SLOTS)
                tc(KT[:, h, cols(t)], KV[p % 2][:, 0:P])
                tc(V[:, t, h, :], KV[p % 2][:, P:2 * P]).then_inc(pairs_out, 1)

            def attend(b, job, part, last_batch=False):
                h, ia, ib = ATT_AT[job]
                banks, _, _, mx, sm, _ = att_work(job, last_batch)
                products, copies, sums = (ape_l, aact_l, adve_l) if last_batch else (ape, aact, adve)
                for i in (ia, ib):
                    k, bk, n = i % 2, banks[i % 2], (i + 1) * P
                    if part == "m":
                        dve.wait_ge(products.sem, products.at(b, ("s", h, i)))
                        tt(bk[:, cols(i)], bk[:, cols(i)], mask[:, :], ALU.add).then_inc(sums.sem, 1)
                        dve.wait_ge(sums.sem, sums.at(b, ("m", h, i)))
                        nc.vector.reduce_max(mx[:, k, 0:1], bk[:, 0:n], AX).then_inc(sums.sem, 1)
                        dve.wait_ge(sums.sem, sums.at(b, ("x", h, i)))
                        ts(mx[:, k, 1:2], mx[:, k, 0:1], -ATT_SCALE, None, ALU.mult).then_inc(sums.sem, 1)
                    if part == "r":
                        dve.wait_ge(copies.sem, copies.at(b, ("e", h, i)))
                        nc.vector.reciprocal(sm[:, k, 1:2], sm[:, k, 0:1]).then_inc(sums.sem, 1)

            def lstm(b, k):
                u = LSTM[k]
                p, s, w0, n = u
                gi, gf, gg, go = (gates[:, k, 0:n] for k in range(4))
                dve.wait_ge(pact.sem, pact.at(b, ("gates", u)))
                c, product = cell[:, 0:n], ig[:, 0:n]
                if s:
                    tt(c, c, gf, ALU.mult).then_inc(pdve.sem, 1)
                    tt(product, gi, gg, ALU.mult).then_inc(pdve.sem, 1)
                    dve.wait_ge(pdve.sem, pdve.at(b, ("ig", u)))
                    tt(c, c, product, ALU.add).then_inc(pdve.sem, 1)
                else:
                    tt(c, gi, gg, ALU.mult).then_inc(pdve.sem, 1)
                dve.wait_ge(pact.sem, pact.at(b, ("tc", u)))
                if s == p - 1:
                    to = hT[:, 0:(N // p) * p].rearrange("q (w p) -> q p w", p=p)[:, s, w0:w0 + n]
                else:
                    to = hid[:, 0:n]
                tt(to, go, ctan[:, 0:n], ALU.mult).then_inc(pdve.sem, 1)

            def post(b, at):
                if at == POST_AT["wo"]:
                    dve.wait_ge(ppe.sem, ppe.at(b, "wo"))
                    dve.wait_ge(stored, 16 * (b + 1))
                    tt(x2[:, :, :], x1a[:, :, :], AA[:, :].rearrange("p (t d) -> p t d", t=T), ALU.add)\
                        .then_inc(pdve.sem, 1)
                    dve.wait_ge(pdve.sem, pdve.at(b, "x2"))
                    statistics(x2, p_st, p_mv, pdve, b, ("st", "mv"))
                if at == POST_AT["z"]:
                    dve.wait_ge(pact.sem, pact.at(b, "sd"))
                    normalise(z2, x2, p_mv, p_sd, p_rs, pdve, b, ("st", "mv", "rs"))
                if at in LSTM_AT:
                    lstm(b, LSTM_AT[at])
                if at == POST_AT["ht"]:
                    dve.wait_ge(ppe.sem, ppe.at(b, "ht"))
                    tt(x2[:, :, :], x2[:, :, :], AA[:, :].rearrange("p (t d) -> p t d", t=T), ALU.add)\
                        .then_inc(pdve.sem, 1)
                    dve.wait_ge(pdve.sem, pdve.at(b, "x3"))
                    statistics(x2, p_st, p_mv, pdve, b, ("st3", "mv3"))
                if at == POST_AT["z3"]:
                    dve.wait_ge(pact.sem, pact.at(b, "sd3"))
                    normalise(z2, x2, p_mv, p_sd, p_rs, pdve, b, ("st3", "mv3", "rs3"))
                for t in range(T):
                    if at == POST_AT[f"lg{t}"]:
                        logits = A[t % 2][:, :].rearrange("p (h g) -> p h g", h=SH)
                        w = sw[:, t, :].rearrange("p (h g) -> p h g", h=SH)
                        dve.wait_ge(ppe.sem, ppe.at(b, ("lg", t)))
                        nc.vector.reduce_max(s_mx[:, :], logits, AX).then_inc(pdve.sem, 1)
                        dve.wait_ge(pdve.sem, pdve.at(b, ("mx", t)))
                        if t:
                            dve.wait_ge(pact.sem, pact.at(b, ("ex", t - 1)))
                        tt(lg.rearrange("p (h g) -> p h g", h=SH), logits, wide(s_mx[:, :], 2, G), ALU.subtract)\
                            .then_inc(pdve.sem, 1)
                        dve.wait_ge(pact.sem, pact.at(b, ("ex", t)))
                        red(s_sm[:, 0, :], w, AX, ALU.add).then_inc(pdve.sem, 1)
                        dve.wait_ge(pdve.sem, pdve.at(b, ("sm", t)))
                        nc.vector.reciprocal(s_sm[:, 1, :], s_sm[:, 0, :]).then_inc(pdve.sem, 1)
                        dve.wait_ge(pdve.sem, pdve.at(b, ("rc", t)))
                        tt(w, w, wide(s_sm[:, 1, :], 2, G), ALU.mult).then_inc(pdve.sem, 1)
                if at == POST_AT["Y"]:
                    dve.wait_ge(ppe.sem, ppe.at(b, "nr"))
                    ts(rn, AB[:, :], EPS, None, ALU.add).then_inc(pdve.sem, 1)
                    dve.wait_ge(pdve.sem, pdve.at(b, "n1"))
                    nc.vector.reciprocal(rn, rn).then_inc(pdve.sem, 1)
                    dve.wait_ge(pdve.sem, pdve.at(b, "n2"))
                    tt(Yn, AA[:, :], rn, ALU.mult).then_inc(pdve.sem, 1)
                    tt(nn_r, AB[0:1, :], rn[0:1, :], ALU.mult).then_inc(pdve.sem, 1)
                if at == POST_AT["sim"]:
                    dve.wait_ge(ppe.sem, ppe.at(b, "sim"))
                    scores = AA[0:G, :].rearrange("p (h g) -> p h g", h=SH)
                    w = sat.rearrange("p (h g) -> p h g", h=SH)
                    nc.vector.reduce_max(s_mx[0:G, :], scores, AX).then_inc(pdve.sem, 1)
                    dve.wait_ge(pdve.sem, pdve.at(b, "amx"))
                    tt(w, scores, wide(s_mx[0:G, :], 2, G), ALU.subtract).then_inc(pdve.sem, 1)
                    dve.wait_ge(pact.sem, pact.at(b, "aex"))
                    red(s_sm[0:G, 0, :], w, AX, ALU.add).then_inc(pdve.sem, 1)
                    dve.wait_ge(pdve.sem, pdve.at(b, "asm"))
                    nc.vector.reciprocal(s_sm[0:G, 1, :], s_sm[0:G, 0, :]).then_inc(pdve.sem, 1)
                    dve.wait_ge(pdve.sem, pdve.at(b, "arc"))
                    tt(w, w, wide(s_sm[0:G, 1, :], 2, G), ALU.mult).then_inc(pdve.sem, 1)
                if at == POST_AT["o"]:
                    dve.wait_ge(ppe.sem, ppe.at(b, "o"))
                    tt(x2[:, :, :], x2[:, :, :], FC[:, :].rearrange("p (t d) -> p t d", t=T), ALU.add)\
                        .then_inc(pdve.sem, 1)

            def step(b, has_front=True, has_post=True, first=False):
                for p in range(POS):
                    for u in range(UNITS):
                        at = p * UNITS + u
                        if has_post and u == 0 and 1 <= p <= 2 * HEADS:
                            attend(b - 1, p - 1, "r")
                        if at % (2 * UNITS) in TOP_AT and (p < POS - HEADS or has_front):
                            top_stage(TOP_AT[at % (2 * UNITS)], b + 1 if p >= POS - HEADS else b,
                                      (p // HEADS + 1) % T, p % HEADS // 2 * 2)
                        if u == 1 and p % 2 == 0 and (p <= POS - HEADS or has_front) and not (first and p == 0):
                            before = p + HEADS - 2
                            normalise_weights(b + before // POS, before % POS // HEADS, before % HEADS)
                        if u == UNITS - 1:
                            collect(b, p)
                            if has_post and p < 2 * HEADS:
                                attend(b - 1, p, "m")
                        if not has_front:
                            if u == 0 and p - 1 in OWN_STEP:
                                attend(b, OWN_STEP[p - 1], "r", True)
                            if u == UNITS - 1 and p in OWN_STEP:
                                attend(b, OWN_STEP[p], "m", True)
                        if has_front:
                            front(b + 1, front_unit(at, first))
                        if has_post:
                            post(b - 1, at)

            setup()
            for at in range(FRONT_AT["z"] + 1, POS * UNITS):
                front(0, at, first=True)
            for p in range(0, HEADS, 2):
                top_keys(0, 0, p, first=(p == 0))
                normalise_weights(0, 0, p)
            dve.wait_ge(merged, MERGED)
            tc(ra_r, FC[64:65, :]).then_inc(setup_dve, 1)
            step(0, has_post=False, first=True)
            with nc.vector.Fori(1, B - 1) as b:
                step(b)
            step(B - 1, has_front=False)
            for n, stage in LAST_AFTER:
                if stage < 2:
                    attend(B - 1, n, "mr"[stage], True)
            for at in range(POS * UNITS):
                post(B - 1, at)


def kernel(**a):
    import numpy as np
    import concourse.bacc as bacc
    from concourse.bass_utils import run_bass_kernel_spmd

    f = np.float32
    a = {k: np.asarray(v) for k, v in a.items()}
    eye = np.eye(P, dtype=f)
    arrays = {
        "x": a["x"], "adjT": a["adj"].T, "w1": a["L0_gnn_W1"], "w2": a["L0_gnn_W2"], "w3": a["L0_gnn_W3"],
        "wqpkT": a["L0_ffn_Wq_pk"].reshape(D, 2 * HEADS, DK).transpose(2, 1, 0),
        "keysT": a["L0_ffn_pk_keys"].transpose(3, 0, 2, 1).reshape(DK, 2 * HEADS, NKEYS),
        "wq": a["L0_ffn_Wq"],
        "table": np.concatenate([a["L0_ffn_keys_table"], a["L0_ffn_values_table"]], axis=1),
        "wo": a["L0_ffn_Wo"], "wg0": a["L1_gnn_Wg0"], "wg1": a["L1_gnn_Wg1"],
        "bg0": a["L1_gnn_bg0"].reshape(1, D), "bg1": a["L1_gnn_bg1"].reshape(1, D),
        "wihT": a["L1_gnn_Wih"].transpose(2, 0, 1), "whhT": a["L1_gnn_Whh"].transpose(2, 0, 1),
        "bih": a["L1_gnn_bih"].reshape(SKIPS, 4, D).transpose(2, 0, 1),
        "bhh": a["L1_gnn_bhh"].reshape(SKIPS, 4, D).transpose(2, 0, 1),
        "wfx": a["L1_ffn_W_fx"], "bfx": a["L1_ffn_b_fx"].reshape(1, SH * SD),
        "wxT": a["L1_ffn_W_x"].reshape(D, SH, SD).transpose(2, 1, 0), "bx": a["L1_ffn_b_x"].reshape(SH, SD).T,
        "wsl": a["L1_ffn_W_slice"], "bsl": np.tile(a["L1_ffn_b_slice"].reshape(1, G), (1, SH)),
        "temp": np.tile(a["L1_ffn_temperature"].reshape(1, SH), (P, 1)),
        "wqs": a["L1_ffn_W_q"], "wks": a["L1_ffn_W_k"], "wvs": a["L1_ffn_W_v"], "wout": a["L1_ffn_W_out"],
        "bout": a["L1_ffn_b_out"].reshape(1, D),
        "c_ident": eye, "c_mask": np.triu(np.full((P, P), MASKED, f), 1),
        "c_iota": np.tile(np.arange(NC, dtype=f), (P, 1)), "c_ones": np.ones((P, P), f),
    }
    order = ["x", "adjT", "w1", "w2", "w3", "wqpkT", "keysT", "wq", "table", "wo", "wg0", "wg1", "bg0", "bg1",
             "wihT", "whhT", "bih", "bhh", "wfx", "bfx", "wxT", "bx", "wsl", "bsl", "temp", "wqs", "wks", "wvs",
             "wout", "bout", "c_ident", "c_mask", "c_iota", "c_ones"]
    nc = bacc.Bacc("TRN2", target_bir_lowering=False, num_devices=1)
    feed, args = {}, []
    for name in order:
        v = np.ascontiguousarray(arrays[name])
        feed[f"in_{name}"] = v
        args.append(nc.dram_tensor(f"in_{name}", v.shape, mybir.dt.from_np(v.dtype), kind="ExternalInput").ap())
    result = nc.dram_tensor("result", (B, N, D), F32, kind="ExternalOutput").ap()
    build(nc, *args, result)
    r = run_bass_kernel_spmd(nc, [feed], core_ids=[0])
    return r.results[0]["result"]
```
